# Optimizing a Trainium2 kernel written in Bass

```python
import numpy as np
import jax
import jax.numpy as jnp

def _softmax(x, axis=-1):
    return jax.nn.softmax(x, axis=axis)

def _gelu(x):
    return jax.nn.gelu(x, approximate=True)

def _silu(x):
    return jax.nn.silu(x)

def _sigmoid(x):
    return jax.nn.sigmoid(x)

def _layernorm(x, axis=-1, eps=1e-05):
    m = jnp.mean(x, axis=axis, keepdims=True)
    v = jnp.var(x, axis=axis, keepdims=True)
    return (x - m) / jnp.sqrt(v + eps)

def _scatter_add(tgt, idx, src, axis=0):
    return tgt.at[idx].add(src)

def _segment_sum(src, seg, n):
    return jax.ops.segment_sum(src, seg, n)
kernel_name = 'mk_decoder_postln_d1_seqx_r4_802212'

def setup_inputs(seed: int=0):
    np.random.seed(seed)
    _w = jnp.asarray

    def _rec_inputs():
        import jax
        import jax.numpy as jnp
        _rk = jax.random.key(seed)
        x = 7.22e-05 + 1 * jax.random.normal(jax.random.fold_in(_rk, 1), (4, 1024, 256), jnp.float32)
        _lenS = 1024 - jax.random.randint(jax.random.fold_in(_rk, 7), (4,), 0, max(1, 1024 // 4) + 1, jnp.int32)
        _lenS2 = 77 - jax.random.randint(jax.random.fold_in(_rk, 8), (4,), 0, max(1, 77 // 4) + 1, jnp.int32)
        _ctx_768P = jax.random.normal(jax.random.fold_in(_rk, 11), (4, 16, 192), jnp.float32)
        _ctx_768c = jax.random.dirichlet(jax.random.fold_in(_rk, 511), 0.3 * jnp.ones((16,), jnp.float32), (4, 77))
        _ctx_768t = jnp.einsum('bsk,bkd->bsd', _ctx_768c, _ctx_768P)
        _ctx_768t = _ctx_768t * jax.lax.rsqrt(jnp.mean(jnp.square(_ctx_768t)) + 1e-12) * 0.953939
        ctx_768 = -7.36909e-05 + 0.999899 * (_ctx_768t + 0.3 * jax.random.normal(jax.random.fold_in(_rk, 611), (4, 77, 192), jnp.float32))
        return (x, ctx_768)
    x, ctx_768 = _rec_inputs()

    def _L0_attn_setup():
        import jax, jax.numpy as jnp
        import numpy as np
        H, DK, DV, L = (16, 64, 64, 128)
        B, S, D = (4, 2048, 256)
        key = jax.random.key(seed)
        k = jax.random.split(key, 6)
        w = 0.02
        return {'x': jax.random.normal(k[0], (B, S, D), jnp.float32), 'Wq': jax.random.normal(k[1], (D, H * DK), jnp.float32) * w, 'Wk': jax.random.normal(k[2], (D, H * DK), jnp.float32) * w, 'Wv': jax.random.normal(k[3], (D, H * DV), jnp.float32) * w, 'Wo': jax.random.normal(k[4], (H * DV, D), jnp.float32) * w, 'betas': jax.random.normal(k[5], (1, H, 1, DV), jnp.float32)}
    _L0_attn_all = _L0_attn_setup()
    _L0_attn_in = {k: v for k, v in _L0_attn_all.items() if k in ('Wq', 'Wk', 'Wv', 'Wo', 'betas')}
    del _L0_attn_all

    def _L0_xattn_setup():
        import jax, jax.numpy as jnp
        import numpy as np
        NUM_HEADS = 16
        HEAD_DIM = 64
        INNER = NUM_HEADS * HEAD_DIM
        QUERY_DIM = 256
        CONTEXT_DIM = 192
        SCALE = HEAD_DIM ** (-0.5)
        key = jax.random.key(seed)
        ks = jax.random.split(key, 6)
        B, NQ, NKV = (8, 256, 512)
        query = jax.random.normal(ks[0], (B, NQ, QUERY_DIM), dtype=jnp.float32)
        context = jax.random.normal(ks[1], (B, NKV, CONTEXT_DIM), dtype=jnp.float32)
        w_q = jax.random.normal(ks[2], (QUERY_DIM, INNER), dtype=jnp.float32) * QUERY_DIM ** (-0.5)
        w_kv = jax.random.normal(ks[3], (CONTEXT_DIM, 2 * INNER), dtype=jnp.float32) * CONTEXT_DIM ** (-0.5)
        w_out = jax.random.normal(ks[4], (INNER, QUERY_DIM), dtype=jnp.float32) * INNER ** (-0.5)
        b_out = jax.random.normal(ks[5], (QUERY_DIM,), dtype=jnp.float32) * 0.01
        return {'query': query, 'context': context, 'w_q': w_q, 'w_kv': w_kv, 'w_out': w_out, 'b_out': b_out}
    _L0_xattn_all = _L0_xattn_setup()
    _L0_xattn_in = {k: v for k, v in _L0_xattn_all.items() if k in ('w_q', 'w_kv', 'w_out', 'b_out')}
    del _L0_xattn_all

    def _L0_ffn_setup():
        import jax, jax.numpy as jnp
        import numpy as np
        from functools import partial
        HEADS = 16
        EPS = 1e-12

        def _l2_normalize(z):
            n = jnp.linalg.norm(z, axis=-1, keepdims=True)
            return z / jnp.maximum(n, EPS)
        key = jax.random.key(seed)
        kx, kq, kk, kv, ko, kf = jax.random.split(key, 6)
        B, S, D, L = (2, 512, 256, 256)
        scale = 0.02
        return {'x': jax.random.normal(kx, (B, S, D), dtype=jnp.float32), 'Wq': jax.random.normal(kq, (D, L), dtype=jnp.float32) * scale, 'Wk': jax.random.normal(kk, (D, L), dtype=jnp.float32) * scale, 'Wv': jax.random.normal(kv, (D, L), dtype=jnp.float32) * scale, 'Wo': jax.random.normal(ko, (L, D), dtype=jnp.float32) * scale, 'Wff': jax.random.normal(kf, (D, D), dtype=jnp.float32) * scale}
    _L0_ffn_all = _L0_ffn_setup()
    _L0_ffn_in = {k: v for k, v in _L0_ffn_all.items() if k in ('Wq', 'Wk', 'Wv', 'Wo', 'Wff')}
    del _L0_ffn_all
    return {'x': x, 'ctx_768': ctx_768, 'L0_attn_Wq': _L0_attn_in['Wq'], 'L0_attn_Wk': _L0_attn_in['Wk'], 'L0_attn_Wv': _L0_attn_in['Wv'], 'L0_attn_Wo': _L0_attn_in['Wo'], 'L0_attn_betas': _L0_attn_in['betas'], 'L0_xattn_w_q': _L0_xattn_in['w_q'], 'L0_xattn_w_kv': _L0_xattn_in['w_kv'], 'L0_xattn_w_out': _L0_xattn_in['w_out'], 'L0_xattn_b_out': _L0_xattn_in['b_out'], 'L0_ffn_Wq': _L0_ffn_in['Wq'], 'L0_ffn_Wk': _L0_ffn_in['Wk'], 'L0_ffn_Wv': _L0_ffn_in['Wv'], 'L0_ffn_Wo': _L0_ffn_in['Wo'], 'L0_ffn_Wff': _L0_ffn_in['Wff']}

def reference(x, ctx_768, L0_attn_Wq, L0_attn_Wk, L0_attn_Wv, L0_attn_Wo, L0_attn_betas, L0_xattn_w_q, L0_xattn_w_kv, L0_xattn_w_out, L0_xattn_b_out, L0_ffn_Wq, L0_ffn_Wk, L0_ffn_Wv, L0_ffn_Wo, L0_ffn_Wff):
    import jax
    import jax.numpy as jnp

    def _L0_attn_ref(x, Wq, Wk, Wv, Wo, betas):
        import jax, jax.numpy as jnp
        import numpy as np
        H, DK, DV, L = (16, 64, 64, 128)
        B, S, D = (4, 2048, 256)
        Bx, Sx, Dx = x.shape
        n_seg = Sx // L
        xs = x.reshape(Bx, n_seg, L, Dx)

        def proj(W, dh):
            p = jnp.einsum('bnld,df->bnlf', xs, W)
            return p.reshape(Bx, n_seg, H, L, dh).transpose(1, 0, 2, 3, 4)
        q = proj(Wq, DK)
        k = proj(Wk, DK)
        v = proj(Wv, DV)
        gate = jax.nn.sigmoid(betas)
        scale = 1.0 / jnp.sqrt(jnp.float32(DK))

        def step(carry, qkv):
            mem, zc = carry
            qs, ks, vs = qkv
            sq = jax.nn.elu(qs) + 1.0
            mem = mem + jnp.einsum('bhsk,bhsv->bhkv', sq, vs)
            zc = zc + (jax.nn.elu(ks) + 1.0).sum(axis=-2, keepdims=True)
            scores = jnp.einsum('bhsk,bhtk->bhst', qs, ks) * scale
            att_dot = jnp.einsum('bhst,bhtv->bhsv', jax.nn.softmax(scores, axis=-1), vs)
            num = jnp.einsum('bhsk,bhkv->bhsv', sq, mem)
            den = sq.sum(axis=-1, keepdims=True) * zc
            att = gate * (num / den) + (1.0 - gate) * att_dot
            out_seg = att.reshape(Bx, L, H * DV) @ Wo
            return ((mem, zc), out_seg)
        mem0 = jnp.zeros((Bx, H, DK, DV), x.dtype)
        zc0 = jnp.zeros((Bx, H, 1, DK), x.dtype)
        _, outs = jax.lax.scan(step, (mem0, zc0), (q, k, v))
        return outs.transpose(1, 0, 2, 3).reshape(Bx, Sx, Dx)

    def _L0_xattn_ref(query, context, w_q, w_kv, w_out, b_out):
        import jax, jax.numpy as jnp
        import numpy as np
        NUM_HEADS = 16
        HEAD_DIM = 64
        INNER = NUM_HEADS * HEAD_DIM
        QUERY_DIM = 256
        CONTEXT_DIM = 192
        SCALE = HEAD_DIM ** (-0.5)
        B, NQ, _ = query.shape
        NKV = context.shape[1]
        q = query @ w_q
        kv = context @ w_kv
        k, v = jnp.split(kv, 2, axis=-1)
        q = q.reshape(B, NQ, NUM_HEADS, HEAD_DIM).transpose(0, 2, 1, 3)
        k = k.reshape(B, NKV, NUM_HEADS, HEAD_DIM).transpose(0, 2, 1, 3)
        v = v.reshape(B, NKV, NUM_HEADS, HEAD_DIM).transpose(0, 2, 1, 3)
        scores = jnp.einsum('bhqd,bhkd->bhqk', q, k) * SCALE
        attn = jax.nn.softmax(scores, axis=-1)
        out = jnp.einsum('bhqk,bhkd->bhqd', attn, v)
        out = out.transpose(0, 2, 1, 3).reshape(B, NQ, INNER)
        return out @ w_out + b_out

    def _L0_ffn_ref(x, Wq, Wk, Wv, Wo, Wff):
        import jax, jax.numpy as jnp
        import numpy as np
        from functools import partial
        HEADS = 16
        EPS = 1e-12

        def _l2_normalize(z):
            n = jnp.linalg.norm(z, axis=-1, keepdims=True)
            return z / jnp.maximum(n, EPS)
        B, S, D = x.shape
        H = HEADS
        L = Wq.shape[1]
        dh = L // H

        def split_heads(t):
            return t.reshape(B, S, H, dh).transpose(0, 2, 1, 3).reshape(B * H, S, dh)
        q = split_heads(x @ Wq)
        k = split_heads(x @ Wk)
        v = split_heads(x @ Wv)
        scores = jnp.einsum('bqd,bkd->bkq', q, k) / jnp.sqrt(jnp.asarray(D, x.dtype))
        attn = jax.nn.softmax(scores, axis=-1)
        out = jnp.einsum('bkq,bkv->bqv', attn, v)
        z = out.reshape(B, H, S, dh).transpose(0, 2, 1, 3).reshape(B, S, L)
        z = z @ Wo
        z = _l2_normalize(z)
        z = z @ Wff
        z = _l2_normalize(z)
        z = jax.nn.gelu(z, approximate=False)
        return z
    x = _layernorm(x + _L0_attn_ref(x, L0_attn_Wq, L0_attn_Wk, L0_attn_Wv, L0_attn_Wo, L0_attn_betas), axis=-1)
    x = _layernorm(x + _L0_xattn_ref(x, ctx_768, L0_xattn_w_q, L0_xattn_w_kv, L0_xattn_w_out, L0_xattn_b_out), axis=-1)
    x = _layernorm(x + _L0_ffn_ref(x, L0_ffn_Wq, L0_ffn_Wk, L0_ffn_Wv, L0_ffn_Wo, L0_ffn_Wff), axis=-1)
    return x

_drawn_inputs = setup_inputs


def setup_inputs(seed=0):
    import zlib

    import numpy as np

    out = dict(_drawn_inputs(seed))
    spreads = {}
    factors = {'L0_attn_Wq': 8.0,
     'L0_attn_Wk': 8.0,
     'L0_attn_Wv': 4.794,
     'L0_attn_Wo': 4.684,
     'L0_attn_betas': 8.0,
     'L0_xattn_b_out': 6.073,
     'L0_ffn_Wq': 24.607,
     'L0_ffn_Wk': 26.766}
    for name, (base, spread) in spreads.items():
        noise = np.random.default_rng([zlib.crc32(name.encode()), seed]).standard_normal(out[name].shape)
        drawn = base * np.exp(spread * noise) if base else spread * noise
        out[name] = jnp.asarray(drawn.astype(out[name].dtype))
    for name, factor in factors.items():
        out[name] = (out[name] * factor).astype(out[name].dtype)
    return out
```

```python
from contextlib import ExitStack

import numpy as np
import concourse.bass as bass
from concourse import mybir

F32 = mybir.dt.float32
F32R = mybir.dt.float32r
BF16 = mybir.dt.bfloat16
ALU = mybir.AluOpType
ACT = mybir.ActivationFunctionType
AX_X = mybir.AxisListType.X

P = 128
D = 256
DC = D // P
H = 16
DH = 64
INNER = H * DH
PAIRS = H // 2
IC = INNER // P
HALF = 512
TOK = 2 * P
QUADS = 8
LN_EPS = 1e-5


def split_matmuls(pe, out, left, right):
    terms = []
    for (lh, ll), (rh, rl) in zip(left, right):
        terms += [(lh, rh), (lh, rl), (ll, rh)]
    for n, (a, b) in enumerate(terms):
        last = pe.matmul(out, a, b, start=n == 0, stop=n == len(terms) - 1)
    return last


def emit_segment_attention(nc, x, wq, wk, wv, wo, betas, x1):
    B, S, _ = x.shape
    ITER = B * S // TOK
    PER_BATCH = S // TOK
    xf = x.rearrange("b s d -> (b s) d")

    with ExitStack() as ctx:
        def sb(name, shape, dt=F32):
            return ctx.enter_context(nc.sbuf_tensor("a_" + name, shape, dt))

        def sem(name):
            return ctx.enter_context(nc.semaphore("a_" + name))

        bank = [ctx.enter_context(nc.psum_tensor(f"a_bank{i}", [P, HALF], F32)) for i in range(8)]
        S_BANK, PT_BANK, ATT_BANK = bank[0:3], bank[3:5], bank[5:7]
        Y_BANK = (bank[2], bank[7])

        ident = sb("ident", [P, P])
        ident2 = sb("ident2", [P, DH])
        block_ones = sb("block_ones", [P, P])
        fold = sb("fold", [P, P])
        neg_half = sb("neg_half", [P, 1])
        beta_rows = sb("beta_rows", [P, INNER])
        beta_cols = sb("beta_cols", [P, PAIRS])
        gate_cols = sb("gate_cols", [P, PAIRS])
        x_in = sb("x_in", [P, 2, D])
        x_res = sb("x_res", [P, 2, D])
        xT_hi = sb("xT_hi", [P, DC, TOK], F32R)
        xT_lo = sb("xT_lo", [P, DC, TOK], F32R)
        qT = sb("qT", [P, 2 * PAIRS, H, 8])
        phi_qT = sb("phi_qT", [P, 4, HALF])
        phi_tok = sb("phi_tok", [P, 4, HALF])
        phiT = sb("phiT", [P, PAIRS, TOK])
        e_k = sb("e_k", [P, 2, HALF])
        relu_k = sb("relu_k", [P, 2, HALF])
        k_pad = sb("k_pad", [P, 2 * PAIRS, 2, H, 8])
        vT = sb("vT", [P, 2 * PAIRS, H, 8])
        v_tok = sb("v_tok", [P, 4, HALF])
        v_gated = sb("v_gated", [P, 4, HALF])
        mem = sb("mem", [P, PAIRS, DH])
        mem_w = sb("mem_w", [P, 2, PAIRS, P])
        z_part = sb("z_part", [P, PAIRS, 4 * PAIRS])
        z_fold = sb("z_fold", [P, 4 * PAIRS])
        z_sum = sb("z_sum", [P, 2, PAIRS])
        z_acc = sb("z_acc", [P, 3, PAIRS])
        z_inv = sb("z_inv", [P, 2, PAIRS])
        z_gate = sb("z_gate", [P, 2, PAIRS])
        z_diag = sb("z_diag", [P, 2, PAIRS, DH])
        s_sum = sb("s_sum", [P, 4, 8])
        s_inv = sb("s_inv", [P, 4, 8])
        neg_max = sb("neg_max", [P, QUADS, 4])
        row_sum = sb("row_sum", [P, QUADS, 4])
        row_inv = sb("row_inv", [P, QUADS, 4])
        prob = sb("prob", [P, 3, 4, P])
        probT = sb("probT", [P, 2, 4, P])
        attT_hi = sb("attT_hi", [P, PAIRS, TOK], F32R)
        attT_lo = sb("attT_lo", [P, PAIRS, TOK], F32R)
        y = sb("y", [P, 2, D])
        stats = sb("stats", [P, 2, 6])
        mean_var = sb("mean_var", [P, 2, 2])
        var_eps = sb("var_eps", [P, 2])
        rstd = sb("rstd", [P, 2])
        normed = sb("normed", [P, 2, D])
        spare = sb("spare", [P, 2])
        stage = [v_tok[:, :, :].rearrange("p a b -> p (a b)"), v_gated[:, :, :].rearrange("p a b -> p (a b)")]

        def w_in(w):
            return w.rearrange("(c p) n -> p c n", p=P)

        sources = [(w_in(w), 2048) for w in (wq, wk, wv, wo)]
        landed = [sem("w_landed0"), sem("w_landed1")]
        high_done, low_done = sem("w_high"), sem("w_low")
        W = []
        for n in range(4):
            W.append((sb(f"w{n}_hi", [P, 2048], F32R), sb(f"w{n}_lo", [P, 2048], F32R)))

        def w_cols(n, c, width, a, b):
            return tuple(w[:, c * width + a:c * width + b] for w in W[n])

        c_zero, c_set, c_ident, c_ones = sem("zero"), sem("set"), sem("ident_done"), sem("ones_done")
        beta_in, beta_exp, gate_ready = sem("beta_in"), sem("beta_exp"), sem("gate_ready")
        gate_step = sem("gate_step")
        x_landed, xres_landed = sem("x_landed"), sem("xres_landed")
        x_turned, xT_hi_ready, xT_lo_ready = sem("x_turned"), sem("xT_hi_ready"), sem("xT_lo_ready")
        q_done, qT_ready, q_exp, phi_ready = sem("q_done"), sem("qT_ready"), sem("q_exp"), sem("phi_ready")
        phi_tok_done, phi_tok_ready = sem("phi_tok_done"), sem("phi_tok_ready")
        ssum_ready, sinv_ready, phin_ready = sem("ssum_ready"), sem("sinv_ready"), sem("phin_ready")
        k_done, k_exp, k_padded, k_summed = sem("k_done"), sem("k_exp"), sem("k_padded"), sem("k_summed")
        phik_ready, zpart_ready, zfold_ready, zfold_done = (sem("phik_ready"), sem("zpart_ready"),
                                                            sem("zfold_ready"), sem("zfold_done"))
        z_read = sem("z_read")
        z_step, zgate_ready, zdiag_ready = sem("z_step"), sem("zgate_ready"), sem("zdiag_ready")
        v_done, vT_ready, v_turned, v_copied, v_gated_ready = (sem("v_done"), sem("vT_ready"), sem("v_turned"),
                                                                sem("v_copied"), sem("v_gated_ready"))
        mem_done, mem_added, gz_done, memw_ready = (sem("mem_done"), sem("mem_added"), sem("gz_done"),
                                                    sem("memw_ready"))
        phi_turned, phiT_ready = sem("phi_turned"), sem("phiT_ready")
        scores_done, max_ready, exp_done = sem("scores_done"), sem("max_ready"), sem("exp_done")
        inv_ready, prob_ready, prob_turned, probT_ready = (sem("inv_ready"), sem("prob_ready"),
                                                           sem("prob_turned"), sem("probT_ready"))
        att_done, att_hi_ready, att_lo_ready = sem("att_done"), sem("att_hi_ready"), sem("att_lo_ready")
        y_done, y_added, ln_step, var_ready, rstd_ready = (sem("y_done"), sem("y_added"), sem("ln_step"),
                                                           sem("var_ready"), sem("rstd_ready"))
        normed_ready, stored = sem("normed_ready"), sem("stored")

        def shift_source(b, r, e):
            return b[r * DH:(r + 1) * DH, :].rearrange("p (j e m i) -> p j e m i", j=2, e=2, i=8)[:, :, e, :, :]

        def shift_target(dst, r, e, f):
            return dst[e * DH:(e + 1) * DH, :, 4 * f + r:4 * f + r + 3:2, :].rearrange("p m j i -> p j m i")

        def att_source(u, e, r):
            return ATT_BANK[u % 2][e * DH:(e + 1) * DH, 0:2 * P].rearrange(
                "p (j q r i) -> p j q r i", j=2, r=2, i=8)[:, :, :, r, :]

        def att_block(dst, e, r, t, f):
            at = t * P + e * DH + 2 * f * 8
            return dst[r * DH:(r + 1) * DH, :, at:at + 16].rearrange("p q (j i) -> p j q i", j=2)

        block = ctx.enter_context(nc.Block())

        @block.sync
        def _(sp):
            for e in range(2):
                sp.dma_start(beta_rows[:, :].rearrange("p (g e d) -> p g e d", e=2, d=DH)[:, :, e, :],
                             betas[0, e * PAIRS:(e + 1) * PAIRS, 0, :].unsqueeze(0).to_broadcast([P, PAIRS, DH])
                             ).then_inc(beta_in, 16)
            with nc.allow_non_contiguous_dma(reason="1024 elements, once"):
                for e in range(2):
                    sp.dma_start(beta_cols[e * DH:(e + 1) * DH, :],
                                 betas[0, e * PAIRS:(e + 1) * PAIRS, 0, :].rearrange("g d -> d g")
                                 ).then_inc(beta_in, 16)
            for n, (src, cols) in enumerate(sources):
                if n >= 2:
                    sp.wait_ge(low_done, n - 1)
                dst = stage[n % 2].rearrange("p (c n) -> p c n", c=src.shape[1])
                sp.dma_start(dst, src).then_inc(landed[n % 2], 16)

            def tokens(array, it):
                return array[bass.ds(it * TOK, TOK), :].rearrange("(t p) d -> p t d", p=P)

            sp.dma_start(x_in[:, :, :], tokens(xf, 0)).then_inc(x_landed, 16)
            sp.dma_start(x_res[:, :, :], tokens(xf, 0)).then_inc(xres_landed, 16)
            with sp.Fori(0, ITER - 1) as it:
                sp.wait_ge(x_turned, it + 1)
                sp.dma_start(x_in[:, :, :], tokens(xf, it + 1)).then_inc(x_landed, 16)
                sp.wait_ge(normed_ready, it * 2 + 2)
                sp.dma_start(tokens(x1, it), normed[:, :, :]).then_inc(stored, 16)
                sp.dma_start(x_res[:, :, :], tokens(xf, it + 1)).then_inc(xres_landed, 16)
            sp.wait_ge(x_turned, ITER)
            sp.dma_start(x_in[:, :, :], tokens(xf, 0)).then_inc(x_landed, 16)
            sp.wait_ge(normed_ready, ITER * 2)
            sp.dma_start(tokens(x1, ITER - 1), normed[:, :, :]).then_inc(stored, 16)
            sp.wait_ge(stored, ITER * 16 + 16)

        @block.tensor
        def _(pe):
            def scores(u, it):
                t, f = u // 4, u % 4
                for j in range(2):
                    p = 2 * f + j
                    last = pe.matmul(S_BANK[u % 3][:, j * 256:(j + 1) * 256],
                                     qT[:, t * PAIRS + p, :, :].rearrange("p c i -> p (c i)"),
                                     k_pad[:, t * PAIRS + p, :, :, :].rearrange("p h c i -> p (h c i)"),
                                     start=True, stop=True)
                last.then_inc(scores_done, 1)

            def turn_probs(u, it):
                pe.wait_ge(prob_ready, it * QUADS + u + 1)
                for j in range(4):
                    last = pe.transpose(PT_BANK[u % 2][:, j * P:(j + 1) * P], prob[:, u % 3, j, :], ident[:, :])
                last.then_inc(prob_turned, 1)

            def attend(u, it):
                t, f = u // 4, u % 4
                pe.wait_ge(probT_ready, it * QUADS + u + 1)
                if u >= 2:
                    pe.wait_ge(att_lo_ready, it * QUADS + u - 1)
                for j in range(2):
                    p = 2 * f + j
                    out = ATT_BANK[u % 2][:, j * P:(j + 1) * P]
                    pe.matmul(out, mem_w[:, t, p, :], phiT[:, p, t * P:(t + 1) * P], start=True, stop=False,
                              skip_group_check=True)
                    for h in range(2):
                        c = (2 * p + h) * DH
                        last = pe.matmul(out[h * DH:(h + 1) * DH, :],
                                         v_gated[:, 2 * t + c // HALF, c % HALF:c % HALF + DH],
                                         probT[:, u % 2, 2 * j + h, :], start=False, stop=True,
                                         skip_group_check=True)
                last.then_inc(att_done, 1)

            def project_out(t, it):
                pe.wait_ge(att_hi_ready, it * QUADS + 4 * t + 4)
                pe.wait_ge(att_lo_ready, it * QUADS + 4 * t + 4)
                s = slice(t * P, (t + 1) * P)
                split_matmuls(pe, Y_BANK[t][:, 0:D],
                              [(attT_hi[:, p, s], attT_lo[:, p, s]) for p in range(PAIRS)],
                              [w_cols(3, p, D, 0, D) for p in range(PAIRS)]).then_inc(y_done, 1)

            pe.wait_ge(c_ident, 3)
            pe.wait_ge(c_ones, 6)
            pe.wait_ge(low_done, 4)
            def turn_x(it):
                pe.wait_ge(x_landed, it * 16 + 16)
                for t in range(2):
                    for c in range(DC):
                        last = pe.transpose(bank[4][:, c * TOK + t * P:c * TOK + (t + 1) * P],
                                            x_in[:, t, c * P:(c + 1) * P], ident[:, :])
                last.then_inc(x_turned, 1)

            turn_x(0)
            with pe.Fori(0, ITER) as it:
                pe.wait_ge(xT_hi_ready, it + 1)
                pe.wait_ge(xT_lo_ready, it + 1)
                xT = [(xT_hi[:, c, :], xT_lo[:, c, :]) for c in range(DC)]
                for n, done in ((0, q_done), (1, k_done), (2, v_done)):
                    for f in range(4):
                        if n == 2:
                            pe.wait_ge(qT_ready, it * 4 + f + 1)
                        if (n, f) == (0, 2):
                            pe.wait_ge(y_added, it * 2 + 1)
                        if (n, f) == (1, 3):
                            pe.wait_ge(y_added, it * 2 + 2)
                        for j in range(2):
                            p = 2 * f + j
                            last = split_matmuls(pe, bank[4 * (n % 2) + f][:, j * TOK:(j + 1) * TOK],
                                                 [w_cols(n, c, INNER, p * P, (p + 1) * P) for c in range(DC)], xT)
                        last.then_inc(done, 1)

                def turn(unit, source, target, done):
                    for j in range(4):
                        last = pe.transpose(target[:, j * P:(j + 1) * P], source[:, j * P:(j + 1) * P], ident[:, :])
                    last.then_inc(done, 1)

                pe.wait_ge(k_summed, it * 4 + 4)
                pe.wait_ge(k_padded, it * 4 + 4)
                for u in range(4):
                    pe.wait_ge(phi_ready, it * 4 + u + 1)
                    turn(u, phi_qT[:, u, :], bank[4 + u], phi_tok_done)
                pe.wait_ge(vT_ready, it * 4 + 4)
                for u in range(4):
                    turn(u, vT[:, 4 * u:4 * u + 4, :, :].rearrange("p m c i -> p (m c i)"), bank[u], v_turned)
                pe.wait_ge(phi_tok_ready, it * 4 + 1)
                pe.wait_ge(zfold_ready, it + 1)
                pe.matmul(bank[4][:, 0:4 * PAIRS], fold[:, :], z_fold[:, :], start=True, stop=True
                          ).then_inc(zfold_done, 1)

                def memory(t, banks):
                    pe.wait_ge(v_copied, it * 4 + 2 * t + 2)
                    pe.wait_ge(phi_tok_ready, it * 4 + 2 * t + 2)
                    for p in range(PAIRS):
                        u, c = 2 * t + p // 4, (p % 4) * P
                        last = pe.matmul(banks[p // 4][:, c:c + P], phi_tok[:, u, c:c + P], v_tok[:, u, c:c + P],
                                         start=True, stop=True)
                    last.then_inc(mem_done, 1)

                memory(0, bank[0:2])
                memory(1, bank[2:4])
                for t in range(2):
                    pe.wait_ge(zdiag_ready, it * 2 + t + 1)
                    pe.matmul(bank[5 + t][:, :], block_ones[:, :], z_diag[:, t, :, :].rearrange("p a b -> p (a b)"),
                              start=True, stop=True).then_inc(gz_done, 1)
                pe.wait_ge(mem_added, it * 2 + 1)
                scores(0, it)
                scores(1, it)
                for u in range(4):
                    pe.wait_ge(phin_ready, it * 4 + u + 1)
                    if u == 0:
                        pe.wait_ge(z_read, it + 1)
                    if u >= 2:
                        pe.wait_ge(memw_ready, it * 2 + u - 1)
                    turn(u, phi_qT[:, u, :], bank[(4, 7, 5, 6)[u]], phi_turned)
                pe.wait_ge(mem_added, it * 2 + 2)
                for u in range(2, QUADS):
                    scores(u, it)
                    if u == 3:
                        pe.wait_ge(phiT_ready, it * 4 + 4)
                    turn_probs(u - 2, it)
                    if u == 3:
                        pe.wait_ge(v_gated_ready, it * 4 + 4)
                    if u >= 3:
                        attend(u - 3, it)
                turn_probs(6, it)
                attend(5, it)
                project_out(0, it)
                turn_probs(7, it)
                attend(6, it)
                attend(7, it)
                turn_x(it + 1)
                project_out(1, it)

        @block.scalar
        def _(act):
            act.wait_ge(beta_in, 64)
            act.activation(beta_rows[:, :], beta_rows[:, :], ACT.Exp, scale=-1.0).then_inc(beta_exp, 1)
            act.activation(beta_cols[:, :], beta_cols[:, :], ACT.Exp, scale=-1.0).then_inc(beta_exp, 1)
            for n in range(4):
                act.wait_ge(landed[n % 2], 16 * (n // 2 + 1))
                act.copy(W[n][0][:, :], stage[n % 2]).then_inc(high_done, 1)

            def exp_scores(u, it):
                act.wait_ge(max_ready, it * QUADS + u + 1)
                for j in range(4):
                    last = act.activation(prob[:, u % 3, j, :], S_BANK[u % 3][:, j * P:(j + 1) * P], ACT.Exp,
                                          bias=neg_max[:, u, j:j + 1], accum_out=row_sum[:, u, j:j + 1])
                last.then_inc(exp_done, 1)

            def high_x(it):
                act.wait_ge(x_turned, it + 1)
                for c in range(DC):
                    last = act.copy(xT_hi[:, c, :].rearrange("p (e t n) -> p t e n", e=2, t=2),
                                    bank[4][:, c * TOK:(c + 1) * TOK].rearrange("p (t e n) -> p t e n", e=2, t=2))
                last.then_inc(xT_hi_ready, 1)

            def take_att(u, it):
                t, f = u // 4, u % 4
                act.wait_ge(att_done, it * QUADS + u + 1)
                for e in range(2):
                    for r in range(2):
                        last = act.copy(att_block(attT_hi, e, r, t, f), att_source(u, e, r))
                last.then_inc(att_hi_ready, 1)

            high_x(0)
            with act.Fori(0, ITER) as it:
                for f in range(4):
                    act.wait_ge(q_done, it * 4 + f + 1)
                    for r in range(2):
                        for e in range(2):
                            last = act.copy(shift_target(qT, r, e, f), shift_source(bank[f], r, e))
                    last.then_inc(qT_ready, 1)
                for f in range(4):
                    act.wait_ge(k_done, it * 4 + f + 1)
                    if f >= 2:
                        act.wait_ge(k_summed, it * 4 + f - 1)
                    act.activation(e_k[:, f % 2, :], bank[4 + f][:, :], ACT.Exp)
                    act.activation(relu_k[:, f % 2, :], bank[4 + f][:, :], ACT.Relu).then_inc(k_exp, 1)
                act.wait_ge(qT_ready, it * 4 + 4)
                for u in range(4):
                    q_unit = qT[:, 4 * u:4 * u + 4, :, :].rearrange("p m c i -> p (m c i)")
                    act.activation(phi_qT[:, u, :], q_unit, ACT.Exp)
                    act.activation(phi_tok[:, u, :], q_unit, ACT.Relu).then_inc(q_exp, 1)
                for f in range(2):
                    act.wait_ge(v_done, it * 4 + f + 1)
                    for r in range(2):
                        for e in range(2):
                            last = act.copy(shift_target(vT, r, e, f), shift_source(bank[f], r, e))
                    last.then_inc(vT_ready, 1)
                for u in range(4):
                    act.wait_ge(phi_tok_done, it * 4 + u + 1)
                    act.copy(phi_tok[:, u, :], bank[4 + u][:, :]).then_inc(phi_tok_ready, 1)
                for u in range(4):
                    act.wait_ge(v_turned, it * 4 + u + 1)
                    act.copy(v_tok[:, u, :], bank[u][:, :]).then_inc(v_copied, 1)
                exp_scores(0, it)
                for u in range(4):
                    t, f = u // 2, u % 2
                    if u == 2:
                        exp_scores(1, it)
                    act.wait_ge(phi_turned, it * 4 + u + 1)
                    act.copy(phiT[:, 4 * f:4 * f + 4, t * P:(t + 1) * P],
                             bank[(4, 7, 5, 6)[u]][:, :].rearrange("p (a b) -> p a b", a=4)
                             ).then_inc(phiT_ready, 1)
                for u in range(2, QUADS):
                    exp_scores(u, it)
                    if u >= 3:
                        take_att(u - 3, it)
                take_att(5, it)
                take_att(6, it)
                take_att(7, it)
                high_x(it + 1)

        @block.gpsimd
        def _(pool):
            pool.memset(ident[:, :], 0.0).then_inc(c_zero, 1)
            pool.memset(ident2[:, :], 0.0).then_inc(c_zero, 1)
            pool.memset(block_ones[:, :], 0.0).then_inc(c_zero, 1)
            pool.memset(fold[:, :], 0.0).then_inc(c_zero, 1)
            pool.memset(neg_half[:, :], -0.5).then_inc(c_set, 1)
            pool.wait_ge(c_zero, 4)
            pool.affine_select(out=ident[:, :], in_=ident[:, :], compare_op=ALU.not_equal, fill=1.0, base=0,
                               pattern=[[-1, P]], channel_multiplier=1).then_inc(c_ident, 1)
            for h in range(2):
                rows = ident2[h * DH:(h + 1) * DH, :]
                pool.wait_ge(c_ident, h + 1)
                pool.affine_select(out=rows, in_=rows, compare_op=ALU.not_equal, fill=1.0, base=0,
                                   pattern=[[-1, DH]], channel_multiplier=1).then_inc(c_ident, 1)
                pool.wait_ge(c_ident, h + 2)
                pool.memset(block_ones[h * DH:(h + 1) * DH, h * DH:(h + 1) * DH], 1.0).then_inc(c_ones, 1)
                pool.wait_ge(c_ones, 3 * h + 1)
                for g in range(2):
                    block_of = fold[h * DH:(h + 1) * DH, g * DH:(g + 1) * DH]
                    pool.affine_select(out=block_of, in_=block_of, compare_op=ALU.not_equal, fill=1.0, base=0,
                                       pattern=[[-1, DH]], channel_multiplier=1).then_inc(c_ones, 1)
                    pool.wait_ge(c_ones, 3 * h + g + 2)
            pool.wait_ge(c_ident, 3)
            pool.wait_ge(c_set, 1)
            pool.wait_ge(gate_ready, 2)

            def normalise(u, it):
                pool.wait_ge(inv_ready, it * QUADS + u + 1)
                pool.tensor_tensor(prob[:, u % 3, :, :], prob[:, u % 3, :, :],
                                   row_inv[:, u, :].unsqueeze(2).to_broadcast([P, 4, P]), ALU.mult
                                   ).then_inc(prob_ready, 1)

            def root(t, it):
                pool.wait_ge(var_ready, it * 2 + t + 1)
                pool.tensor_tensor(rstd[:, t:t + 1], var_eps[:, t:t + 1], neg_half[:, :], ALU.pow
                                   ).then_inc(rstd_ready, 1)

            with pool.Fori(0, ITER) as it:
                for u in range(4):
                    pool.wait_ge(sinv_ready, it * 4 + u + 1)
                    pool.tensor_tensor(phi_qT[:, u, :].rearrange("p (h d) -> p h d", d=DH),
                                       phi_tok[:, u, :].rearrange("p (h d) -> p h d", d=DH),
                                       s_inv[:, u, :].unsqueeze(2).to_broadcast([P, 8, DH]), ALU.mult
                                       ).then_inc(phin_ready, 1)
                for t in range(2):
                    pool.wait_ge(zgate_ready, it * 2 + t + 1)
                    pool.tensor_tensor(z_diag[:, t, :, :], ident2[:, :].unsqueeze(1).to_broadcast([P, PAIRS, DH]),
                                       z_gate[:, t, :].unsqueeze(2).to_broadcast([P, PAIRS, DH]), ALU.mult
                                       ).then_inc(zdiag_ready, 1)
                for u in range(4):
                    f = u % 2
                    pool.wait_ge(v_copied, it * 4 + u + 1)
                    pool.tensor_tensor(v_gated[:, u, :], v_tok[:, u, :], beta_rows[:, f * HALF:(f + 1) * HALF],
                                       ALU.mult).then_inc(v_gated_ready, 1)
                for u in range(QUADS):
                    normalise(u, it)
                root(0, it)
                root(1, it)

        @block.vector
        def _(dve):
            dve.wait_ge(beta_exp, 2)
            dve.tensor_scalar(beta_rows[:, :], beta_rows[:, :], 1.0, None, ALU.add).then_inc(gate_step, 1)
            dve.tensor_scalar(beta_cols[:, :], beta_cols[:, :], 1.0, None, ALU.add).then_inc(gate_step, 1)
            dve.wait_ge(gate_step, 2)
            dve.reciprocal(beta_rows[:, :], beta_rows[:, :]).then_inc(gate_step, 1)
            dve.reciprocal(gate_cols[:, :], beta_cols[:, :]).then_inc(gate_ready, 1)
            dve.wait_ge(gate_step, 3)
            dve.tensor_scalar(beta_rows[:, :], beta_rows[:, :], -1.0, 1.0, ALU.mult, ALU.add
                              ).then_inc(gate_ready, 1)
            dve.wait_ge(gate_ready, 2)
            dve.memset(k_pad[:, :, :, :, :].rearrange("p a b c d -> p (a b c d)"), 0.0)
            dve.memset(mem_w[:, :, :, :].rearrange("p a b c -> p (a b c)"), 0.0).then_inc(gate_step, 1)
            dve.memset(stats[:, :, :].rearrange("p a b -> p (a b)"), 0.0).then_inc(stored, 16)
            dve.memset(mean_var[:, :, :].rearrange("p a b -> p (a b)"), 0.0).then_inc(y_added, 2)
            dve.wait_ge(gate_step, 4)
            for n in range(4):
                dve.wait_ge(high_done, n + 1)
                dve.tensor_tensor(W[n][1][:, :], stage[n % 2], W[n][0][:, :].bitcast(F32), ALU.subtract
                                  ).then_inc(low_done, 1)
            dve.wait_ge(low_done, 4)

            def maxima(u, it):
                dve.wait_ge(scores_done, it * QUADS + u + 1)
                dve.tensor_reduce(neg_max[:, u, :], S_BANK[u % 3][:, :].rearrange("p (a b) -> p a b", a=4),
                                  AX_X, ALU.max, negate=True).then_inc(max_ready, 1)

            def inverse(u, it):
                dve.wait_ge(exp_done, it * QUADS + u + 1)
                dve.reciprocal(row_inv[:, u, :], row_sum[:, u, :]).then_inc(inv_ready, 1)

            def low_att(u, it):
                t, f = u // 4, u % 4
                dve.wait_ge(att_hi_ready, it * QUADS + u + 1)
                for e in range(2):
                    for r in range(2):
                        last = dve.tensor_tensor(att_block(attT_lo, e, r, t, f), att_source(u, e, r),
                                                 att_block(attT_hi, e, r, t, f).bitcast(F32), ALU.subtract)
                last.then_inc(att_lo_ready, 1)

            def residual(t, it):
                if t == 0:
                    dve.wait_ge(xres_landed, it * 16 + 16)
                dve.wait_ge(y_done, it * 2 + t + 1)
                dve.tensor_tensor(y[:, t, :], Y_BANK[t][:, 0:D], x_res[:, t, :], ALU.add).then_inc(y_added, 1)
                dve.wait_ge(y_added, it * 2 + 2 + t + 1)
                dve.bn_stats(stats[:, t, :], y[:, t, :]).then_inc(ln_step, 1)
                dve.wait_ge(ln_step, it * 4 + 2 * t + 1)
                dve.memset(spare[:, t:t + 1], 0.0)
                dve.bn_aggr(mean_var[:, t, :], stats[:, t, :]).then_inc(ln_step, 1)
                dve.wait_ge(ln_step, it * 4 + 2 * t + 2)
                dve.tensor_scalar(var_eps[:, t:t + 1], mean_var[:, t, 1:2], LN_EPS, None, ALU.add
                                  ).then_inc(var_ready, 1)

            def normalise(t, it):
                dve.wait_ge(rstd_ready, it * 2 + t + 1)
                dve.wait_ge(stored, it * 16 + 16)
                dve.tensor_scalar(normed[:, t, :], y[:, t, :], mean_var[:, t, 0:1], rstd[:, t:t + 1],
                                  ALU.subtract, ALU.mult).then_inc(normed_ready, 1)

            def take_probT(u, it):
                dve.wait_ge(prob_turned, it * QUADS + u + 1)
                dve.tensor_copy(probT[:, u % 2, :, :].rearrange("p a b -> p (a b)"), PT_BANK[u % 2][:, :]
                                ).then_inc(probT_ready, 1)

            def low_x(it):
                dve.wait_ge(xT_hi_ready, it + 1)
                for c in range(DC):
                    last = dve.tensor_tensor(
                        xT_lo[:, c, :].rearrange("p (e t n) -> p t e n", e=2, t=2),
                        bank[4][:, c * TOK:(c + 1) * TOK].rearrange("p (t e n) -> p t e n", e=2, t=2),
                        xT_hi[:, c, :].rearrange("p (e t n) -> p t e n", e=2, t=2).bitcast(F32), ALU.subtract)
                last.then_inc(xT_lo_ready, 1)

            low_x(0)
            with dve.Fori(0, B) as b:
                dve.memset(mem[:, :, :].rearrange("p a b -> p (a b)"), 0.0).then_inc(z_step, 1)
                dve.memset(z_acc[:, 2, :], 0.0).then_inc(z_step, 1)
                with dve.Fori(0, PER_BATCH) as n:
                    it = b * PER_BATCH + n
                    zb = b * (2 + 4 * PER_BATCH) + n * 4 + 2
                    for f in range(4):
                        dve.wait_ge(k_done, it * 4 + f + 1)
                        dve.wait_ge(k_exp, it * 4 + f + 1)
                        for r in range(2):
                            for e in range(2):
                                last = dve.tensor_scalar(shift_target(k_pad[:, :, e, :, :], r, e, f),
                                                         shift_source(bank[4 + f], r, e), DH ** -0.5, None, ALU.mult)
                        last.then_inc(k_padded, 1)
                        dve.scalar_tensor_tensor(out=e_k[:, f % 2, :], in0=e_k[:, f % 2, :], scalar=1.0,
                                                 in1=relu_k[:, f % 2, :], op0=ALU.min, op1=ALU.add
                                                 ).then_inc(phik_ready, 1)
                        dve.wait_ge(phik_ready, it * 4 + f + 1)
                        dve.tensor_reduce(z_part[:, 2 * f:2 * f + 2, :].rearrange("p j m -> p (j m)"),
                                          e_k[:, f % 2, :].rearrange("p (m i) -> p m i", i=8), AX_X, ALU.add
                                          ).then_inc(k_summed, 1)
                    for u in range(4):
                        dve.wait_ge(q_exp, it * 4 + u + 1)
                        dve.scalar_tensor_tensor(out=phi_qT[:, u, :], in0=phi_qT[:, u, :], scalar=1.0,
                                                 in1=phi_tok[:, u, :], op0=ALU.min, op1=ALU.add
                                                 ).then_inc(phi_ready, 1)
                    dve.wait_ge(k_summed, it * 4 + 4)
                    dve.tensor_reduce(z_fold[:, :], z_part[:, :, :].rearrange("p a m -> p m a"), AX_X, ALU.add
                                      ).then_inc(zfold_ready, 1)
                    for f in range(2, 4):
                        dve.wait_ge(v_done, it * 4 + f + 1)
                        for r in range(2):
                            for e in range(2):
                                last = dve.tensor_copy(shift_target(vT, r, e, f), shift_source(bank[f], r, e))
                        last.then_inc(vT_ready, 1)
                    for u in range(4):
                        dve.wait_ge(phi_tok_ready, it * 4 + u + 1)
                        dve.tensor_reduce(s_sum[:, u, :], phi_tok[:, u, :].rearrange("p (h d) -> p h d", d=DH),
                                          AX_X, ALU.add).then_inc(ssum_ready, 1)
                        dve.wait_ge(ssum_ready, it * 4 + u + 1)
                        dve.reciprocal(s_inv[:, u, :], s_sum[:, u, :]).then_inc(sinv_ready, 1)
                    dve.wait_ge(zfold_done, it + 1)
                    for e in range(2):
                        rows = slice(e * DH, (e + 1) * DH)
                        last = dve.tensor_copy(z_sum[rows, :, :].rearrange("p t g -> p (t g)"),
                                               bank[4][rows, e * 16:(e + 1) * 16])
                    last.then_inc(z_read, 1)
                    dve.wait_ge(z_read, it + 1)
                    dve.wait_ge(z_step, zb)
                    dve.tensor_tensor(z_acc[:, 0, :], z_acc[:, 2, :], z_sum[:, 0, :], ALU.add).then_inc(z_step, 1)
                    dve.wait_ge(z_step, zb + 1)
                    dve.tensor_tensor(z_acc[:, 1, :], z_acc[:, 0, :], z_sum[:, 1, :], ALU.add).then_inc(z_step, 1)
                    dve.wait_ge(z_step, zb + 2)
                    dve.tensor_copy(z_acc[:, 2, :], z_acc[:, 1, :]).then_inc(z_step, 1)
                    dve.reciprocal(z_inv[:, :, :], z_acc[:, 0:2, :]).then_inc(z_step, 1)
                    dve.wait_ge(z_step, zb + 4)
                    for t in range(2):
                        dve.tensor_tensor(z_gate[:, t, :], z_inv[:, t, :], gate_cols[:, :], ALU.mult
                                          ).then_inc(zgate_ready, 1)
                    for t in range(2):
                        banks = (bank[0:2], bank[2:4])[t]
                        if t == 1:
                            dve.wait_ge(memw_ready, it * 2 + 1)
                        dve.wait_ge(mem_done, it * 2 + t + 1)
                        for h in range(2):
                            rows = slice(h * DH, (h + 1) * DH)
                            for g in range(2):
                                m = mem[rows, 4 * g:4 * g + 4, :]
                                last = dve.tensor_tensor(
                                    m, banks[g][rows, :].rearrange("p (a h d) -> p a h d", a=4, h=2)[:, :, h, :],
                                    m, ALU.add)
                        last.then_inc(mem_added, 1)
                        dve.wait_ge(mem_added, it * 2 + t + 1)
                        dve.wait_ge(gz_done, it * 2 + t + 1)
                        for h in range(2):
                            rows = slice(h * DH, (h + 1) * DH)
                            last = dve.tensor_tensor(
                                mem_w[rows, t, :, h * DH:(h + 1) * DH],
                                bank[5 + t][rows, :].rearrange("p (a d) -> p a d", a=PAIRS),
                                mem[rows, :, :], ALU.mult)
                        last.then_inc(memw_ready, 1)
                    maxima(0, it)
                    maxima(1, it)
                    inverse(0, it)
                    inverse(1, it)
                    for u in range(2, QUADS):
                        maxima(u, it)
                        take_probT(u - 2, it)
                        if u >= 4:
                            low_att(u - 4, it)
                        inverse(u, it)
                    take_probT(6, it)
                    low_att(4, it)
                    take_probT(7, it)
                    low_att(5, it)
                    low_att(6, it)
                    low_att(7, it)
                    low_x(it + 1)
                    residual(0, it)
                    normalise(0, it)
                    residual(1, it)
                    normalise(1, it)


def emit_cross_attention(nc, x1, context, wq, wkv, wo, bias, x2):
    B, CTX, CD = context.shape
    CK = CD // 2
    ITER = x2.shape[0] // TOK
    PER_BATCH = ITER // B
    NW = 2 * CTX

    with ExitStack() as ctx:
        def sb(name, shape, dt=F32):
            return ctx.enter_context(nc.sbuf_tensor("x_" + name, shape, dt))

        def sem(name):
            return ctx.enter_context(nc.semaphore("x_" + name))

        bank = [ctx.enter_context(nc.psum_tensor(f"x_bank{i}", [P, HALF], F32)) for i in range(8)]
        S_BANK, PT_BANK, ATT_BANK, Y_BANK = bank[0:3], bank[3:5], bank[5:7], bank[7]

        ident = sb("ident", [P, P])
        neg_half = sb("neg_half", [P, 1])
        bias_rows = sb("bias_rows", [P, D])
        ctx_in = sb("ctx_in", [CTX, B, CD])
        ctxT = sb("ctxT", [CK, 2, B, CTX])
        w_kv = sb("w_kv", [CK, 2, 2 * INNER])
        k_pad = sb("k_pad", [P, B, PAIRS, 2, CTX])
        v_all = sb("v_all", [P, B, INNER])
        v_now = sb("v_now", [P, INNER])
        x_in = sb("x_in", [P, 2, D])
        x_res = sb("x_res", [P, 2, D])
        x_bias = sb("x_bias", [P, 2, D])
        xT_hi = sb("xT_hi", [P, DC, TOK], F32R)
        xT_lo = sb("xT_lo", [P, DC, TOK], F32R)
        qT = sb("qT", [P, PAIRS, TOK])
        neg_max = sb("neg_max", [P, QUADS, 4])
        row_sum = sb("row_sum", [P, QUADS, 4])
        row_inv = sb("row_inv", [P, QUADS, 4])
        prob = sb("prob", [P, 3, 4, CTX])
        probT = sb("probT", [P, 2, 4, P])
        attT_hi = sb("attT_hi", [P, PAIRS, TOK], F32R)
        attT_lo = sb("attT_lo", [P, PAIRS, TOK], F32R)
        y = sb("y", [P, 2, D])
        stats = sb("stats", [P, 2, 6])
        mean_var = sb("mean_var", [P, 2, 2])
        var_eps = sb("var_eps", [P, 2])
        rstd = sb("rstd", [P, 2])
        normed = sb("normed", [P, 2, D])
        spare = sb("spare", [P, 2])
        stage = [sb(f"stage{n}", [P, 2048]) for n in range(2)]
        sources = [w.rearrange("(c p) n -> p c n", p=P) for w in (wq, wo)]
        W = [(sb(f"w{n}_hi", [P, 2048], F32R), sb(f"w{n}_lo", [P, 2048], F32R)) for n in range(2)]

        def w_cols(n, c, width, a, b):
            return tuple(w[:, c * width + a:c * width + b] for w in W[n])

        c_zero, c_ident, zeroed = sem("zero"), sem("ident_done"), sem("zeroed")
        landed = [sem("w_landed0"), sem("w_landed1")]
        high_done, low_done, ctx_landed, wkv_landed, bias_landed = (sem("w_high"), sem("w_low"), sem("ctx_landed"),
                                                                    sem("wkv_landed"), sem("bias_landed"))
        ctx_turned, ctxT_ready, ctx_k_done, ctx_k_ready = (sem("ctx_turned"), sem("ctxT_ready"),
                                                           sem("ctx_k_done"), sem("ctx_k_ready"))
        ctx_v_done, ctx_v_ready, v_now_ready = sem("ctx_v_done"), sem("ctx_v_ready"), sem("v_now_ready")
        x_landed, xres_landed, xbias_ready = sem("x_landed"), sem("xres_landed"), sem("xbias_ready")
        x_turned, xT_hi_ready, xT_lo_ready = sem("x_turned"), sem("xT_hi_ready"), sem("xT_lo_ready")
        q_done, qT_ready = sem("q_done"), sem("qT_ready")
        scores_done, max_ready, exp_done = sem("scores_done"), sem("max_ready"), sem("exp_done")
        inv_ready, prob_ready, prob_turned, probT_ready = (sem("inv_ready"), sem("prob_ready"),
                                                           sem("prob_turned"), sem("probT_ready"))
        att_done, att_hi_ready, att_lo_ready = sem("att_done"), sem("att_hi_ready"), sem("att_lo_ready")
        y_done, y_added, ln_step, var_ready, rstd_ready = (sem("y_done"), sem("y_added"), sem("ln_step"),
                                                           sem("var_ready"), sem("rstd_ready"))
        normed_ready, stored = sem("normed_ready"), sem("stored")

        block = ctx.enter_context(nc.Block())

        @block.sync
        def _(sp):
            sp.dma_start(ctx_in[:, :, :], context.rearrange("b s d -> s b d")).then_inc(ctx_landed, 16)
            sp.dma_start(w_kv[:, :, :], wkv.rearrange("(c p) n -> p c n", p=CK)).then_inc(wkv_landed, 16)
            for n in range(2):
                sp.dma_start(stage[n][:, :].rearrange("p (c n) -> p c n", c=sources[n].shape[1]), sources[n]
                             ).then_inc(landed[n], 16)
            sp.dma_start(bias_rows[:, :], bias.unsqueeze(0).to_broadcast([P, D])).then_inc(bias_landed, 16)

            def tokens(array, it):
                return array[bass.ds(it * TOK, TOK), :].rearrange("(t p) d -> p t d", p=P)

            sp.dma_start(x_in[:, :, :], tokens(x1, 0)).then_inc(x_landed, 16)
            sp.dma_start(x_res[:, :, :], tokens(x1, 0)).then_inc(xres_landed, 16)
            sp.wait_ge(ctx_v_ready, 2 * B)

            def values(b):
                sp.wait_ge(att_done, b * PER_BATCH * QUADS + 1)
                sp.dma_start(v_now[:, :], v_all[:, bass.ds(b, 1), :].rearrange("p b n -> p (b n)")
                             ).then_inc(v_now_ready, 16)

            def forward(it):
                sp.wait_ge(x_turned, it + 1)
                sp.dma_start(x_in[:, :, :], tokens(x1, it + 1)).then_inc(x_landed, 16)
                sp.wait_ge(normed_ready, it * 2 + 2)
                sp.dma_start(tokens(x2, it), normed[:, :, :]).then_inc(stored, 16)
                sp.dma_start(x_res[:, :, :], tokens(x1, it + 1)).then_inc(xres_landed, 16)

            with sp.Fori(0, B - 1) as b:
                values(b)
                with sp.Fori(0, PER_BATCH) as n:
                    forward(b * PER_BATCH + n)
            values(B - 1)
            with sp.Fori((B - 1) * PER_BATCH, ITER - 1) as it:
                forward(it)
            sp.wait_ge(normed_ready, ITER * 2)
            sp.dma_start(tokens(x2, ITER - 1), normed[:, :, :]).then_inc(stored, 16)
            sp.wait_ge(stored, ITER * 16 + 16)

        @block.tensor
        def _(pe):
            def scores(u, it, b):
                t, f = u // 4, u % 4
                for j in range(2):
                    p = 2 * f + j
                    last = pe.matmul(S_BANK[u % 3][:, j * NW:(j + 1) * NW], qT[:, p, t * P:(t + 1) * P],
                                     k_pad[:, bass.ds(b, 1), p, :, :].rearrange("p b h n -> p (b h n)"),
                                     start=True, stop=True)
                last.then_inc(scores_done, 1)

            def turn_probs(u, it):
                pe.wait_ge(prob_ready, it * QUADS + u + 1)
                for j in range(4):
                    last = pe.transpose(PT_BANK[u % 2][0:CTX, j * P:(j + 1) * P], prob[:, u % 3, j, :], ident[:, :])
                last.then_inc(prob_turned, 1)

            def attend(u, it):
                f = u % 4
                pe.wait_ge(probT_ready, it * QUADS + u + 1)
                if u >= 2:
                    pe.wait_ge(att_lo_ready, it * QUADS + u - 1)
                for j in range(2):
                    for h in range(2):
                        c = (2 * (2 * f + j) + h) * DH
                        last = pe.matmul(ATT_BANK[u % 2][h * DH:(h + 1) * DH, j * P:(j + 1) * P],
                                         v_now[:, c:c + DH], probT[:, u % 2, 2 * j + h, :], start=True, stop=True)
                last.then_inc(att_done, 1)

            def project_out(t, it):
                pe.wait_ge(att_hi_ready, it * QUADS + 4 * t + 4)
                pe.wait_ge(att_lo_ready, it * QUADS + 4 * t + 4)
                if t == 1:
                    pe.wait_ge(y_added, it * 2 + 2 + 1)
                s = slice(t * P, (t + 1) * P)
                split_matmuls(pe, Y_BANK[:, 0:D],
                              [(attT_hi[:, p, s], attT_lo[:, p, s]) for p in range(PAIRS)],
                              [w_cols(1, p, D, 0, D) for p in range(PAIRS)]).then_inc(y_done, 1)

            pe.wait_ge(c_ident, 1)
            pe.wait_ge(ctx_landed, 16)
            for c in range(2):
                for b in range(B):
                    last = pe.transpose(bank[c][0:CK, b * CTX:(b + 1) * CTX], ctx_in[:, b, c * CK:(c + 1) * CK],
                                        ident[0:CTX, 0:CTX])
            last.then_inc(ctx_turned, 1)
            pe.wait_ge(ctxT_ready, 1)
            pe.wait_ge(wkv_landed, 16)
            for p in range(PAIRS):
                if p >= 6:
                    pe.wait_ge(ctx_k_ready, p - 5)
                for c in range(2):
                    last = pe.matmul(bank[2 + p % 6][:, 0:B * CTX], w_kv[:, c, p * P:(p + 1) * P],
                                     ctxT[:, c, :, :].rearrange("p b n -> p (b n)"), start=c == 0, stop=c == 1)
                last.then_inc(ctx_k_done, 1)
            for n in range(2 * B):
                b, f = n // 2, n % 2
                if n >= 2:
                    pe.wait_ge(ctx_v_ready, n - 1)
                for c in range(2):
                    last = pe.matmul(bank[n % 2][0:CTX, :], ctxT[:, c, b, :],
                                     w_kv[:, c, INNER + f * HALF:INNER + (f + 1) * HALF], start=c == 0, stop=c == 1)
                last.then_inc(ctx_v_done, 1)
            pe.wait_ge(ctx_k_ready, PAIRS)
            pe.wait_ge(ctx_v_ready, 2 * B)
            pe.wait_ge(low_done, 2)
            with pe.Fori(0, B) as b:
                with pe.Fori(0, PER_BATCH) as n:
                    it = b * PER_BATCH + n
                    pe.wait_ge(x_landed, it * 16 + 16)
                    pe.wait_ge(y_added, it * 2 + 2)
                    for t in range(2):
                        for c in range(DC):
                            last = pe.transpose(bank[7][:, c * TOK + t * P:c * TOK + (t + 1) * P],
                                                x_in[:, t, c * P:(c + 1) * P], ident[:, :])
                    last.then_inc(x_turned, 1)
                    pe.wait_ge(xT_hi_ready, it + 1)
                    pe.wait_ge(xT_lo_ready, it + 1)
                    for f in range(4):
                        for j in range(2):
                            p = 2 * f + j
                            last = split_matmuls(pe, bank[f][:, j * TOK:(j + 1) * TOK],
                                                 [w_cols(0, c, INNER, p * P, (p + 1) * P) for c in range(DC)],
                                                 [(xT_hi[:, c, :], xT_lo[:, c, :]) for c in range(DC)])
                        last.then_inc(q_done, 1)
                    pe.wait_ge(qT_ready, it * 4 + 4)
                    pe.wait_ge(v_now_ready, b * 16 + 16)
                    for u in range(QUADS):
                        scores(u, it, b)
                        if u >= 2:
                            turn_probs(u - 2, it)
                        if u >= 3:
                            attend(u - 3, it)
                    turn_probs(6, it)
                    attend(5, it)
                    project_out(0, it)
                    turn_probs(7, it)
                    attend(6, it)
                    attend(7, it)
                    project_out(1, it)

        @block.scalar
        def _(act):
            for n in range(2):
                act.wait_ge(landed[n], 16)
                act.copy(W[n][0][:, :], stage[n][:, :]).then_inc(high_done, 1)
            act.wait_ge(zeroed, 3)
            for n in range(2 * B):
                b, f = n // 2, n % 2
                act.wait_ge(ctx_v_done, n + 1)
                act.copy(v_all[0:CTX, b, f * HALF:(f + 1) * HALF], bank[n % 2][0:CTX, :]).then_inc(ctx_v_ready, 1)

            def exp_scores(u, it):
                act.wait_ge(max_ready, it * QUADS + u + 1)
                for j in range(4):
                    last = act.activation(prob[:, u % 3, j, :], S_BANK[u % 3][:, j * CTX:(j + 1) * CTX], ACT.Exp,
                                          bias=neg_max[:, u, j:j + 1], accum_out=row_sum[:, u, j:j + 1])
                last.then_inc(exp_done, 1)

            def take_probT(u, it):
                act.wait_ge(prob_turned, it * QUADS + u + 1)
                act.copy(probT[0:CTX, u % 2, :, :].rearrange("p a b -> p (a b)"), PT_BANK[u % 2][0:CTX, :]
                         ).then_inc(probT_ready, 1)

            def take_att(u, it):
                t, f = u // 4, u % 4
                act.wait_ge(att_done, it * QUADS + u + 2)
                act.copy(attT_hi[:, 2 * f:2 * f + 2, t * P:(t + 1) * P],
                         ATT_BANK[u % 2][:, 0:2 * P].rearrange("p (a b) -> p a b", a=2)
                         ).then_inc(att_hi_ready, 1)

            with act.Fori(0, ITER) as it:
                act.wait_ge(x_turned, it + 1)
                act.copy(xT_hi[:, :, :].rearrange("p a b -> p (a b)"), bank[7][:, :]).then_inc(xT_hi_ready, 1)
                for f in range(4):
                    act.wait_ge(q_done, it * 4 + f + 1)
                    act.mul(qT[:, 2 * f:2 * f + 2, :].rearrange("p a b -> p (a b)"), bank[f][:, :], DH ** -0.5
                            ).then_inc(qT_ready, 1)
                for u in range(QUADS):
                    if u >= 2:
                        take_probT(u - 2, it)
                    exp_scores(u, it)
                    if u >= 3:
                        take_att(u - 3, it)
                take_probT(6, it)
                take_att(5, it)
                take_probT(7, it)
                take_att(6, it)
                take_att(7, it)

        @block.gpsimd
        def _(pool):
            pool.memset(ident[:, :], 0.0).then_inc(c_zero, 1)
            pool.memset(neg_half[:, :], -0.5).then_inc(c_zero, 1)
            pool.wait_ge(c_zero, 2)
            pool.affine_select(out=ident[:, :], in_=ident[:, :], compare_op=ALU.not_equal, fill=1.0, base=0,
                               pattern=[[-1, P]], channel_multiplier=1).then_inc(c_ident, 1)
            pool.wait_ge(bias_landed, 16)

            def normalise(u, it):
                pool.wait_ge(inv_ready, it * QUADS + u + 1)
                pool.tensor_tensor(prob[:, u % 3, :, :], prob[:, u % 3, :, :],
                                   row_inv[:, u, :].unsqueeze(2).to_broadcast([P, 4, CTX]), ALU.mult
                                   ).then_inc(prob_ready, 1)

            with pool.Fori(0, ITER) as it:
                pool.wait_ge(xres_landed, it * 16 + 16)
                pool.wait_ge(y_added, it * 2 + 2)
                pool.tensor_tensor(x_bias[:, :, :], x_res[:, :, :],
                                   bias_rows[:, :].unsqueeze(1).to_broadcast([P, 2, D]), ALU.add
                                   ).then_inc(xbias_ready, 1)
                for u in range(QUADS):
                    normalise(u, it)
                for t in range(2):
                    pool.wait_ge(var_ready, it * 2 + t + 1)
                    pool.tensor_tensor(rstd[:, t:t + 1], var_eps[:, t:t + 1], neg_half[:, :], ALU.pow
                                       ).then_inc(rstd_ready, 1)

        @block.vector
        def _(dve):
            dve.memset(k_pad[:, :, :, :, :].rearrange("p a b c d -> p (a b c d)"), 0.0).then_inc(zeroed, 1)
            dve.memset(v_all[:, :, :].rearrange("p a b -> p (a b)"), 0.0).then_inc(zeroed, 1)
            dve.memset(probT[:, :, :, :].rearrange("p a b c -> p (a b c)"), 0.0).then_inc(zeroed, 1)
            dve.memset(stats[:, :, :].rearrange("p a b -> p (a b)"), 0.0).then_inc(stored, 16)
            dve.memset(mean_var[:, :, :].rearrange("p a b -> p (a b)"), 0.0).then_inc(y_added, 2)
            dve.memset(spare[:, :], 0.0).then_inc(att_done, 1)
            dve.wait_ge(zeroed, 3)
            dve.wait_ge(ctx_turned, 1)
            for c in range(2):
                last = dve.tensor_copy(ctxT[:, c, :, :].rearrange("p b n -> p (b n)"), bank[c][0:CK, 0:B * CTX])
            last.then_inc(ctxT_ready, 1)
            for p in range(PAIRS):
                dve.wait_ge(ctx_k_done, p + 1)
                for h in range(2):
                    rows = slice(h * DH, (h + 1) * DH)
                    last = dve.tensor_copy(k_pad[rows, :, p, h, :],
                                           bank[2 + p % 6][rows, 0:B * CTX].rearrange("p (b n) -> p b n", b=B))
                last.then_inc(ctx_k_ready, 1)
            for n in range(2):
                dve.wait_ge(high_done, n + 1)
                dve.tensor_tensor(W[n][1][:, :], stage[n][:, :], W[n][0][:, :].bitcast(F32), ALU.subtract
                                  ).then_inc(low_done, 1)

            def maxima(u, it):
                dve.wait_ge(scores_done, it * QUADS + u + 1)
                dve.tensor_reduce(neg_max[:, u, :], S_BANK[u % 3][:, 0:4 * CTX].rearrange("p (a b) -> p a b", a=4),
                                  AX_X, ALU.max, negate=True).then_inc(max_ready, 1)

            def inverse(u, it):
                dve.wait_ge(exp_done, it * QUADS + u + 1)
                dve.reciprocal(row_inv[:, u, :], row_sum[:, u, :]).then_inc(inv_ready, 1)

            def low_att(u, it):
                t, f = u // 4, u % 4
                dve.wait_ge(att_hi_ready, it * QUADS + u + 1)
                s = slice(t * P, (t + 1) * P)
                dve.tensor_tensor(attT_lo[:, 2 * f:2 * f + 2, s],
                                  ATT_BANK[u % 2][:, 0:2 * P].rearrange("p (a b) -> p a b", a=2),
                                  attT_hi[:, 2 * f:2 * f + 2, s].bitcast(F32), ALU.subtract
                                  ).then_inc(att_lo_ready, 1)

            def residual(t, it):
                if t == 0:
                    dve.wait_ge(xbias_ready, it + 1)
                dve.wait_ge(y_done, it * 2 + t + 1)
                dve.tensor_tensor(y[:, t, :], Y_BANK[:, 0:D], x_bias[:, t, :], ALU.add).then_inc(y_added, 1)
                dve.wait_ge(y_added, it * 2 + 2 + t + 1)
                dve.bn_stats(stats[:, t, :], y[:, t, :]).then_inc(ln_step, 1)
                dve.wait_ge(ln_step, it * 4 + 2 * t + 1)
                dve.memset(spare[:, t:t + 1], 0.0)
                dve.bn_aggr(mean_var[:, t, :], stats[:, t, :]).then_inc(ln_step, 1)
                dve.wait_ge(ln_step, it * 4 + 2 * t + 2)
                dve.tensor_scalar(var_eps[:, t:t + 1], mean_var[:, t, 1:2], LN_EPS, None, ALU.add
                                  ).then_inc(var_ready, 1)

            def normalise(t, it):
                dve.wait_ge(rstd_ready, it * 2 + t + 1)
                dve.wait_ge(stored, it * 16 + 16)
                dve.tensor_scalar(normed[:, t, :], y[:, t, :], mean_var[:, t, 0:1], rstd[:, t:t + 1],
                                  ALU.subtract, ALU.mult).then_inc(normed_ready, 1)

            with dve.Fori(0, ITER) as it:
                dve.wait_ge(xT_hi_ready, it + 1)
                dve.tensor_tensor(xT_lo[:, :, :].rearrange("p a b -> p (a b)"), bank[7][:, :],
                                  xT_hi[:, :, :].rearrange("p a b -> p (a b)").bitcast(F32), ALU.subtract
                                  ).then_inc(xT_lo_ready, 1)
                for u in range(QUADS):
                    maxima(u, it)
                    if u >= 3:
                        low_att(u - 3, it)
                    inverse(u, it)
                low_att(5, it)
                residual(0, it)
                low_att(6, it)
                low_att(7, it)
                normalise(0, it)
                residual(1, it)
                normalise(1, it)


def emit_query_softmax(nc, x2, wq, wk, wv, wo, wff, parts, out):
    HD = D // H
    B, S = out.shape[0], out.shape[1]
    KT = S // P
    GROUPS = H // 4
    TILES = B * KT
    Q_PART = (0, 1, 0, 1, 2, 0, 2, 1)
    K_PART = (0, 0, 1, 1, 0, 2, 1, 2)
    outf = out.rearrange("b s d -> (b s) d")

    with ExitStack() as ctx:
        def sb(name, shape, dt=F32):
            return ctx.enter_context(nc.sbuf_tensor("f_" + name, shape, dt))

        def sem(name):
            return ctx.enter_context(nc.semaphore("f_" + name))

        ring = [ctx.enter_context(nc.psum_tensor(f"f_ring{i}", [P, S], F32)) for i in range(3)]
        acc = ctx.enter_context(nc.psum_tensor("f_acc", [P, S], F32))

        ident = sb("ident", [P, P])
        neg_half = sb("neg_half", [P, KT])
        W = [sb(f"w{n}_in", [P, DC, D]) for n in range(3)]
        W_hi = [sb(f"w{n}_hi", [P, DC, D], F32R) for n in range(3)]
        W_lo = [sb(f"w{n}_lo", [P, DC, D], F32R) for n in range(3)]
        w_out = sb("w_out", [P, GROUPS, D])
        w_ff = sb("w_ff", [P, DC, D])
        x_in = sb("x_in", [P, KT, D])
        xT_hi = sb("xT_hi", [P, DC, S], F32R)
        xT_lo = sb("xT_lo", [P, DC, S], F32R)
        third = sb("third", [P, 4, 3, S], BF16)
        rest = sb("rest", [P, 2, S])
        v = sb("v", [P, KT, D])
        q_stack = sb("q_stack", [P, 2, 4, S], BF16)
        k_stack = sb("k_stack", [P, 2, 4, S], BF16)
        neg_max = sb("neg_max", [P, 2, 4])
        row_sum = sb("row_sum", [P, 2, 4])
        row_inv = sb("row_inv", [P, 2, 4])
        prob = sb("prob", [P, 8, S])
        v_norm = sb("v_norm", [P, 2, 4, 32])
        zT = sb("zT", [P, GROUPS, S])
        z = v
        z2T = rest
        square = prob[:, 6:8, :].rearrange("p a (b d) -> p (a b) d", d=D)
        squares = sb("squares", [P, 2, KT])
        clamped = sb("clamped", [P, 2, KT])
        z_inv = sb("z_inv", [P, 2, KT])
        z_all = sb("z_all", [P, TILES, D])
        stats = sb("stats", [P, 4, 6])
        mean_var = sb("mean_var", [P, 4, 2])
        var_eps = sb("var_eps", [P, 4])
        rstd = sb("rstd", [P, 4])
        spare = sb("spare", [P, 4])
        x_fin = [prob[:, n, :] for n in range(2)]
        y_fin = [prob[:, 2 + n, :] for n in range(2)]
        o_fin = [prob[:, 4 + n, :] for n in range(2)]

        c_zero, c_ident, zeroed, w_landed = sem("zero"), sem("ident_done"), sem("zeroed"), sem("w_landed")
        high_done, low_done = sem("w_high"), sem("w_low")
        x_landed, x_turned, xT_hi_ready, xT_lo_ready = (sem("x_landed"), sem("x_turned"), sem("xT_hi_ready"),
                                                        sem("xT_lo_ready"))
        qk_done, first_ready, rest_ready, second_ready, third_ready = (
            sem("qk_done"), sem("first_ready"), sem("rest_ready"), sem("second_ready"), sem("third_ready"))
        v_done, v_ready, parts_stored, stack_landed = (sem("v_done"), sem("v_ready"), sem("parts_stored"),
                                                       [sem("stack0_landed"), sem("stack1_landed")])
        scores_done, max_ready, exp_done, inv_ready, vnorm_ready, pv_done = (
            sem("scores_done"), sem("max_ready"), sem("exp_done"), sem("inv_ready"), sem("vnorm_ready"),
            sem("pv_done"))
        zT_ready = sem("zT_ready")
        z_done, square_done, clamp_done, inv2_ready, z_ready = (sem("z_done"), sem("square_done"),
                                                                sem("clamp_done"), sem("inv2_ready"), sem("z_ready"))
        z_turned, zT2_ready, z2_done, z2_ready = sem("z_turned"), sem("zT2_ready"), sem("z2_done"), sem("z2_ready")
        gelu_done, xf_landed, yf_ready, ln_step, var_ready, rstd_ready, of_ready, stored = (
            sem("gelu_done"), [sem("xf0_landed"), sem("xf1_landed")], sem("yf_ready"), sem("ln_step"),
            sem("var_ready"), sem("rstd_ready"), sem("of_ready"), [sem("stored0"), sem("stored1")])

        block = ctx.enter_context(nc.Block())
        NSTACK = 16 * 16

        @block.sync
        def _(sp):
            for n, w in enumerate((wq, wk, wv)):
                sp.dma_start(W[n][:, :, :], w.rearrange("(c p) n -> p c n", p=P)).then_inc(w_landed, 16)
            sp.dma_start(w_ff[:, :, :], wff.rearrange("(c p) n -> p c n", p=P)).then_inc(w_landed, 16)
            sp.wait_ge(zeroed, 1)
            for j in range(4):
                sp.dma_start(w_out[32 * j:32 * j + HD, :, :],
                             wo.rearrange("(g h i) n -> h i g n", g=GROUPS, h=4)[j]).then_inc(w_landed, 16)

            def load_stacks(b, group, slot):
                for n, (stack, order) in enumerate(((q_stack, Q_PART), (k_stack, K_PART))):
                    for blk, part in enumerate(order):
                        src = parts[n, part, bass.ds(group * 4 * HD, 4 * HD), :].rearrange("(h i) s -> i h s", i=HD)
                        sp.dma_start(stack[blk * HD:(blk + 1) * HD, slot, :, :], src).then_inc(stack_landed[slot], 16)

            with sp.Fori(0, B) as b:
                sp.wait_ge(x_turned, b * 1 + 1)
                sp.dma_start(x_in[:, :, :], x2[bass.ds(b * S, S), :].rearrange("(t p) d -> p t d", p=P)
                             ).then_inc(x_landed, 16)
                for m in range(4):
                    sp.wait_ge(third_ready, b * 4 + m + 1)
                    sp.dma_start(parts[m // 2, :, (m % 2) * P:(m % 2 + 1) * P, :].rearrange("a p s -> p a s"),
                                 third[:, m, :, :]).then_inc(parts_stored, 16)
                sp.wait_ge(parts_stored, b * 64 + 64)
                for group in range(GROUPS):
                    if group >= 2:
                        sp.wait_ge(scores_done, b * 128 + (group - 1) * 32)
                    load_stacks(b, group, group % 2)
            for n in range(TILES // 4):
                if n < 2:
                    sp.wait_ge(zT_ready, B * GROUPS)
                else:
                    sp.wait_ge(yf_ready, n - 1)
                sp.dma_start(x_fin[n % 2].rearrange("p (t d) -> p t d", d=D),
                             x2[n * 4 * P:(n + 1) * 4 * P, :].rearrange("(t p) d -> p t d", p=P)
                             ).then_inc(xf_landed[n % 2], 16)

        @block.tensor
        def _(pe):
            pe.wait_ge(c_ident, 1)
            pe.wait_ge(low_done, 3)
            pe.wait_ge(w_landed, 16 * 8)

            def scores(b, step, j):
                n = step * 4 + j
                slot, kt = (step // KT) % 2, step % KT
                if n >= 3:
                    pe.wait_ge(exp_done, b * 128 + n - 2)
                for f in range(2):
                    last = pe.matmul(ring[n % 3][:, f * HALF:(f + 1) * HALF],
                                     k_stack[:, slot, j, kt * P:(kt + 1) * P],
                                     q_stack[:, slot, j, f * HALF:(f + 1) * HALF], start=True, stop=True)
                last.then_inc(scores_done, 1)

            def values(b, step):
                group, kt = step // KT, step % KT
                if kt == 0 and group > 0:
                    pe.wait_ge(zT_ready, b * GROUPS + group)
                pe.wait_ge(vnorm_ready, b * GROUPS * KT + step + 1 + 1)
                for f in range(2):
                    for j in range(4):
                        last = pe.matmul(acc[32 * j:32 * j + 32, f * HALF:(f + 1) * HALF],
                                         v_norm[:, step % 2, j, :],
                                         prob[:, (step % 2) * 4 + j, f * HALF:(f + 1) * HALF],
                                         start=kt == 0, stop=kt == KT - 1, skip_group_check=True)
                last.then_inc(pv_done, 1)

            with pe.Fori(0, B) as b:
                pe.wait_ge(x_landed, b * 16 + 16)
                pe.wait_ge(z2_ready, b + 1)
                for c in range(DC):
                    for t in range(KT):
                        last = pe.transpose(ring[c][:, t * P:(t + 1) * P], x_in[:, t, c * P:(c + 1) * P], ident[:, :])
                last.then_inc(x_turned, 1)
                pe.wait_ge(xT_hi_ready, b * 2 + 2)
                pe.wait_ge(xT_lo_ready, b * 2 + 2)
                xT = [(xT_hi[:, c, :], xT_lo[:, c, :]) for c in range(DC)]
                target = (ring[2], acc, ring[0], ring[1])
                for m in range(4):
                    n, s = m // 2, slice((m % 2) * P, (m % 2 + 1) * P)
                    for f in range(2):
                        last = split_matmuls(pe, target[m][:, f * HALF:(f + 1) * HALF],
                                             [(W_hi[n][:, c, s], W_lo[n][:, c, s]) for c in range(DC)],
                                             [tuple(a[:, f * HALF:(f + 1) * HALF] for a in xT[c]) for c in range(DC)])
                    last.then_inc(qk_done, 1)
                for t in range(KT):
                    if t % 4 == 0:
                        pe.wait_ge(rest_ready, b * 4 + t // 4 + 1)
                    s = slice(t * P, (t + 1) * P)
                    last = split_matmuls(pe, (ring[2], acc)[t // 4][:, (t % 4) * D:(t % 4 + 1) * D],
                                         [tuple(a[:, s] for a in xT[c]) for c in range(DC)],
                                         [(W_hi[2][:, c, :], W_lo[2][:, c, :]) for c in range(DC)])
                    if t % 4 == 3:
                        last.then_inc(v_done, 1)
                pe.wait_ge(rest_ready, b * 4 + 4)
                pe.wait_ge(v_ready, b * 2 + 2)
                for step in range(GROUPS * KT):
                    if step % KT == 0:
                        pe.wait_ge(stack_landed[(step // KT) % 2],
                                   b * 2 * NSTACK + (step // KT // 2 + 1) * NSTACK)
                    for j in range(3):
                        scores(b, step, j)
                    if step > 0:
                        values(b, step - 1)
                    scores(b, step, 3)
                values(b, GROUPS * KT - 1)
                pe.wait_ge(exp_done, b * 128 + 128)
                pe.wait_ge(zT_ready, b * GROUPS + GROUPS)
                for t in range(KT):
                    for g in range(GROUPS):
                        last = pe.matmul(ring[t // 4][:, (t % 4) * D:(t % 4 + 1) * D], zT[:, g, t * P:(t + 1) * P],
                                         w_out[:, g, :], start=g == 0, stop=g == GROUPS - 1)
                    last.then_inc(z_done, 1)
                pe.wait_ge(z_ready, b * 2 + 2)
                for c in range(DC):
                    for t in range(KT):
                        last = pe.transpose((ring[2], acc)[c][:, t * P:(t + 1) * P], z[:, t, c * P:(c + 1) * P],
                                            ident[:, :])
                last.then_inc(z_turned, 1)
                pe.wait_ge(zT2_ready, b * 2 + 2)
                for t in range(KT):
                    for c in range(DC):
                        last = pe.matmul(ring[t // 4][:, (t % 4) * D:(t % 4 + 1) * D], z2T[:, c, t * P:(t + 1) * P],
                                         w_ff[:, c, :], start=c == 0, stop=c == DC - 1)
                    last.then_inc(z2_done, 1)

        @block.scalar
        def _(act):
            def take_outputs(b, group):
                act.wait_ge(pv_done, b * GROUPS * KT + (group + 1) * KT + 2)
                act.copy(zT[:, group, :], acc[:, :]).then_inc(zT_ready, 1)

            for n in range(3):
                act.wait_ge(w_landed, 16 * 8)
                act.copy(W_hi[n][:, :, :].rearrange("p a b -> p (a b)"), W[n][:, :, :].rearrange("p a b -> p (a b)")
                         ).then_inc(high_done, 1)
            with act.Fori(0, B) as b:
                act.wait_ge(x_turned, b + 2)
                for c in range(DC):
                    act.copy(xT_hi[:, c, :], ring[c][:, :]).then_inc(xT_hi_ready, 1)
                for m in range(4):
                    scale = D ** -0.5 if m < 2 else 1.0
                    act.wait_ge(qk_done, b * 4 + m + 1)
                    act.mul(third[:, m, 0, :], (ring[2], acc, ring[0], ring[1])[m][:, :], scale
                            ).then_inc(first_ready, 1)
                    act.wait_ge(rest_ready, b * 4 + m + 1)
                    act.copy(third[:, m, 1, :], rest[:, m % 2, :]).then_inc(second_ready, 1)
                for f in range(2):
                    act.wait_ge(v_done, b * 2 + f + 1)
                    act.copy(v[:, 4 * f:4 * f + 4, :].rearrange("p a b -> p (a b)"), (ring[2], acc)[f][:, :]
                             ).then_inc(v_ready, 1)
                for step in range(GROUPS * KT):
                    act.wait_ge(pv_done, b * GROUPS * KT + step + 1)
                    for j in range(4):
                        n = step * 4 + j
                        act.wait_ge(max_ready, b * 128 + n + 1)
                        act.activation(prob[:, (step % 2) * 4 + j, :], ring[n % 3][:, :], ACT.Exp,
                                       bias=neg_max[:, step % 2, j:j + 1],
                                       accum_out=row_sum[:, step % 2, j:j + 1]).then_inc(exp_done, 1)
                    if step % KT == 0 and step > 0:
                        take_outputs(b, step // KT - 1)
                take_outputs(b, GROUPS - 1)
                for r, done in ((0, z_done), (1, z2_done)):
                    for t in range(KT):
                        act.wait_ge(done, b * KT + t // 2 * 2 + 2)
                        act.activation(square[:, t, :], ring[t // 4][:, (t % 4) * D:(t % 4 + 1) * D], ACT.Square,
                                       accum_out=squares[:, r, t:t + 1]).then_inc(square_done, 1)
                    if r == 0:
                        act.wait_ge(z_turned, b + 1)
                        for c in range(DC):
                            act.copy(z2T[:, c, :], (ring[2], acc)[c][:, :]).then_inc(zT2_ready, 1)
            for n in range(TILES // 4):
                act.wait_ge(z2_ready, B + 1)
                act.activation(z_all[:, 4 * n:4 * n + 4, :].rearrange("p a b -> p (a b)"),
                               z_all[:, 4 * n:4 * n + 4, :].rearrange("p a b -> p (a b)"), ACT.Gelu
                               ).then_inc(gelu_done, 1)
            for n in range(TILES // 4):
                act.wait_ge(of_ready, n + 1)
                act.dma_start(outf[n * 4 * P:(n + 1) * 4 * P, :].rearrange("(t p) d -> p t d", p=P),
                              o_fin[n % 2].rearrange("p (t d) -> p t d", d=D)).then_inc(stored[n % 2], 16)
            act.wait_ge(stored[0], 16 * (TILES // 8))
            act.wait_ge(stored[1], 16 * (TILES // 8))

        @block.gpsimd
        def _(pool):
            pool.memset(ident[:, :], 0.0).then_inc(c_zero, 1)
            pool.memset(neg_half[:, :], -0.5).then_inc(c_zero, 1)
            pool.memset(v_norm[:, :, :, :], 0.0).then_inc(c_zero, 1)
            pool.wait_ge(c_zero, 3)
            pool.affine_select(out=ident[:, :], in_=ident[:, :], compare_op=ALU.not_equal, fill=1.0, base=0,
                               pattern=[[-1, P]], channel_multiplier=1).then_inc(c_ident, 1)
            pool.wait_ge(c_ident, 1)
            pool.memset(spare[:, :], 0.0).then_inc(vnorm_ready, 1)
            with pool.Fori(0, B) as b:
                for step in range(GROUPS * KT):
                    group, kt = step // KT, step % KT
                    pool.wait_ge(inv_ready, b * GROUPS * KT + step + 1)
                    pool.tensor_tensor(v_norm[:, step % 2, :, 0:HD],
                                       v[:, kt, group * 4 * HD:(group + 1) * 4 * HD].rearrange(
                                           "p (h d) -> p h d", d=HD),
                                       row_inv[:, step % 2, :].unsqueeze(2).to_broadcast([P, 4, HD]), ALU.mult
                                       ).then_inc(vnorm_ready, 1)
                for r in range(2):
                    pool.wait_ge(clamp_done, b * 2 + r + 1)
                    pool.tensor_tensor(z_inv[:, r, :], clamped[:, r, :], neg_half[:, :], ALU.pow
                                       ).then_inc(inv2_ready, 1)
            for n in range(TILES // 4):
                pool.wait_ge(var_ready, n + 1)
                pool.tensor_tensor(rstd[:, :], var_eps[:, :], neg_half[:, 0:4], ALU.pow).then_inc(rstd_ready, 1)

        @block.vector
        def _(dve):
            dve.memset(w_out[:, :, :].rearrange("p a b -> p (a b)"), 0.0).then_inc(zeroed, 1)
            dve.memset(stats[:, 0, :], 0.0).then_inc(x_turned, 1)
            dve.memset(stats[:, 1, :], 0.0).then_inc(z2_ready, 1)
            dve.memset(stats[:, 2, :], 0.0).then_inc(pv_done, 2)
            for n in range(3):
                dve.wait_ge(high_done, n + 1)
                dve.tensor_tensor(W_lo[n][:, :, :].rearrange("p a b -> p (a b)"),
                                  W[n][:, :, :].rearrange("p a b -> p (a b)"),
                                  W_hi[n][:, :, :].rearrange("p a b -> p (a b)").bitcast(F32), ALU.subtract
                                  ).then_inc(low_done, 1)
            with dve.Fori(0, B) as b:
                for c in range(DC):
                    dve.wait_ge(xT_hi_ready, b * 2 + c + 1)
                    dve.tensor_tensor(xT_lo[:, c, :], ring[c][:, :], xT_hi[:, c, :].bitcast(F32), ALU.subtract
                                      ).then_inc(xT_lo_ready, 1)
                for m in range(4):
                    scale = D ** -0.5 if m < 2 else 1.0
                    dve.wait_ge(first_ready, b * 4 + m + 1)
                    if m >= 2:
                        dve.wait_ge(third_ready, b * 4 + m - 1)
                    dve.scalar_tensor_tensor(out=rest[:, m % 2, :], in0=(ring[2], acc, ring[0], ring[1])[m][:, :],
                                             scalar=scale, in1=third[:, m, 0, :], op0=ALU.mult,
                                             op1=ALU.subtract).then_inc(rest_ready, 1)
                    dve.wait_ge(second_ready, b * 4 + m + 1)
                    dve.tensor_tensor(third[:, m, 2, :], rest[:, m % 2, :], third[:, m, 1, :], ALU.subtract
                                      ).then_inc(third_ready, 1)

                def inverse(step):
                    dve.wait_ge(exp_done, b * 128 + step * 4 + 4)
                    dve.reciprocal(row_inv[:, step % 2, :], row_sum[:, step % 2, :]).then_inc(inv_ready, 1)

                for step in range(GROUPS * KT):
                    for j in range(4):
                        n = step * 4 + j
                        dve.wait_ge(scores_done, b * 128 + n + 1)
                        dve.tensor_reduce(neg_max[:, step % 2, j:j + 1], ring[n % 3][:, :], AX_X, ALU.max,
                                          negate=True).then_inc(max_ready, 1)
                        if j == 0 and step > 0:
                            inverse(step - 1)
                inverse(GROUPS * KT - 1)
                for r, dst in ((0, z[:, :, :]), (1, z_all[:, bass.ds(b * KT, KT), :])):
                    dve.wait_ge(square_done, b * 2 * KT + (r + 1) * KT)
                    dve.tensor_scalar(clamped[:, r, :], squares[:, r, :], 1e-24, None, ALU.max
                                      ).then_inc(clamp_done, 1)
                    dve.wait_ge(inv2_ready, b * 2 + r + 1)
                    for f in range(2):
                        last = dve.tensor_tensor(
                            dst[:, 4 * f:4 * f + 4, :], ring[f][:, :].rearrange("p (t d) -> p t d", d=D),
                            z_inv[:, r, 4 * f:4 * f + 4].unsqueeze(2).to_broadcast([P, 4, D]), ALU.mult)
                        if r == 0:
                            last.then_inc(z_ready, 1)
                    if r == 1:
                        last.then_inc(z2_ready, 1)
            for n in range(TILES // 4):
                dve.wait_ge(gelu_done, n + 1)
                dve.wait_ge(xf_landed[n % 2], 16 * (n // 2 + 1))
                dve.tensor_tensor(y_fin[n % 2], z_all[:, 4 * n:4 * n + 4, :].rearrange("p a b -> p (a b)"),
                                  x_fin[n % 2], ALU.add).then_inc(yf_ready, 1)
                dve.wait_ge(yf_ready, n + 1)
                for t in range(4):
                    last = dve.bn_stats(stats[:, t, :], y_fin[n % 2][:, t * D:(t + 1) * D])
                last.then_inc(ln_step, 1)
                dve.wait_ge(ln_step, 2 * n + 1)
                for t in range(4):
                    last = dve.bn_aggr(mean_var[:, t, :], stats[:, t, :])
                last.then_inc(ln_step, 1)
                dve.wait_ge(ln_step, 2 * n + 2)
                dve.tensor_scalar(var_eps[:, :], mean_var[:, :, 1], LN_EPS, None, ALU.add).then_inc(var_ready, 1)
                dve.wait_ge(rstd_ready, n + 1)
                if n >= 2:
                    dve.wait_ge(stored[n % 2], 16 * (n // 2))
                for t in range(4):
                    s = slice(t * D, (t + 1) * D)
                    last = dve.tensor_scalar(o_fin[n % 2][:, s], y_fin[n % 2][:, s], mean_var[:, t, 0:1],
                                             rstd[:, t:t + 1], ALU.subtract, ALU.mult)
                last.then_inc(of_ready, 1)


def build_layer(nc, x, ctx_768, attn_wq, attn_wk, attn_wv, attn_wo, betas, x_wq, x_wkv, x_wo, x_bias,
                f_wq, f_wk, f_wv, f_wo, f_wff, out):
    B, S, _ = x.shape
    x1 = nc.dram_tensor("after_attention", (B * S, D), F32).ap()
    x2 = nc.dram_tensor("after_cross_attention", (B * S, D), F32).ap()
    parts = nc.dram_tensor("qk_thirds", (2, 3, D, S), BF16).ap()
    emit_segment_attention(nc, x, attn_wq, attn_wk, attn_wv, attn_wo, betas, x1)
    emit_cross_attention(nc, x1, ctx_768, x_wq, x_wkv, x_wo, x_bias, x2)
    emit_query_softmax(nc, x2, f_wq, f_wk, f_wv, f_wo, f_wff, parts, out)


_INS = ['x', 'ctx_768', 'L0_attn_Wq', 'L0_attn_Wk', 'L0_attn_Wv', 'L0_attn_Wo', 'L0_attn_betas', 'L0_xattn_w_q',
        'L0_xattn_w_kv', 'L0_xattn_w_out', 'L0_xattn_b_out', 'L0_ffn_Wq', 'L0_ffn_Wk', 'L0_ffn_Wv', 'L0_ffn_Wo',
        'L0_ffn_Wff']


def kernel(**inputs):
    import concourse.bacc as _bacc
    from concourse.bass_utils import run_bass_kernel_spmd as _run

    nc = _bacc.Bacc("TRN2", target_bir_lowering=False, num_devices=1)
    arrays, args = {}, []
    for name in _INS:
        a = np.ascontiguousarray(inputs[name])
        arrays[f"in_{name}_dram"] = a
        args.append(nc.dram_tensor(f"in_{name}_dram", a.shape, mybir.dt.from_np(a.dtype), kind="ExternalInput").ap())
    args.append(nc.dram_tensor("out_0_dram", inputs["x"].shape, F32, kind="ExternalOutput").ap())
    build_layer(nc, *args)
    r = _run(nc, [arrays], core_ids=[0])
    return r.results[0]["out_0_dram"]
```

```python
from contextlib import ExitStack

import numpy as np
import concourse.bass as bass
from concourse import mybir

F32 = mybir.dt.float32
F32R = mybir.dt.float32r
BF16 = mybir.dt.bfloat16
ALU = mybir.AluOpType
ACT = mybir.ActivationFunctionType
AX_X = mybir.AxisListType.X

P = 128
D = 256
DC = D // P
H = 16
DH = 64
INNER = H * DH
PAIRS = H // 2
IC = INNER // P
HALF = 512
TOK = 2 * P
QUADS = 8
LN_EPS = 1e-5


def split_matmuls(pe, out, left, right):
    terms = []
    for (lh, ll), (rh, rl) in zip(left, right):
        terms += [(lh, rh), (lh, rl), (ll, rh)]
    for n, (a, b) in enumerate(terms):
        last = pe.matmul(out, a, b, start=n == 0, stop=n == len(terms) - 1)
    return last


def emit_segment_attention(nc, x, wq, wk, wv, wo, betas, x1):
    B, S, _ = x.shape
    ITER = B * S // TOK
    PER_BATCH = S // TOK
    xf = x.rearrange("b s d -> (b s) d")

    with ExitStack() as ctx:
        def sb(name, shape, dt=F32):
            return ctx.enter_context(nc.sbuf_tensor("a_" + name, shape, dt))

        def sem(name):
            return nc.alloc_semaphore("a_" + name)

        bank = [ctx.enter_context(nc.psum_tensor(f"a_bank{i}", [P, HALF], F32)) for i in range(8)]
        S_BANK, PT_BANK, ATT_BANK = bank[0:3], bank[3:5], bank[5:7]
        Y_BANK = (bank[2], bank[7])

        ident = sb("ident", [P, P])
        ident2 = sb("ident2", [P, DH])
        block_ones = sb("block_ones", [P, P])
        fold = sb("fold", [P, P])
        neg_half = sb("neg_half", [P, 1])
        beta_rows = sb("beta_rows", [P, INNER])
        beta_cols = sb("beta_cols", [P, PAIRS])
        gate_cols = sb("gate_cols", [P, PAIRS])
        x_in = sb("x_in", [P, 2, D])
        x_res = sb("x_res", [P, 2, D])
        xT_hi = sb("xT_hi", [P, DC, TOK], F32R)
        xT_lo = sb("xT_lo", [P, DC, TOK], F32R)
        qT = sb("qT", [P, 2 * PAIRS, H, 8])
        phi_qT = sb("phi_qT", [P, 4, HALF])
        phi_tok = sb("phi_tok", [P, 4, HALF])
        phiT = sb("phiT", [P, PAIRS, TOK])
        e_k = sb("e_k", [P, 2, HALF])
        relu_k = sb("relu_k", [P, 2, HALF])
        k_pad = sb("k_pad", [P, 2 * PAIRS, 2, H, 8])
        vT = sb("vT", [P, 2 * PAIRS, H, 8])
        v_tok = sb("v_tok", [P, 4, HALF])
        v_gated = sb("v_gated", [P, 4, HALF])
        mem = sb("mem", [P, PAIRS, DH])
        mem_w = sb("mem_w", [P, 2, PAIRS, P])
        z_part = sb("z_part", [P, PAIRS, 4 * PAIRS])
        z_fold = sb("z_fold", [P, 4 * PAIRS])
        z_sum = sb("z_sum", [P, 2, PAIRS])
        z_acc = sb("z_acc", [P, 3, PAIRS])
        z_inv = sb("z_inv", [P, 2, PAIRS])
        z_gate = sb("z_gate", [P, 2, PAIRS])
        z_diag = sb("z_diag", [P, 2, PAIRS, DH])
        s_sum = sb("s_sum", [P, 4, 8])
        s_inv = sb("s_inv", [P, 4, 8])
        neg_max = sb("neg_max", [P, QUADS, 4])
        row_sum = sb("row_sum", [P, QUADS, 4])
        row_inv = sb("row_inv", [P, QUADS, 4])
        prob = sb("prob", [P, 3, 4, P])
        probT = sb("probT", [P, 2, 4, P])
        attT_hi = sb("attT_hi", [P, PAIRS, TOK], F32R)
        attT_lo = sb("attT_lo", [P, PAIRS, TOK], F32R)
        y = sb("y", [P, 2, D])
        stats = sb("stats", [P, 2, 6])
        mean_var = sb("mean_var", [P, 2, 2])
        var_eps = sb("var_eps", [P, 2])
        rstd = sb("rstd", [P, 2])
        normed = sb("normed", [P, 2, D])
        spare = sb("spare", [P, 2])
        stage = [v_tok[:, :, :].rearrange("p a b -> p (a b)"), v_gated[:, :, :].rearrange("p a b -> p (a b)")]

        def w_in(w):
            return w.rearrange("(c p) n -> p c n", p=P)

        sources = [(w_in(w), 2048) for w in (wq, wk, wv, wo)]
        landed = [sem("w_landed0"), sem("w_landed1")]
        high_done, low_done = sem("w_high"), sem("w_low")
        W = []
        for n in range(4):
            W.append((sb(f"w{n}_hi", [P, 2048], F32R), sb(f"w{n}_lo", [P, 2048], F32R)))

        def w_cols(n, c, width, a, b):
            return tuple(w[:, c * width + a:c * width + b] for w in W[n])

        c_zero, c_set, c_ident, c_ones = sem("zero"), sem("set"), sem("ident_done"), sem("ones_done")
        beta_in, beta_exp, gate_ready = sem("beta_in"), sem("beta_exp"), sem("gate_ready")
        gate_step = sem("gate_step")
        x_landed, xres_landed = sem("x_landed"), sem("xres_landed")
        x_turned, xT_hi_ready, xT_lo_ready = sem("x_turned"), sem("xT_hi_ready"), sem("xT_lo_ready")
        q_done, qT_ready, q_exp, phi_ready = sem("q_done"), sem("qT_ready"), sem("q_exp"), sem("phi_ready")
        phi_tok_done, phi_tok_ready = sem("phi_tok_done"), sem("phi_tok_ready")
        ssum_ready, sinv_ready, phin_ready = sem("ssum_ready"), sem("sinv_ready"), sem("phin_ready")
        k_done, k_exp, k_padded, k_summed = sem("k_done"), sem("k_exp"), sem("k_padded"), sem("k_summed")
        phik_ready, zpart_ready, zfold_ready, zfold_done = (sem("phik_ready"), sem("zpart_ready"),
                                                            sem("zfold_ready"), sem("zfold_done"))
        z_read = sem("z_read")
        z_step, zgate_ready, zdiag_ready = sem("z_step"), sem("zgate_ready"), sem("zdiag_ready")
        v_done, vT_ready, v_turned, v_copied, v_gated_ready = (sem("v_done"), sem("vT_ready"), sem("v_turned"),
                                                                sem("v_copied"), sem("v_gated_ready"))
        mem_done, mem_added, gz_done, memw_ready = (sem("mem_done"), sem("mem_added"), sem("gz_done"),
                                                    sem("memw_ready"))
        phi_turned, phiT_ready = sem("phi_turned"), sem("phiT_ready")
        scores_done, max_ready, exp_done = sem("scores_done"), sem("max_ready"), sem("exp_done")
        inv_ready, prob_ready, prob_turned, probT_ready = (sem("inv_ready"), sem("prob_ready"),
                                                           sem("prob_turned"), sem("probT_ready"))
        att_done, att_hi_ready, att_lo_ready = sem("att_done"), sem("att_hi_ready"), sem("att_lo_ready")
        y_done, y_added, ln_step, var_ready, rstd_ready = (sem("y_done"), sem("y_added"), sem("ln_step"),
                                                           sem("var_ready"), sem("rstd_ready"))
        normed_ready, stored = sem("normed_ready"), sem("stored")

        def shift_source(b, r, e):
            return b[r * DH:(r + 1) * DH, :].rearrange("p (j e m i) -> p j e m i", j=2, e=2, i=8)[:, :, e, :, :]

        def shift_target(dst, r, e, f):
            return dst[e * DH:(e + 1) * DH, :, 4 * f + r:4 * f + r + 3:2, :].rearrange("p m j i -> p j m i")

        def att_source(u, e, r):
            return ATT_BANK[u % 2][e * DH:(e + 1) * DH, 0:2 * P].rearrange(
                "p (j q r i) -> p j q r i", j=2, r=2, i=8)[:, :, :, r, :]

        def att_block(dst, e, r, t, f):
            at = t * P + e * DH + 2 * f * 8
            return dst[r * DH:(r + 1) * DH, :, at:at + 16].rearrange("p q (j i) -> p j q i", j=2)

        block = ctx.enter_context(nc.Block())

        @block.sync
        def _(sp):
            for e in range(2):
                sp.dma_start(beta_rows[:, :].rearrange("p (g e d) -> p g e d", e=2, d=DH)[:, :, e, :],
                             betas[0, e * PAIRS:(e + 1) * PAIRS, 0, :].unsqueeze(0).to_broadcast([P, PAIRS, DH])
                             ).then_inc(beta_in, 16)
            with nc.allow_non_contiguous_dma(reason="1024 elements, once"):
                for e in range(2):
                    sp.dma_start(beta_cols[e * DH:(e + 1) * DH, :],
                                 betas[0, e * PAIRS:(e + 1) * PAIRS, 0, :].rearrange("g d -> d g")
                                 ).then_inc(beta_in, 16)
            for n, (src, cols) in enumerate(sources):
                if n >= 2:
                    sp.wait_ge(low_done, n - 1)
                dst = stage[n % 2].rearrange("p (c n) -> p c n", c=src.shape[1])
                sp.dma_start(dst, src).then_inc(landed[n % 2], 16)

            def tokens(array, it):
                return array[bass.ds(it * TOK, TOK), :].rearrange("(t p) d -> p t d", p=P)

            sp.dma_start(x_in[:, :, :], tokens(xf, 0)).then_inc(x_landed, 16)
            sp.dma_start(x_res[:, :, :], tokens(xf, 0)).then_inc(xres_landed, 16)
            with sp.Fori(0, ITER - 1) as it:
                sp.wait_ge(x_turned, it + 1)
                sp.dma_start(x_in[:, :, :], tokens(xf, it + 1)).then_inc(x_landed, 16)
                sp.wait_ge(normed_ready, it * 2 + 2)
                sp.dma_start(tokens(x1, it), normed[:, :, :]).then_inc(stored, 16)
                sp.dma_start(x_res[:, :, :], tokens(xf, it + 1)).then_inc(xres_landed, 16)
            sp.wait_ge(x_turned, ITER)
            sp.dma_start(x_in[:, :, :], tokens(xf, 0)).then_inc(x_landed, 16)
            sp.wait_ge(normed_ready, ITER * 2)
            sp.dma_start(tokens(x1, ITER - 1), normed[:, :, :]).then_inc(stored, 16)
            sp.wait_ge(stored, ITER * 16 + 16)

        @block.tensor
        def _(pe):
            def scores(u, it):
                t, f = u // 4, u % 4
                for j in range(2):
                    p = 2 * f + j
                    last = pe.matmul(S_BANK[u % 3][:, j * 256:(j + 1) * 256],
                                     qT[:, t * PAIRS + p, :, :].rearrange("p c i -> p (c i)"),
                                     k_pad[:, t * PAIRS + p, :, :, :].rearrange("p h c i -> p (h c i)"),
                                     start=True, stop=True)
                last.then_inc(scores_done, 1)

            def turn_probs(u, it):
                pe.wait_ge(prob_ready, it * QUADS + u + 1)
                for j in range(4):
                    last = pe.transpose(PT_BANK[u % 2][:, j * P:(j + 1) * P], prob[:, u % 3, j, :], ident[:, :])
                last.then_inc(prob_turned, 1)

            def attend(u, it):
                t, f = u // 4, u % 4
                pe.wait_ge(probT_ready, it * QUADS + u + 1)
                if u >= 2:
                    pe.wait_ge(att_lo_ready, it * QUADS + u - 1)
                for j in range(2):
                    p = 2 * f + j
                    out = ATT_BANK[u % 2][:, j * P:(j + 1) * P]
                    pe.matmul(out, mem_w[:, t, p, :], phiT[:, p, t * P:(t + 1) * P], start=True, stop=False,
                              skip_group_check=True)
                    for h in range(2):
                        c = (2 * p + h) * DH
                        last = pe.matmul(out[h * DH:(h + 1) * DH, :],
                                         v_gated[:, 2 * t + c // HALF, c % HALF:c % HALF + DH],
                                         probT[:, u % 2, 2 * j + h, :], start=False, stop=True,
                                         skip_group_check=True)
                last.then_inc(att_done, 1)

            def project_out(t, it):
                pe.wait_ge(att_hi_ready, it * QUADS + 4 * t + 4)
                pe.wait_ge(att_lo_ready, it * QUADS + 4 * t + 4)
                s = slice(t * P, (t + 1) * P)
                split_matmuls(pe, Y_BANK[t][:, 0:D],
                              [(attT_hi[:, p, s], attT_lo[:, p, s]) for p in range(PAIRS)],
                              [w_cols(3, p, D, 0, D) for p in range(PAIRS)]).then_inc(y_done, 1)

            pe.wait_ge(c_ident, 3)
            pe.wait_ge(c_ones, 6)
            pe.wait_ge(low_done, 4)
            def turn_x(it):
                pe.wait_ge(x_landed, it * 16 + 16)
                for t in range(2):
                    for c in range(DC):
                        last = pe.transpose(bank[4][:, c * TOK + t * P:c * TOK + (t + 1) * P],
                                            x_in[:, t, c * P:(c + 1) * P], ident[:, :])
                last.then_inc(x_turned, 1)

            turn_x(0)
            with pe.Fori(0, ITER) as it:
                pe.wait_ge(xT_hi_ready, it + 1)
                pe.wait_ge(xT_lo_ready, it + 1)
                xT = [(xT_hi[:, c, :], xT_lo[:, c, :]) for c in range(DC)]
                for n, done in ((0, q_done), (1, k_done), (2, v_done)):
                    for f in range(4):
                        if n == 2:
                            pe.wait_ge(qT_ready, it * 4 + f + 1)
                        if (n, f) == (0, 2):
                            pe.wait_ge(y_added, it * 2 + 1)
                        if (n, f) == (1, 3):
                            pe.wait_ge(y_added, it * 2 + 2)
                        for j in range(2):
                            p = 2 * f + j
                            last = split_matmuls(pe, bank[4 * (n % 2) + f][:, j * TOK:(j + 1) * TOK],
                                                 [w_cols(n, c, INNER, p * P, (p + 1) * P) for c in range(DC)], xT)
                        last.then_inc(done, 1)

                def turn(unit, source, target, done):
                    for j in range(4):
                        last = pe.transpose(target[:, j * P:(j + 1) * P], source[:, j * P:(j + 1) * P], ident[:, :])
                    last.then_inc(done, 1)

                pe.wait_ge(k_summed, it * 4 + 4)
                pe.wait_ge(k_padded, it * 4 + 4)
                for u in range(4):
                    pe.wait_ge(phi_ready, it * 4 + u + 1)
                    turn(u, phi_qT[:, u, :], bank[4 + u], phi_tok_done)
                pe.wait_ge(vT_ready, it * 4 + 4)
                for u in range(4):
                    turn(u, vT[:, 4 * u:4 * u + 4, :, :].rearrange("p m c i -> p (m c i)"), bank[u], v_turned)
                pe.wait_ge(phi_tok_ready, it * 4 + 1)
                pe.wait_ge(zfold_ready, it + 1)
                pe.matmul(bank[4][:, 0:4 * PAIRS], fold[:, :], z_fold[:, :], start=True, stop=True
                          ).then_inc(zfold_done, 1)

                def memory(t, banks):
                    pe.wait_ge(v_copied, it * 4 + 2 * t + 2)
                    pe.wait_ge(phi_tok_ready, it * 4 + 2 * t + 2)
                    for p in range(PAIRS):
                        u, c = 2 * t + p // 4, (p % 4) * P
                        last = pe.matmul(banks[p // 4][:, c:c + P], phi_tok[:, u, c:c + P], v_tok[:, u, c:c + P],
                                         start=True, stop=True)
                    last.then_inc(mem_done, 1)

                memory(0, bank[0:2])
                memory(1, bank[2:4])
                for t in range(2):
                    pe.wait_ge(zdiag_ready, it * 2 + t + 1)
                    pe.matmul(bank[5 + t][:, :], block_ones[:, :], z_diag[:, t, :, :].rearrange("p a b -> p (a b)"),
                              start=True, stop=True).then_inc(gz_done, 1)
                pe.wait_ge(mem_added, it * 2 + 1)
                scores(0, it)
                scores(1, it)
                for u in range(4):
                    pe.wait_ge(phin_ready, it * 4 + u + 1)
                    if u == 0:
                        pe.wait_ge(z_read, it + 1)
                    if u >= 2:
                        pe.wait_ge(memw_ready, it * 2 + u - 1)
                    turn(u, phi_qT[:, u, :], bank[(4, 7, 5, 6)[u]], phi_turned)
                pe.wait_ge(mem_added, it * 2 + 2)
                for u in range(2, QUADS):
                    scores(u, it)
                    if u == 3:
                        pe.wait_ge(phiT_ready, it * 4 + 4)
                    turn_probs(u - 2, it)
                    if u == 3:
                        pe.wait_ge(v_gated_ready, it * 4 + 4)
                    if u >= 3:
                        attend(u - 3, it)
                turn_probs(6, it)
                attend(5, it)
                project_out(0, it)
                turn_probs(7, it)
                attend(6, it)
                attend(7, it)
                turn_x(it + 1)
                project_out(1, it)

        @block.scalar
        def _(act):
            act.wait_ge(beta_in, 64)
            act.activation(beta_rows[:, :], beta_rows[:, :], ACT.Exp, scale=-1.0).then_inc(beta_exp, 1)
            act.activation(beta_cols[:, :], beta_cols[:, :], ACT.Exp, scale=-1.0).then_inc(beta_exp, 1)
            for n in range(4):
                act.wait_ge(landed[n % 2], 16 * (n // 2 + 1))
                act.copy(W[n][0][:, :], stage[n % 2]).then_inc(high_done, 1)

            def exp_scores(u, it):
                act.wait_ge(max_ready, it * QUADS + u + 1)
                for j in range(4):
                    last = act.activation(prob[:, u % 3, j, :], S_BANK[u % 3][:, j * P:(j + 1) * P], ACT.Exp,
                                          bias=neg_max[:, u, j:j + 1], accum_out=row_sum[:, u, j:j + 1])
                last.then_inc(exp_done, 1)

            def high_x(it):
                act.wait_ge(x_turned, it + 1)
                for c in range(DC):
                    last = act.copy(xT_hi[:, c, :].rearrange("p (e t n) -> p t e n", e=2, t=2),
                                    bank[4][:, c * TOK:(c + 1) * TOK].rearrange("p (t e n) -> p t e n", e=2, t=2))
                last.then_inc(xT_hi_ready, 1)

            def take_att(u, it):
                t, f = u // 4, u % 4
                act.wait_ge(att_done, it * QUADS + u + 1)
                for e in range(2):
                    for r in range(2):
                        last = act.copy(att_block(attT_hi, e, r, t, f), att_source(u, e, r))
                last.then_inc(att_hi_ready, 1)

            high_x(0)
            with act.Fori(0, ITER) as it:
                for f in range(4):
                    act.wait_ge(q_done, it * 4 + f + 1)
                    for r in range(2):
                        for e in range(2):
                            last = act.copy(shift_target(qT, r, e, f), shift_source(bank[f], r, e))
                    last.then_inc(qT_ready, 1)
                for f in range(4):
                    act.wait_ge(k_done, it * 4 + f + 1)
                    if f >= 2:
                        act.wait_ge(k_summed, it * 4 + f - 1)
                    act.activation(e_k[:, f % 2, :], bank[4 + f][:, :], ACT.Exp)
                    act.activation(relu_k[:, f % 2, :], bank[4 + f][:, :], ACT.Relu).then_inc(k_exp, 1)
                act.wait_ge(qT_ready, it * 4 + 4)
                for u in range(4):
                    q_unit = qT[:, 4 * u:4 * u + 4, :, :].rearrange("p m c i -> p (m c i)")
                    act.activation(phi_qT[:, u, :], q_unit, ACT.Exp)
                    act.activation(phi_tok[:, u, :], q_unit, ACT.Relu).then_inc(q_exp, 1)
                for f in range(2):
                    act.wait_ge(v_done, it * 4 + f + 1)
                    for r in range(2):
                        for e in range(2):
                            last = act.copy(shift_target(vT, r, e, f), shift_source(bank[f], r, e))
                    last.then_inc(vT_ready, 1)
                for u in range(4):
                    act.wait_ge(phi_tok_done, it * 4 + u + 1)
                    act.copy(phi_tok[:, u, :], bank[4 + u][:, :]).then_inc(phi_tok_ready, 1)
                for u in range(4):
                    act.wait_ge(v_turned, it * 4 + u + 1)
                    act.copy(v_tok[:, u, :], bank[u][:, :]).then_inc(v_copied, 1)
                exp_scores(0, it)
                for u in range(4):
                    t, f = u // 2, u % 2
                    if u == 2:
                        exp_scores(1, it)
                    act.wait_ge(phi_turned, it * 4 + u + 1)
                    act.copy(phiT[:, 4 * f:4 * f + 4, t * P:(t + 1) * P],
                             bank[(4, 7, 5, 6)[u]][:, :].rearrange("p (a b) -> p a b", a=4)
                             ).then_inc(phiT_ready, 1)
                for u in range(2, QUADS):
                    exp_scores(u, it)
                    if u >= 3:
                        take_att(u - 3, it)
                take_att(5, it)
                take_att(6, it)
                take_att(7, it)
                high_x(it + 1)

        @block.gpsimd
        def _(pool):
            pool.memset(ident[:, :], 0.0).then_inc(c_zero, 1)
            pool.memset(ident2[:, :], 0.0).then_inc(c_zero, 1)
            pool.memset(block_ones[:, :], 0.0).then_inc(c_zero, 1)
            pool.memset(fold[:, :], 0.0).then_inc(c_zero, 1)
            pool.memset(neg_half[:, :], -0.5).then_inc(c_set, 1)
            pool.wait_ge(c_zero, 4)
            pool.affine_select(out=ident[:, :], in_=ident[:, :], compare_op=ALU.not_equal, fill=1.0, base=0,
                               pattern=[[-1, P]], channel_multiplier=1).then_inc(c_ident, 1)
            for h in range(2):
                rows = ident2[h * DH:(h + 1) * DH, :]
                pool.wait_ge(c_ident, h + 1)
                pool.affine_select(out=rows, in_=rows, compare_op=ALU.not_equal, fill=1.0, base=0,
                                   pattern=[[-1, DH]], channel_multiplier=1).then_inc(c_ident, 1)
                pool.wait_ge(c_ident, h + 2)
                pool.memset(block_ones[h * DH:(h + 1) * DH, h * DH:(h + 1) * DH], 1.0).then_inc(c_ones, 1)
                pool.wait_ge(c_ones, 3 * h + 1)
                for g in range(2):
                    block_of = fold[h * DH:(h + 1) * DH, g * DH:(g + 1) * DH]
                    pool.affine_select(out=block_of, in_=block_of, compare_op=ALU.not_equal, fill=1.0, base=0,
                                       pattern=[[-1, DH]], channel_multiplier=1).then_inc(c_ones, 1)
                    pool.wait_ge(c_ones, 3 * h + g + 2)
            pool.wait_ge(c_ident, 3)
            pool.wait_ge(c_set, 1)
            pool.wait_ge(gate_ready, 2)

            def normalise(u, it):
                pool.wait_ge(inv_ready, it * QUADS + u + 1)
                pool.tensor_tensor(prob[:, u % 3, :, :], prob[:, u % 3, :, :],
                                   row_inv[:, u, :].unsqueeze(2).to_broadcast([P, 4, P]), ALU.mult
                                   ).then_inc(prob_ready, 1)

            def root(t, it):
                pool.wait_ge(var_ready, it * 2 + t + 1)
                pool.tensor_tensor(rstd[:, t:t + 1], var_eps[:, t:t + 1], neg_half[:, :], ALU.pow
                                   ).then_inc(rstd_ready, 1)

            with pool.Fori(0, ITER) as it:
                for u in range(4):
                    pool.wait_ge(sinv_ready, it * 4 + u + 1)
                    pool.tensor_tensor(phi_qT[:, u, :].rearrange("p (h d) -> p h d", d=DH),
                                       phi_tok[:, u, :].rearrange("p (h d) -> p h d", d=DH),
                                       s_inv[:, u, :].unsqueeze(2).to_broadcast([P, 8, DH]), ALU.mult
                                       ).then_inc(phin_ready, 1)
                for t in range(2):
                    pool.wait_ge(zgate_ready, it * 2 + t + 1)
                    pool.tensor_tensor(z_diag[:, t, :, :], ident2[:, :].unsqueeze(1).to_broadcast([P, PAIRS, DH]),
                                       z_gate[:, t, :].unsqueeze(2).to_broadcast([P, PAIRS, DH]), ALU.mult
                                       ).then_inc(zdiag_ready, 1)
                for u in range(4):
                    f = u % 2
                    pool.wait_ge(v_copied, it * 4 + u + 1)
                    pool.tensor_tensor(v_gated[:, u, :], v_tok[:, u, :], beta_rows[:, f * HALF:(f + 1) * HALF],
                                       ALU.mult).then_inc(v_gated_ready, 1)
                for u in range(QUADS):
                    normalise(u, it)
                root(0, it)
                root(1, it)

        @block.vector
        def _(dve):
            dve.wait_ge(beta_exp, 2)
            dve.tensor_scalar(beta_rows[:, :], beta_rows[:, :], 1.0, None, ALU.add).then_inc(gate_step, 1)
            dve.tensor_scalar(beta_cols[:, :], beta_cols[:, :], 1.0, None, ALU.add).then_inc(gate_step, 1)
            dve.wait_ge(gate_step, 2)
            dve.reciprocal(beta_rows[:, :], beta_rows[:, :]).then_inc(gate_step, 1)
            dve.reciprocal(gate_cols[:, :], beta_cols[:, :]).then_inc(gate_ready, 1)
            dve.wait_ge(gate_step, 3)
            dve.tensor_scalar(beta_rows[:, :], beta_rows[:, :], -1.0, 1.0, ALU.mult, ALU.add
                              ).then_inc(gate_ready, 1)
            dve.wait_ge(gate_ready, 2)
            dve.memset(k_pad[:, :, :, :, :].rearrange("p a b c d -> p (a b c d)"), 0.0)
            dve.memset(mem_w[:, :, :, :].rearrange("p a b c -> p (a b c)"), 0.0).then_inc(gate_step, 1)
            dve.memset(stats[:, :, :].rearrange("p a b -> p (a b)"), 0.0).then_inc(stored, 16)
            dve.memset(mean_var[:, :, :].rearrange("p a b -> p (a b)"), 0.0).then_inc(y_added, 2)
            dve.wait_ge(gate_step, 4)
            for n in range(4):
                dve.wait_ge(high_done, n + 1)
                dve.tensor_tensor(W[n][1][:, :], stage[n % 2], W[n][0][:, :].bitcast(F32), ALU.subtract
                                  ).then_inc(low_done, 1)
            dve.wait_ge(low_done, 4)

            def maxima(u, it):
                dve.wait_ge(scores_done, it * QUADS + u + 1)
                dve.tensor_reduce(neg_max[:, u, :], S_BANK[u % 3][:, :].rearrange("p (a b) -> p a b", a=4),
                                  AX_X, ALU.max, negate=True).then_inc(max_ready, 1)

            def inverse(u, it):
                dve.wait_ge(exp_done, it * QUADS + u + 1)
                dve.reciprocal(row_inv[:, u, :], row_sum[:, u, :]).then_inc(inv_ready, 1)

            def low_att(u, it):
                t, f = u // 4, u % 4
                dve.wait_ge(att_hi_ready, it * QUADS + u + 1)
                for e in range(2):
                    for r in range(2):
                        last = dve.tensor_tensor(att_block(attT_lo, e, r, t, f), att_source(u, e, r),
                                                 att_block(attT_hi, e, r, t, f).bitcast(F32), ALU.subtract)
                last.then_inc(att_lo_ready, 1)

            def residual(t, it):
                if t == 0:
                    dve.wait_ge(xres_landed, it * 16 + 16)
                dve.wait_ge(y_done, it * 2 + t + 1)
                dve.tensor_tensor(y[:, t, :], Y_BANK[t][:, 0:D], x_res[:, t, :], ALU.add).then_inc(y_added, 1)
                dve.wait_ge(y_added, it * 2 + 2 + t + 1)
                dve.bn_stats(stats[:, t, :], y[:, t, :]).then_inc(ln_step, 1)
                dve.wait_ge(ln_step, it * 4 + 2 * t + 1)
                dve.memset(spare[:, t:t + 1], 0.0)
                dve.bn_aggr(mean_var[:, t, :], stats[:, t, :]).then_inc(ln_step, 1)
                dve.wait_ge(ln_step, it * 4 + 2 * t + 2)
                dve.tensor_scalar(var_eps[:, t:t + 1], mean_var[:, t, 1:2], LN_EPS, None, ALU.add
                                  ).then_inc(var_ready, 1)

            def normalise(t, it):
                dve.wait_ge(rstd_ready, it * 2 + t + 1)
                dve.wait_ge(stored, it * 16 + 16)
                dve.tensor_scalar(normed[:, t, :], y[:, t, :], mean_var[:, t, 0:1], rstd[:, t:t + 1],
                                  ALU.subtract, ALU.mult).then_inc(normed_ready, 1)

            def take_probT(u, it):
                dve.wait_ge(prob_turned, it * QUADS + u + 1)
                dve.tensor_copy(probT[:, u % 2, :, :].rearrange("p a b -> p (a b)"), PT_BANK[u % 2][:, :]
                                ).then_inc(probT_ready, 1)

            def low_x(it):
                dve.wait_ge(xT_hi_ready, it + 1)
                for c in range(DC):
                    last = dve.tensor_tensor(
                        xT_lo[:, c, :].rearrange("p (e t n) -> p t e n", e=2, t=2),
                        bank[4][:, c * TOK:(c + 1) * TOK].rearrange("p (t e n) -> p t e n", e=2, t=2),
                        xT_hi[:, c, :].rearrange("p (e t n) -> p t e n", e=2, t=2).bitcast(F32), ALU.subtract)
                last.then_inc(xT_lo_ready, 1)

            low_x(0)
            with dve.Fori(0, B) as b:
                dve.memset(mem[:, :, :].rearrange("p a b -> p (a b)"), 0.0).then_inc(z_step, 1)
                dve.memset(z_acc[:, 2, :], 0.0).then_inc(z_step, 1)
                with dve.Fori(0, PER_BATCH) as n:
                    it = b * PER_BATCH + n
                    zb = b * (2 + 4 * PER_BATCH) + n * 4 + 2
                    for f in range(4):
                        dve.wait_ge(k_done, it * 4 + f + 1)
                        dve.wait_ge(k_exp, it * 4 + f + 1)
                        for r in range(2):
                            for e in range(2):
                                last = dve.tensor_scalar(shift_target(k_pad[:, :, e, :, :], r, e, f),
                                                         shift_source(bank[4 + f], r, e), DH ** -0.5, None, ALU.mult)
                        last.then_inc(k_padded, 1)
                        dve.scalar_tensor_tensor(out=e_k[:, f % 2, :], in0=e_k[:, f % 2, :], scalar=1.0,
                                                 in1=relu_k[:, f % 2, :], op0=ALU.min, op1=ALU.add
                                                 ).then_inc(phik_ready, 1)
                        dve.wait_ge(phik_ready, it * 4 + f + 1)
                        dve.tensor_reduce(z_part[:, 2 * f:2 * f + 2, :].rearrange("p j m -> p (j m)"),
                                          e_k[:, f % 2, :].rearrange("p (m i) -> p m i", i=8), AX_X, ALU.add
                                          ).then_inc(k_summed, 1)
                    for u in range(4):
                        dve.wait_ge(q_exp, it * 4 + u + 1)
                        dve.scalar_tensor_tensor(out=phi_qT[:, u, :], in0=phi_qT[:, u, :], scalar=1.0,
                                                 in1=phi_tok[:, u, :], op0=ALU.min, op1=ALU.add
                                                 ).then_inc(phi_ready, 1)
                    dve.wait_ge(k_summed, it * 4 + 4)
                    dve.tensor_reduce(z_fold[:, :], z_part[:, :, :].rearrange("p a m -> p m a"), AX_X, ALU.add
                                      ).then_inc(zfold_ready, 1)
                    for f in range(2, 4):
                        dve.wait_ge(v_done, it * 4 + f + 1)
                        for r in range(2):
                            for e in range(2):
                                last = dve.tensor_copy(shift_target(vT, r, e, f), shift_source(bank[f], r, e))
                        last.then_inc(vT_ready, 1)
                    for u in range(4):
                        dve.wait_ge(phi_tok_ready, it * 4 + u + 1)
                        dve.tensor_reduce(s_sum[:, u, :], phi_tok[:, u, :].rearrange("p (h d) -> p h d", d=DH),
                                          AX_X, ALU.add).then_inc(ssum_ready, 1)
                        dve.wait_ge(ssum_ready, it * 4 + u + 1)
                        dve.reciprocal(s_inv[:, u, :], s_sum[:, u, :]).then_inc(sinv_ready, 1)
                    dve.wait_ge(zfold_done, it + 1)
                    for e in range(2):
                        rows = slice(e * DH, (e + 1) * DH)
                        last = dve.tensor_copy(z_sum[rows, :, :].rearrange("p t g -> p (t g)"),
                                               bank[4][rows, e * 16:(e + 1) * 16])
                    last.then_inc(z_read, 1)
                    dve.wait_ge(z_read, it + 1)
                    dve.wait_ge(z_step, zb)
                    dve.tensor_tensor(z_acc[:, 0, :], z_acc[:, 2, :], z_sum[:, 0, :], ALU.add).then_inc(z_step, 1)
                    dve.wait_ge(z_step, zb + 1)
                    dve.tensor_tensor(z_acc[:, 1, :], z_acc[:, 0, :], z_sum[:, 1, :], ALU.add).then_inc(z_step, 1)
                    dve.wait_ge(z_step, zb + 2)
                    dve.tensor_copy(z_acc[:, 2, :], z_acc[:, 1, :]).then_inc(z_step, 1)
                    dve.reciprocal(z_inv[:, :, :], z_acc[:, 0:2, :]).then_inc(z_step, 1)
                    dve.wait_ge(z_step, zb + 4)
                    for t in range(2):
                        dve.tensor_tensor(z_gate[:, t, :], z_inv[:, t, :], gate_cols[:, :], ALU.mult
                                          ).then_inc(zgate_ready, 1)
                    for t in range(2):
                        banks = (bank[0:2], bank[2:4])[t]
                        if t == 1:
                            dve.wait_ge(memw_ready, it * 2 + 1)
                        dve.wait_ge(mem_done, it * 2 + t + 1)
                        for h in range(2):
                            rows = slice(h * DH, (h + 1) * DH)
                            for g in range(2):
                                m = mem[rows, 4 * g:4 * g + 4, :]
                                last = dve.tensor_tensor(
                                    m, banks[g][rows, :].rearrange("p (a h d) -> p a h d", a=4, h=2)[:, :, h, :],
                                    m, ALU.add)
                        last.then_inc(mem_added, 1)
                        dve.wait_ge(mem_added, it * 2 + t + 1)
                        dve.wait_ge(gz_done, it * 2 + t + 1)
                        for h in range(2):
                            rows = slice(h * DH, (h + 1) * DH)
                            last = dve.tensor_tensor(
                                mem_w[rows, t, :, h * DH:(h + 1) * DH],
                                bank[5 + t][rows, :].rearrange("p (a d) -> p a d", a=PAIRS),
                                mem[rows, :, :], ALU.mult)
                        last.then_inc(memw_ready, 1)
                    maxima(0, it)
                    maxima(1, it)
                    inverse(0, it)
                    inverse(1, it)
                    for u in range(2, QUADS):
                        maxima(u, it)
                        take_probT(u - 2, it)
                        if u >= 4:
                            low_att(u - 4, it)
                        inverse(u, it)
                    take_probT(6, it)
                    low_att(4, it)
                    take_probT(7, it)
                    low_att(5, it)
                    low_att(6, it)
                    low_att(7, it)
                    low_x(it + 1)
                    residual(0, it)
                    normalise(0, it)
                    residual(1, it)
                    normalise(1, it)


def emit_cross_attention(nc, x1, context, wq, wkv, wo, bias, x2):
    B, CTX, CD = context.shape
    CK = CD // 2
    ITER = x2.shape[0] // TOK
    PER_BATCH = ITER // B
    NW = 2 * CTX

    with ExitStack() as ctx:
        def sb(name, shape, dt=F32):
            return ctx.enter_context(nc.sbuf_tensor("x_" + name, shape, dt))

        def sem(name):
            return nc.alloc_semaphore("x_" + name)

        bank = [ctx.enter_context(nc.psum_tensor(f"x_bank{i}", [P, HALF], F32)) for i in range(8)]
        S_BANK, PT_BANK, ATT_BANK, Q_BANK, Y_BANK = bank[0:2], bank[2:4], bank[4:6], bank[6], bank[7]

        ident = sb("ident", [P, P])
        neg_half = sb("neg_half", [P, 1])
        bias_rows = sb("bias_rows", [P, D])
        ctx_in = sb("ctx_in", [CTX, B, CD])
        ctxT = sb("ctxT", [CK, 2, B, CTX])
        w_kv = sb("w_kv", [CK, 2, 2 * INNER])
        k_pad = sb("k_pad", [P, B, PAIRS, 2, CTX])
        v_all = sb("v_all", [P, B, INNER])
        v_now = sb("v_now", [P, INNER])
        x_in = sb("x_in", [P, 2, D])
        x_res = sb("x_res", [P, 2, D])
        x_bias = sb("x_bias", [P, 2, D])
        xT_hi = sb("xT_hi", [P, DC, TOK], F32R)
        xT_lo = sb("xT_lo", [P, DC, TOK], F32R)
        qT = sb("qT", [P, 2, PAIRS, TOK])
        neg_max = sb("neg_max", [P, QUADS, 4])
        row_sum = sb("row_sum", [P, QUADS, 4])
        row_inv = sb("row_inv", [P, QUADS, 4])
        prob = sb("prob", [P, 4, 4, CTX])
        probT = sb("probT", [P, 2, 4, P])
        attT_hi = sb("attT_hi", [P, 4, 2, P], F32R)
        attT_lo = sb("attT_lo", [P, 4, 2, P], F32R)
        y = sb("y", [P, 2, D])
        stats = sb("stats", [P, 2, 6])
        mean_var = sb("mean_var", [P, 2, 2])
        var_eps = sb("var_eps", [P, 2])
        rstd = sb("rstd", [P, 2])
        normed = sb("normed", [P, 2, D])
        spare = sb("spare", [P, 2])
        stage = [sb(f"stage{n}", [P, 2048]) for n in range(2)]
        sources = [w.rearrange("(c p) n -> p c n", p=P) for w in (wq, wo)]
        W = [(sb(f"w{n}_hi", [P, 2048], F32R), sb(f"w{n}_lo", [P, 2048], F32R)) for n in range(2)]

        def w_cols(n, c, width, a, b):
            return tuple(w[:, c * width + a:c * width + b] for w in W[n])

        c_zero, c_ident, zeroed = sem("zero"), sem("ident_done"), sem("zeroed")
        landed = [sem("w_landed0"), sem("w_landed1")]
        high_done, low_done, ctx_landed, wkv_landed, bias_landed = (sem("w_high"), sem("w_low"), sem("ctx_landed"),
                                                                    sem("wkv_landed"), sem("bias_landed"))
        ctx_turned, ctxT_ready, ctx_k_done, ctx_k_ready = (sem("ctx_turned"), sem("ctxT_ready"),
                                                           sem("ctx_k_done"), sem("ctx_k_ready"))
        ctx_v_done, ctx_v_ready = sem("ctx_v_done"), sem("ctx_v_ready")
        v_landed = [sem(f"v_landed{f}") for f in range(4)]
        x_landed, xres_landed, xbias_ready = sem("x_landed"), sem("xres_landed"), sem("xbias_ready")
        x_turned, xT_hi_ready, xT_lo_ready = sem("x_turned"), sem("xT_hi_ready"), sem("xT_lo_ready")
        q_done, qT_ready = sem("q_done"), sem("qT_ready")
        scores_done, max_ready, exp_done = sem("scores_done"), sem("max_ready"), sem("exp_done")
        inv_ready, prob_ready, prob_turned, probT_ready = (sem("inv_ready"), sem("prob_ready"),
                                                           sem("prob_turned"), sem("probT_ready"))
        att_done, att_hi_ready, att_lo_ready = sem("att_done"), sem("att_hi_ready"), sem("att_lo_ready")
        y_done, y_added, ln_step, var_ready, rstd_ready = (sem("y_done"), sem("y_added"), sem("ln_step"),
                                                           sem("var_ready"), sem("rstd_ready"))
        normed_ready, stored = sem("normed_ready"), sem("stored")

        TURN, ATTEND, PROJECT = 2, 3, 5

        def all_pairs(engine, pair):
            pair(0, 0, True)
            with engine.Fori(1, PER_BATCH // 2) as n:
                pair(0, n, False)
            with engine.Fori(1, B) as b:
                with engine.Fori(0, PER_BATCH // 2) as n:
                    pair(b, b * (PER_BATCH // 2) + n, False)

        block = ctx.enter_context(nc.Block())

        @block.sync
        def _(sp):
            sp.dma_start(ctx_in[:, :, :], context.rearrange("b s d -> s b d")).then_inc(ctx_landed, 16)
            sp.dma_start(w_kv[:, :, :], wkv.rearrange("(c p) n -> p c n", p=CK)).then_inc(wkv_landed, 16)
            for n in range(2):
                sp.dma_start(stage[n][:, :].rearrange("p (c n) -> p c n", c=sources[n].shape[1]), sources[n]
                             ).then_inc(landed[n], 16)
            sp.dma_start(bias_rows[:, :], bias.unsqueeze(0).to_broadcast([P, D])).then_inc(bias_landed, 16)

            def tokens(array, it):
                return array[bass.ds(it * TOK, TOK), :].rearrange("(t p) d -> p t d", p=P)

            sp.dma_start(x_in[:, :, :], tokens(x1, 0)).then_inc(x_landed, 16)
            sp.dma_start(x_res[:, :, :], tokens(x1, 0)).then_inc(xres_landed, 16)
            sp.wait_ge(ctx_v_ready, 2 * B)

            sp.wait_ge(x_turned, 1)
            sp.dma_start(x_in[:, :, :], tokens(x1, 1)).then_inc(x_landed, 16)

            def values(b, first=False):
                for f in range(4):
                    if not first:
                        sp.wait_ge(att_done, b * (PER_BATCH * QUADS) - 3 + f)
                    sp.dma_start(v_now[:, f * 4 * DH:(f + 1) * 4 * DH],
                                 v_all[:, bass.ds(b, 1), f * 4 * DH:(f + 1) * 4 * DH].rearrange("p b n -> p (b n)")
                                 ).then_inc(v_landed[f], 16)

            def ahead(it, distance):
                sp.wait_ge(x_turned, it + 2)
                sp.dma_start(x_in[:, :, :], tokens(x1, it + distance)).then_inc(x_landed, 16)

            def forward(it):
                sp.wait_ge(normed_ready, it * 2)
                sp.dma_start(tokens(x2, it - 1), normed[:, :, :]).then_inc(stored, 16)
                sp.wait_ge(xbias_ready, it)
                sp.dma_start(x_res[:, :, :], tokens(x1, it)).then_inc(xres_landed, 16)

            values(0, first=True)
            ahead(0, 2)
            with sp.Fori(1, PER_BATCH) as it:
                ahead(it, 2)
                forward(it)
            with sp.Fori(1, B - 1) as b:
                ahead(b * PER_BATCH, 2)
                values(b)
                forward(b * PER_BATCH)
                with sp.Fori(1, PER_BATCH) as n:
                    ahead(b * PER_BATCH + n, 2)
                    forward(b * PER_BATCH + n)
            for it in range(ITER - PER_BATCH, ITER):
                ahead(it, 2 if it + 2 < ITER else 0)
                if it == ITER - PER_BATCH:
                    values(B - 1)
                forward(it)
            sp.wait_ge(normed_ready, ITER * 2)
            sp.dma_start(tokens(x2, ITER - 1), normed[:, :, :]).then_inc(stored, 16)
            sp.wait_ge(stored, ITER * 16 + 16)

        @block.tensor
        def _(pe):
            now = 0

            def turn_x(it, first=False):
                pe.wait_ge(x_landed, it * 16 + 16)
                if not first:
                    pe.wait_ge(qT_ready, it * 4)
                for t in range(2):
                    for c in range(DC):
                        last = pe.transpose(Q_BANK[:, c * TOK + t * P:c * TOK + (t + 1) * P],
                                            x_in[:, t, c * P:(c + 1) * P], ident[:, :])
                last.then_inc(x_turned, 1)

            def project_q(p, it):
                f, j = p // 2, p % 2
                if p == 0:
                    pe.wait_ge(xT_hi_ready, it + 1)
                    pe.wait_ge(xT_lo_ready, it + 1)
                elif j == 0:
                    pe.wait_ge(qT_ready, it * 4 + f)
                last = split_matmuls(pe, Q_BANK[:, j * TOK:(j + 1) * TOK],
                                     [w_cols(0, c, INNER, p * P, (p + 1) * P) for c in range(DC)],
                                     [(xT_hi[:, c, :], xT_lo[:, c, :]) for c in range(DC)])
                if j == 1:
                    last.then_inc(q_done, 1)

            def scores(u, it, b, first):
                t, f = u // 4, u % 4
                if not first or u >= 2:
                    pe.wait_ge(exp_done, it * QUADS + u - 1)
                for j in range(2):
                    p = 2 * f + j
                    last = pe.matmul(S_BANK[u % 2][:, j * NW:(j + 1) * NW], qT[:, now, p, t * P:(t + 1) * P],
                                     k_pad[:, bass.ds(b, 1), p, :, :].rearrange("p b h n -> p (b h n)"),
                                     start=True, stop=True)
                last.then_inc(scores_done, 1)

            def turn_probs(u, it):
                pe.wait_ge(prob_ready, it * QUADS + u + 1)
                for j in range(4):
                    last = pe.transpose(PT_BANK[u % 2][0:CTX, j * P:(j + 1) * P], prob[:, u % 4, j, :], ident[:, :])
                last.then_inc(prob_turned, 1)

            def attend(u, it, b, first):
                f = u % 4
                if 0 <= u < 4:
                    pe.wait_ge(v_landed[f], b * 16 + 16)
                pe.wait_ge(probT_ready, it * QUADS + u + 1)
                if not first or u >= 2:
                    pe.wait_ge(att_lo_ready, it * QUADS + u - 1)
                for j in range(2):
                    for h in range(2):
                        c = (2 * (2 * f + j) + h) * DH
                        last = pe.matmul(ATT_BANK[u % 2][h * DH:(h + 1) * DH, j * P:(j + 1) * P],
                                         v_now[:, c:c + DH], probT[:, u % 2, 2 * j + h, :], start=True, stop=True)
                last.then_inc(att_done, 1)

            def project_out(u, it, first):
                f = u % 4
                pe.wait_ge(att_hi_ready, it * QUADS + u + 1)
                pe.wait_ge(att_lo_ready, it * QUADS + u + 1)
                if f == 0 and not (first and u == 0):
                    pe.wait_ge(y_added, it * 2 + u // 4)
                n = 0
                for j in range(2):
                    left = [part[:, u % 4, j, :] for part in (attT_hi, attT_lo)]
                    right = w_cols(1, 2 * f + j, D, 0, D)
                    for a, c in ((0, 0), (0, 1), (1, 0)):
                        last = pe.matmul(Y_BANK[:, 0:D], left[a], right[c], start=f == 0 and n == 0,
                                         stop=f == 3 and n == 5, skip_group_check=True)
                        n += 1
                if f == 3:
                    last.then_inc(y_done, 1)

            def step(u, parity, it, b, first, new=True):
                nonlocal now
                now = parity
                if new:
                    scores(u, it, b, first)
                    if u < 6:
                        project_q(u, it + 1)
                    if u == 6:
                        project_q(6, it + 1)
                        project_q(7, it + 1)
                if new and u >= TURN or u < TURN and not first:
                    turn_probs(u - TURN, it)
                if new and u >= ATTEND or u < ATTEND and not first:
                    attend(u - ATTEND, it, b, first)
                if new and u >= PROJECT or u < PROJECT and not first:
                    project_out(u - PROJECT, it, first)
                if new and u == 7:
                    turn_x(it + 2)

            pe.wait_ge(c_ident, 1)
            pe.wait_ge(ctx_landed, 16)
            for c in range(2):
                for b in range(B):
                    last = pe.transpose(bank[c][0:CK, b * CTX:(b + 1) * CTX], ctx_in[:, b, c * CK:(c + 1) * CK],
                                        ident[0:CTX, 0:CTX])
            last.then_inc(ctx_turned, 1)
            pe.wait_ge(ctxT_ready, 1)
            pe.wait_ge(wkv_landed, 16)
            for p in range(PAIRS):
                if p >= 6:
                    pe.wait_ge(ctx_k_ready, p - 5)
                for c in range(2):
                    last = pe.matmul(bank[2 + p % 6][:, 0:B * CTX], w_kv[:, c, p * P:(p + 1) * P],
                                     ctxT[:, c, :, :].rearrange("p b n -> p (b n)"), start=c == 0, stop=c == 1)
                last.then_inc(ctx_k_done, 1)
            for n in range(2 * B):
                b, f = n // 2, n % 2
                if n >= 2:
                    pe.wait_ge(ctx_v_ready, n - 1)
                for c in range(2):
                    last = pe.matmul(bank[n % 2][0:CTX, :], ctxT[:, c, b, :],
                                     w_kv[:, c, INNER + f * HALF:INNER + (f + 1) * HALF], start=c == 0, stop=c == 1)
                last.then_inc(ctx_v_done, 1)
            pe.wait_ge(ctx_k_ready, PAIRS)
            pe.wait_ge(ctx_v_ready, 2 * B)
            pe.wait_ge(low_done, 2)
            turn_x(0, first=True)
            for p in range(PAIRS):
                project_q(p, 0)
            turn_x(1)
            pe.wait_ge(qT_ready, 4)

            def pair(b, n, start):
                for parity in range(2):
                    for u in range(QUADS):
                        step(u, parity, 2 * n + parity, b, start and parity == 0)

            all_pairs(pe, pair)
            for u in range(PROJECT):
                step(u, 0, ITER, B, False, new=False)

        @block.scalar
        def _(act):
            for n in range(2):
                act.wait_ge(landed[n], 16)
                act.copy(W[n][0][:, :], stage[n][:, :]).then_inc(high_done, 1)
            act.wait_ge(zeroed, 3)
            for n in range(2 * B):
                b, f = n // 2, n % 2
                act.wait_ge(ctx_v_done, n + 1)
                act.copy(v_all[0:CTX, b, f * HALF:(f + 1) * HALF], bank[n % 2][0:CTX, :]).then_inc(ctx_v_ready, 1)

            def exp_scores(u, it):
                act.wait_ge(max_ready, it * QUADS + u + 1)
                for j in range(4):
                    last = act.activation(prob[:, u % 4, j, :], S_BANK[u % 2][:, j * CTX:(j + 1) * CTX], ACT.Exp,
                                          bias=neg_max[:, u, j:j + 1], accum_out=row_sum[:, u, j:j + 1])
                last.then_inc(exp_done, 1)

            def take_att(u, it):
                act.wait_ge(att_done, it * QUADS + u + 1)
                act.copy(attT_hi[:, u % 4, :, :], ATT_BANK[u % 2][:, 0:2 * P].rearrange("p (a b) -> p a b", a=2)
                         ).then_inc(att_hi_ready, 1)

            def high_x(it):
                act.wait_ge(x_turned, it + 1)
                act.copy(xT_hi[:, :, :].rearrange("p a b -> p (a b)"), Q_BANK[:, :]).then_inc(xT_hi_ready, 1)

            high_x(0)
            high_x(1)

            def pair(b, n, start):
                for parity in range(2):
                    it = 2 * n + parity
                    for u in range(QUADS):
                        exp_scores(u, it)
                        if u >= ATTEND or not (start and parity == 0):
                            take_att(u - ATTEND, it)
                    high_x(it + 2)

            all_pairs(act, pair)
            for u in range(ATTEND):
                take_att(u - ATTEND, ITER)

        @block.gpsimd
        def _(pool):
            pool.memset(ident[:, :], 0.0).then_inc(c_zero, 1)
            pool.memset(neg_half[:, :], -0.5).then_inc(c_zero, 1)
            pool.wait_ge(c_zero, 2)
            pool.affine_select(out=ident[:, :], in_=ident[:, :], compare_op=ALU.not_equal, fill=1.0, base=0,
                               pattern=[[-1, P]], channel_multiplier=1).then_inc(c_ident, 1)
            pool.wait_ge(bias_landed, 16)

            def normalise(u, it):
                pool.wait_ge(inv_ready, it * QUADS + u + 1)
                pool.tensor_tensor(prob[:, u % 4, :, :], prob[:, u % 4, :, :],
                                   row_inv[:, u, :].unsqueeze(2).to_broadcast([P, 4, CTX]), ALU.mult
                                   ).then_inc(prob_ready, 1)

            def add_bias(it, first=False):
                pool.wait_ge(xres_landed, it * 16 + 16)
                if not first:
                    pool.wait_ge(y_added, it * 2)
                pool.tensor_tensor(x_bias[:, :, :], x_res[:, :, :],
                                   bias_rows[:, :].unsqueeze(1).to_broadcast([P, 2, D]), ALU.add
                                   ).then_inc(xbias_ready, 1)

            def root(t, it):
                pool.wait_ge(var_ready, it * 2 + t + 1)
                pool.tensor_tensor(rstd[:, t:t + 1], var_eps[:, t:t + 1], neg_half[:, :], ALU.pow
                                   ).then_inc(rstd_ready, 1)

            def pair(b, n, start):
                for parity in range(2):
                    it = 2 * n + parity
                    first = start and parity == 0
                    for u in range(QUADS):
                        normalise(u, it)
                        if u == 1 and not first:
                            root(0, it - 1)
                        if u == 5 and not first:
                            root(1, it - 1)
                    add_bias(it, first)

            all_pairs(pool, pair)
            root(0, ITER - 1)
            root(1, ITER - 1)

        @block.vector
        def _(dve):
            dve.memset(k_pad[:, :, :, :, :].rearrange("p a b c d -> p (a b c d)"), 0.0).then_inc(zeroed, 1)
            dve.memset(v_all[:, :, :].rearrange("p a b -> p (a b)"), 0.0).then_inc(zeroed, 1)
            dve.memset(probT[:, :, :, :].rearrange("p a b c -> p (a b c)"), 0.0).then_inc(zeroed, 1)
            dve.memset(stats[:, :, :].rearrange("p a b -> p (a b)"), 0.0).then_inc(stored, 16)
            dve.wait_ge(zeroed, 3)
            dve.wait_ge(ctx_turned, 1)
            for c in range(2):
                last = dve.tensor_copy(ctxT[:, c, :, :].rearrange("p b n -> p (b n)"), bank[c][0:CK, 0:B * CTX])
            last.then_inc(ctxT_ready, 1)
            for p in range(PAIRS):
                dve.wait_ge(ctx_k_done, p + 1)
                for h in range(2):
                    rows = slice(h * DH, (h + 1) * DH)
                    last = dve.tensor_copy(k_pad[rows, :, p, h, :],
                                           bank[2 + p % 6][rows, 0:B * CTX].rearrange("p (b n) -> p b n", b=B))
                last.then_inc(ctx_k_ready, 1)
            for n in range(2):
                dve.wait_ge(high_done, n + 1)
                dve.tensor_tensor(W[n][1][:, :], stage[n][:, :], W[n][0][:, :].bitcast(F32), ALU.subtract
                                  ).then_inc(low_done, 1)

            def maxima(u, it):
                dve.wait_ge(scores_done, it * QUADS + u + 1)
                dve.tensor_reduce(neg_max[:, u, :], S_BANK[u % 2][:, 0:4 * CTX].rearrange("p (a b) -> p a b", a=4),
                                  AX_X, ALU.max, negate=True).then_inc(max_ready, 1)

            def inverse(u, it):
                dve.wait_ge(exp_done, it * QUADS + u + 1)
                dve.reciprocal(row_inv[:, u, :], row_sum[:, u, :]).then_inc(inv_ready, 1)

            def low_att(u, it):
                dve.wait_ge(att_hi_ready, it * QUADS + u + 1)
                dve.tensor_tensor(attT_lo[:, u % 4, :, :],
                                  ATT_BANK[u % 2][:, 0:2 * P].rearrange("p (a b) -> p a b", a=2),
                                  attT_hi[:, u % 4, :, :].bitcast(F32), ALU.subtract
                                  ).then_inc(att_lo_ready, 1)

            def residual(t, it):
                if t == 0:
                    dve.wait_ge(xbias_ready, it + 1)
                dve.wait_ge(y_done, it * 2 + t + 1)
                dve.tensor_tensor(y[:, t, :], Y_BANK[:, 0:D], x_bias[:, t, :], ALU.add).then_inc(y_added, 1)
                dve.wait_ge(y_added, it * 2 + t + 1)
                dve.bn_stats(stats[:, t, :], y[:, t, :]).then_inc(ln_step, 1)
                dve.wait_ge(ln_step, it * 4 + 2 * t + 1)
                dve.memset(spare[:, t:t + 1], 0.0)
                dve.bn_aggr(mean_var[:, t, :], stats[:, t, :]).then_inc(ln_step, 1)
                dve.wait_ge(ln_step, it * 4 + 2 * t + 2)
                dve.tensor_scalar(var_eps[:, t:t + 1], mean_var[:, t, 1:2], LN_EPS, None, ALU.add
                                  ).then_inc(var_ready, 1)

            def normalise(t, it):
                dve.wait_ge(rstd_ready, it * 2 + t + 1)
                dve.wait_ge(stored, it * 16 + 16)
                dve.tensor_scalar(normed[:, t, :], y[:, t, :], mean_var[:, t, 0:1], rstd[:, t:t + 1],
                                  ALU.subtract, ALU.mult).then_inc(normed_ready, 1)

            def low_x(it):
                dve.wait_ge(xT_hi_ready, it + 1)
                dve.tensor_tensor(xT_lo[:, :, :].rearrange("p a b -> p (a b)"), Q_BANK[:, :],
                                  xT_hi[:, :, :].rearrange("p a b -> p (a b)").bitcast(F32), ALU.subtract
                                  ).then_inc(xT_lo_ready, 1)

            def take_q(f, it, parity):
                dve.wait_ge(q_done, it * 4 + f + 1)
                dve.tensor_scalar(qT[:, parity, 2 * f:2 * f + 2, :].rearrange("p a b -> p (a b)"), Q_BANK[:, :],
                                  DH ** -0.5, None, ALU.mult).then_inc(qT_ready, 1)

            def take_probT(u, it):
                dve.wait_ge(prob_turned, it * QUADS + u + 1)
                dve.tensor_copy(probT[0:CTX, u % 2, :, :].rearrange("p a b -> p (a b)"), PT_BANK[u % 2][0:CTX, :]
                                ).then_inc(probT_ready, 1)

            low_x(0)
            for f in range(4):
                take_q(f, 0, 0)
            low_x(1)

            def step(u, parity, it, first, new=True):
                if new:
                    maxima(u, it)
                if u in (1, 5) and not first:
                    residual(u // 4, it - 1)
                if new and u >= TURN or u < TURN and not first:
                    take_probT(u - TURN, it)
                if new and u in (1, 3, 5, 6):
                    take_q((1, 3, 5, 6).index(u), it + 1, 1 - parity)
                if new:
                    inverse(u, it)
                if u in (1, 5) and not first:
                    normalise(u // 4, it - 1)
                if new and u >= ATTEND or u < ATTEND and not first:
                    low_att(u - ATTEND, it)
                if new and u == 7:
                    low_x(it + 2)

            def pair(b, n, start):
                for parity in range(2):
                    for u in range(QUADS):
                        step(u, parity, 2 * n + parity, start and parity == 0)

            all_pairs(dve, pair)
            for u in range(PROJECT + 1):
                step(u, 0, ITER, False, new=False)


HD = D // H
GROUPS = H // 4
Q_PART = (0, 1, 0, 1, 2, 0, 2, 1)
K_PART = (0, 0, 1, 1, 0, 2, 1, 2)
NSTACK = 16 * 16


def load_stacks(sp, parts, b, group, slot, stacks, landed):
    for n, (stack, order) in enumerate(zip(stacks, (Q_PART, K_PART))):
        for blk, part in enumerate(order):
            src = parts[bass.ds(b, 1), n, part, group * 4 * HD:(group + 1) * 4 * HD, :].rearrange(
                "b (h i) s -> i (b h) s", i=HD)
            sp.dma_start(stack[blk * HD:(blk + 1) * HD, slot, :, :], src).then_inc(landed[slot], 16)


def emit_query_softmax(nc, x2, wq, wk, wv, wo, wff, parts, out):
    B, S = out.shape[0], out.shape[1]
    with ExitStack() as ctx:
        def sb(name, shape, dt=F32):
            return ctx.enter_context(nc.sbuf_tensor("f_" + name, shape, dt))

        v_all = sb("v_all", [P, B, S // P, D])
        stacks = [sb(f"stack{n}", [P, 2, 4, S], BF16) for n in range(2)]
        stack_landed = [ctx.enter_context(nc.semaphore(f"f_stack{n}_landed")) for n in range(2)]
        emit_thirds(nc, x2, wq, wk, wv, parts, v_all, stacks, stack_landed, B, S)
        zT_all = sb("zT_all", [P, B, GROUPS, S])
        w_out = sb("w_out", [P, GROUPS, D])
        w_ff = sb("w_ff", [P, DC, D])
        emit_key_softmax(nc, parts, v_all, stacks, stack_landed, zT_all, wo, wff, w_out, w_ff, B, S)
        emit_gelu_output(nc, x2, zT_all, w_out, w_ff, out, B, S)


def emit_thirds(nc, x2, wq, wk, wv, parts, v_all, stacks, stack_landed, B, S):
    KT = S // P
    with ExitStack() as ctx:
        def sb(name, shape, dt=F32):
            return ctx.enter_context(nc.sbuf_tensor("p_" + name, shape, dt))

        def sem(name):
            return ctx.enter_context(nc.semaphore("p_" + name))

        wide = [ctx.enter_context(nc.psum_tensor(f"p_wide{i}", [P, S], F32)) for i in range(4)]
        X_WIDE, QK_WIDE, V_WIDE = wide[0:2], (wide[2], wide[3], wide[0], wide[1]), wide[2:4]
        ident = sb("ident", [P, P])
        W = [sb(f"w{n}_in", [P, DC, D]) for n in range(3)]
        W_hi = [sb(f"w{n}_hi", [P, DC, D], F32R) for n in range(3)]
        W_lo = [sb(f"w{n}_lo", [P, DC, D], F32R) for n in range(3)]
        x_in = sb("x_in", [P, KT, D])
        xT_hi = sb("xT_hi", [P, 2, DC, S], F32R)
        xT_lo = sb("xT_lo", [P, 2, DC, S], F32R)
        third = sb("third", [P, 4, 3, S], BF16)
        rest = sb("rest", [P, 2, S])

        c_zero, c_ident = sem("zero"), sem("ident_done")
        w_landed = [sem(f"w{n}_landed") for n in range(3)]
        high_done, low_done = sem("w_high"), sem("w_low")
        x_landed, x_turned, xT_hi_ready, xT_lo_ready = (sem("x_landed"), sem("x_turned"), sem("xT_hi_ready"),
                                                        sem("xT_lo_ready"))
        qk_done, first_ready, rest_ready, second_ready, third_ready = (
            sem("qk_done"), sem("first_ready"), sem("rest_ready"), sem("second_ready"), sem("third_ready"))
        v_done, v_ready = sem("v_done"), sem("v_ready")
        parts_stored = [sem(f"parts{m}_stored") for m in range(4)]

        block = ctx.enter_context(nc.Block())

        @block.sync
        def _(sp):
            def load_x(b):
                sp.dma_start(x_in[:, :, :], x2[bass.ds(b * S, S), :].rearrange("(t p) d -> p t d", p=P)
                             ).then_inc(x_landed, 16)

            def batch(b, last=False):
                if not last:
                    sp.wait_ge(x_turned, b + 1)
                    load_x(b + 1)
                for m in range(4):
                    sp.wait_ge(third_ready, b * 4 + m + 1)
                    sp.dma_start(parts[bass.ds(b, 1), m // 2, :, (m % 2) * P:(m % 2 + 1) * P, :].rearrange(
                        "b a p s -> p (b a) s"), third[:, m, :, :]).then_inc(parts_stored[m], 16)

            load_x(0)
            for n, w in enumerate((wq, wk, wv)):
                sp.dma_start(W[n][:, :, :], w.rearrange("(c p) n -> p c n", p=P)).then_inc(w_landed[n], 16)
            batch(0)
            batch(1)
            for m in range(4):
                sp.wait_ge(parts_stored[m], 16)
            for group in range(2):
                load_stacks(sp, parts, 0, group, group, stacks, stack_landed)
            with sp.Fori(2, B - 1) as b:
                batch(b)
            batch(B - 1, last=True)
            for m in range(4):
                sp.wait_ge(parts_stored[m], 16 * B)

        @block.tensor
        def _(pe):
            pe.wait_ge(c_ident, 1)

            def turn_x(b, first=False):
                pe.wait_ge(x_landed, b * 16 + 16)
                if not first:
                    pe.wait_ge(rest_ready, b * 4)
                for c in range(DC):
                    for t in range(KT):
                        last = pe.transpose(X_WIDE[c][:, t * P:(t + 1) * P], x_in[:, t, c * P:(c + 1) * P],
                                            ident[:, :])
                last.then_inc(x_turned, 1)

            def project(m, b, parity, first):
                n, s = m // 2, slice((m % 2) * P, (m % 2 + 1) * P)
                if m < 2 and not first:
                    pe.wait_ge(v_ready, b * 2 - 1 + m)
                for f in range(2):
                    last = split_matmuls(pe, QK_WIDE[m][:, f * HALF:(f + 1) * HALF],
                                         [(W_hi[n][:, c, s], W_lo[n][:, c, s]) for c in range(DC)],
                                         [tuple(a[:, parity, c, f * HALF:(f + 1) * HALF] for a in (xT_hi, xT_lo))
                                          for c in range(DC)])
                last.then_inc(qk_done, 1)

            def project_v(f, b, parity):
                pe.wait_ge(rest_ready, b * 4 + f + 1)
                for t in range(4 * f, 4 * f + 4):
                    s = slice(t * P, (t + 1) * P)
                    last = split_matmuls(pe, V_WIDE[f][:, (t % 4) * D:(t % 4 + 1) * D],
                                         [tuple(a[:, parity, c, s] for a in (xT_hi, xT_lo)) for c in range(DC)],
                                         [(W_hi[2][:, c, :], W_lo[2][:, c, :]) for c in range(DC)])
                last.then_inc(v_done, 1)

            def batch(b, parity, first=False, last=False):
                pe.wait_ge(xT_hi_ready, b * 2 + 2)
                pe.wait_ge(xT_lo_ready, b * 2 + 2)
                for m in range(4):
                    project(m, b, parity, first)
                project_v(0, b, parity)
                if not last:
                    turn_x(b + 1)
                project_v(1, b, parity)

            turn_x(0, first=True)
            pe.wait_ge(low_done, 3)
            batch(0, 0, first=True)
            with pe.Fori(0, B // 2 - 1) as n:
                batch(2 * n + 1, 1)
                batch(2 * n + 2, 0)
            batch(B - 1, 1, last=True)

        @block.scalar
        def _(act):
            def high_x(b, parity):
                act.wait_ge(x_turned, b + 1)
                for c in range(DC):
                    act.copy(xT_hi[:, parity, c, :], X_WIDE[c][:, :]).then_inc(xT_hi_ready, 1)

            def batch(b, parity, first=False, last=False):
                for m in range(4):
                    scale = D ** -0.5 if m < 2 else 1.0
                    act.wait_ge(qk_done, b * 4 + m + 1)
                    if not first:
                        act.wait_ge(parts_stored[m], b * 16)
                    act.mul(third[:, m, 0, :], QK_WIDE[m][:, :], scale).then_inc(first_ready, 1)
                    act.wait_ge(rest_ready, b * 4 + m + 1)
                    act.copy(third[:, m, 1, :], rest[:, m % 2, :]).then_inc(second_ready, 1)
                for f in range(2):
                    act.wait_ge(v_done, b * 2 + f + 1)
                    act.copy(v_all[:, bass.ds(b, 1), 4 * f:4 * f + 4, :].rearrange("p b t d -> p (b t d)"),
                             V_WIDE[f][:, :]).then_inc(v_ready, 1)
                    if f == 0 and not last:
                        high_x(b + 1, 1 - parity)

            high_x(0, 0)
            for n in range(3):
                act.wait_ge(w_landed[n], 16)
                act.copy(W_hi[n][:, :, :].rearrange("p a b -> p (a b)"), W[n][:, :, :].rearrange("p a b -> p (a b)")
                         ).then_inc(high_done, 1)
            batch(0, 0, first=True)
            with act.Fori(0, B // 2 - 1) as n:
                batch(2 * n + 1, 1)
                batch(2 * n + 2, 0)
            batch(B - 1, 1, last=True)

        @block.gpsimd
        def _(pool):
            pool.memset(ident[:, :], 0.0).then_inc(c_zero, 1)
            pool.wait_ge(c_zero, 1)
            pool.affine_select(out=ident[:, :], in_=ident[:, :], compare_op=ALU.not_equal, fill=1.0, base=0,
                               pattern=[[-1, P]], channel_multiplier=1).then_inc(c_ident, 1)

        @block.vector
        def _(dve):
            def low_x(b, parity):
                for c in range(DC):
                    dve.wait_ge(xT_hi_ready, b * 2 + c + 1)
                    dve.tensor_tensor(xT_lo[:, parity, c, :], X_WIDE[c][:, :],
                                      xT_hi[:, parity, c, :].bitcast(F32), ALU.subtract).then_inc(xT_lo_ready, 1)

            def batch(b, parity, last=False):
                for m in range(4):
                    scale = D ** -0.5 if m < 2 else 1.0
                    dve.wait_ge(first_ready, b * 4 + m + 1)
                    dve.scalar_tensor_tensor(out=rest[:, m % 2, :], in0=QK_WIDE[m][:, :], scalar=scale,
                                             in1=third[:, m, 0, :], op0=ALU.mult, op1=ALU.subtract
                                             ).then_inc(rest_ready, 1)
                    dve.wait_ge(second_ready, b * 4 + m + 1)
                    dve.tensor_tensor(third[:, m, 2, :], rest[:, m % 2, :], third[:, m, 1, :], ALU.subtract
                                      ).then_inc(third_ready, 1)
                if not last:
                    low_x(b + 1, 1 - parity)

            low_x(0, 0)
            for n in range(3):
                dve.wait_ge(high_done, n + 1)
                dve.tensor_tensor(W_lo[n][:, :, :].rearrange("p a b -> p (a b)"),
                                  W[n][:, :, :].rearrange("p a b -> p (a b)"),
                                  W_hi[n][:, :, :].rearrange("p a b -> p (a b)").bitcast(F32), ALU.subtract
                                  ).then_inc(low_done, 1)
            with dve.Fori(0, B // 2 - 1) as n:
                for parity in range(2):
                    batch(2 * n + parity, parity)
            batch(B - 2, 0)
            batch(B - 1, 1, last=True)


def emit_key_softmax(nc, parts, v_all, stacks, stack_landed, zT_all, wo, wff, w_out, w_ff, B, S):
    KT = S // P
    STEPS = GROUPS * KT
    TURNS = 4 * STEPS
    PIECE = S // 4
    q_stack, k_stack = stacks
    with ExitStack() as ctx:
        def sb(name, shape, dt=F32):
            return ctx.enter_context(nc.sbuf_tensor("s_" + name, shape, dt))

        def sem(name):
            return ctx.enter_context(nc.semaphore("s_" + name))

        ring = [ctx.enter_context(nc.psum_tensor(f"s_ring{i}", [P, S], F32)) for i in range(3)]
        acc = ctx.enter_context(nc.psum_tensor("s_acc", [P, S], F32))
        neg_max = sb("neg_max", [P, 2, 4])
        row_sum = sb("row_sum", [P, 2, 4])
        row_inv = sb("row_inv", [P, 2, 4])
        prob = sb("prob", [P, 4, 4, S])
        v_norm = sb("v_norm", [P, 4, 4, 32])

        zeroed, v_zeroed, w_landed = sem("zeroed"), sem("v_zeroed"), sem("w_landed")
        scores_done, max_ready, exp_done, inv_ready, vnorm_ready, pv_done, zT_ready = (
            sem("scores_done"), sem("max_ready"), sem("exp_done"), sem("inv_ready"), sem("vnorm_ready"),
            sem("pv_done"), sem("zT_ready"))

        block = ctx.enter_context(nc.Block())

        @block.sync
        def _(sp):
            sp.dma_start(w_ff[:, :, :], wff.rearrange("(c p) n -> p c n", p=P)).then_inc(w_landed, 16)
            sp.wait_ge(zeroed, 1)
            for j in range(4):
                sp.dma_start(w_out[32 * j:32 * j + HD, :, :],
                             wo.rearrange("(g h i) n -> h i g n", g=GROUPS, h=4)[j]).then_inc(w_landed, 16)

            def batch(b, first=0):
                for group in range(first, GROUPS):
                    sp.wait_ge(scores_done, b * TURNS + (group - 1) * (TURNS // GROUPS))
                    load_stacks(sp, parts, b, group, group % 2, stacks, stack_landed)

            batch(0, first=2)
            with sp.Fori(1, B) as b:
                batch(b)
            sp.wait_ge(w_landed, 16 * 5)

        @block.tensor
        def _(pe):
            def scores(b, step, j, first):
                n = step * 4 + j
                slot, kt = (step // KT) % 2, step % KT
                if n >= 3:
                    pe.wait_ge(exp_done, b * TURNS + n - 2)
                elif not first:
                    pe.wait_ge(exp_done, b * TURNS + (TURNS - 1 - (TURNS - 1 - n) % 3) - TURNS + 1)
                for f in range(2):
                    last = pe.matmul(ring[n % 3][:, f * HALF:(f + 1) * HALF],
                                     k_stack[:, slot, j, kt * P:(kt + 1) * P],
                                     q_stack[:, slot, j, f * HALF:(f + 1) * HALF], start=True, stop=True)
                last.then_inc(scores_done, 1)

            def values(b, step, piece, first):
                kt, s = step % KT, slice(piece * PIECE, (piece + 1) * PIECE)
                if piece == 0:
                    pe.wait_ge(vnorm_ready, b * STEPS + step + 1)
                    if kt == 0 and not (first and step == 0):
                        pe.wait_ge(zT_ready, b * GROUPS + step // KT)
                for j in range(4):
                    last = pe.matmul(acc[32 * j:32 * j + 32, s], v_norm[:, step % 4, j, :], prob[:, step % 4, j, s],
                                     start=kt == 0 and piece % 2 == 0, stop=kt == KT - 1, skip_group_check=True)
                if piece == 3:
                    last.then_inc(pv_done, 1)

            def batch(b, first=False):
                for step in range(STEPS):
                    if step % KT == 0:
                        pe.wait_ge(stack_landed[(step // KT) % 2], b * (2 * NSTACK) + (step // KT // 2 + 1) * NSTACK)
                    for j in range(4):
                        scores(b, step, j, first)
                        if step >= 2 or not first:
                            values(b, step - 2, j, first)

            batch(0, first=True)
            with pe.Fori(1, B) as b:
                batch(b)
            for step in range(2):
                for j in range(4):
                    values(B, step - 2, j, False)

        @block.scalar
        def _(act):
            def take_outputs(b, group):
                act.wait_ge(pv_done, b * STEPS + (group + 1) * KT)
                batch_at, group = (b, group) if group >= 0 else (b - 1, group + GROUPS)
                act.copy(zT_all[:, bass.ds(batch_at, 1), group, :].rearrange("p b s -> p (b s)"), acc[:, :]
                         ).then_inc(zT_ready, 1)

            def batch(b, first=False):
                for step in range(STEPS):
                    for j in range(4):
                        n = step * 4 + j
                        act.wait_ge(max_ready, b * TURNS + n + 1)
                        act.activation(prob[:, step % 4, j, :], ring[n % 3][:, :], ACT.Exp,
                                       bias=neg_max[:, step % 2, j:j + 1],
                                       accum_out=row_sum[:, step % 2, j:j + 1]).then_inc(exp_done, 1)
                        if step % KT == 1 and j == 2 and not (first and step == 1):
                            take_outputs(b, step // KT - 1)

            batch(0, first=True)
            with act.Fori(1, B) as b:
                batch(b)
            take_outputs(B, -1)

        @block.gpsimd
        def _(pool):
            pool.memset(v_norm[:, :, :, :], 0.0).then_inc(v_zeroed, 1)
            pool.wait_ge(v_zeroed, 1)
            with pool.Fori(0, B) as b:
                for step in range(STEPS):
                    group, kt = step // KT, step % KT
                    pool.wait_ge(inv_ready, b * STEPS + step + 1)
                    pool.tensor_tensor(v_norm[:, step % 4, :, 0:HD],
                                       v_all[:, bass.ds(b, 1), kt, group * 4 * HD:(group + 1) * 4 * HD].rearrange(
                                           "p b (h d) -> p (b h) d", d=HD),
                                       row_inv[:, step % 2, :].unsqueeze(2).to_broadcast([P, 4, HD]), ALU.mult
                                       ).then_inc(vnorm_ready, 1)

        @block.vector
        def _(dve):
            dve.memset(w_out[:, :, :].rearrange("p a b -> p (a b)"), 0.0).then_inc(zeroed, 1)

            def inverse(b, step):
                dve.wait_ge(exp_done, b * TURNS + step * 4 + 4)
                dve.reciprocal(row_inv[:, step % 2, :], row_sum[:, step % 2, :]).then_inc(inv_ready, 1)

            def batch(b, first=False):
                for step in range(STEPS):
                    for j in range(4):
                        n = step * 4 + j
                        dve.wait_ge(scores_done, b * TURNS + n + 1)
                        dve.tensor_reduce(neg_max[:, step % 2, j:j + 1], ring[n % 3][:, :], AX_X, ALU.max,
                                          negate=True).then_inc(max_ready, 1)
                        if j == 0 and not (first and step == 0):
                            inverse(b, step - 1)

            batch(0, first=True)
            with dve.Fori(1, B) as b:
                batch(b)
            inverse(B, -1)


def emit_gelu_output(nc, x2, zT_all, w_out, w_ff, out, B, S):
    GT = HALF // P
    outf = out.rearrange("b s d -> (b s) d")
    with ExitStack() as ctx:
        def sb(name, shape, dt=F32):
            return ctx.enter_context(nc.sbuf_tensor("g_" + name, shape, dt))

        def sem(name):
            return ctx.enter_context(nc.semaphore("g_" + name))

        z1_bank = [ctx.enter_context(nc.psum_tensor(f"g_z1_{c}", [P, HALF], F32)) for c in range(DC)]
        z2_bank = ctx.enter_context(nc.psum_tensor("g_z2", [P, GT * D], F32))
        norm_bank = ctx.enter_context(nc.psum_tensor("g_norm", [P, HALF], F32))
        ones = sb("ones", [P, 1])
        neg_half = sb("neg_half", [P, GT])
        z1T = sb("z1T", [P, 2, DC, HALF])
        square = sb("square", [P, 2, DC, HALF])
        clamped = sb("clamped", [P, 2, GT])
        norm_inv = sb("norm_inv", [P, 2, GT])
        both_inv = sb("both_inv", [P, GT])
        square_sum = sb("square_sum", [P, GT])
        z = sb("z", [P, GT * D])
        x_fin = sb("x_fin", [P, 2, GT * D])
        y = sb("y", [P, GT * D])
        o_fin = sb("o_fin", [P, 2, GT * D])
        stats = sb("stats", [P, GT, 6])
        mean_var = sb("mean_var", [P, GT, 2])
        var_eps = sb("var_eps", [P, GT])
        rstd = sb("rstd", [P, GT])
        spare = sb("spare", [P, 1])

        c_set = sem("set")
        z1_done, z1_taken, norm_done, clamp1_done, inv1_ready = (
            sem("z1_done"), sem("z1_taken"), sem("norm_done"), sem("clamp1_done"), sem("inv1_ready"))
        z2_done, square_done, clamp2_done, inv2_ready, both_ready, z_ready = (
            sem("z2_done"), sem("square_done"), sem("clamp2_done"), sem("inv2_ready"), sem("both_ready"),
            sem("z_ready"))
        gelu_done, y_ready, ln_step, var_ready, rstd_ready, o_ready = (
            sem("gelu_done"), sem("y_ready"), sem("ln_step"), sem("var_ready"), sem("rstd_ready"), sem("o_ready"))
        x_landed, stored = [sem("x0_landed"), sem("x1_landed")], [sem("stored0"), sem("stored1")]

        block = ctx.enter_context(nc.Block())


        @block.sync
        def _(sp):
            def tokens(array, group):
                return array[bass.ds(group * HALF, HALF), :].rearrange("(t p) d -> p t d", p=P)

            def load(group, parity):
                sp.dma_start(x_fin[:, parity, :].rearrange("p (t d) -> p t d", d=D), tokens(x2, group)
                             ).then_inc(x_landed[parity], 16)

            load(0, 0)
            load(1, 1)
            with sp.Fori(0, B - 1) as b:
                for parity in range(2):
                    sp.wait_ge(y_ready, 2 * b + parity + 1)
                    load(2 * b + parity + 2, parity)
                    sp.wait_ge(o_ready, 2 * b + parity + 1)
                    sp.dma_start(tokens(outf, 2 * b + parity),
                                 o_fin[:, parity, :].rearrange("p (t d) -> p t d", d=D)).then_inc(stored[parity], 16)
            for parity in range(2):
                sp.wait_ge(o_ready, 2 * B - 1 + parity)
                sp.dma_start(tokens(outf, 2 * B - 2 + parity),
                             o_fin[:, parity, :].rearrange("p (t d) -> p t d", d=D)).then_inc(stored[parity], 16)
            for parity in range(2):
                sp.wait_ge(stored[parity], 16 * B)

        @block.tensor
        def _(pe):
            pe.wait_ge(c_set, 1)

            def first_projection(b, half, first):
                if not (first and half == 0):
                    pe.wait_ge(z1_taken, 2 * b + half)
                for c in range(DC):
                    for g in range(GROUPS):
                        last = pe.matmul(z1_bank[c][:, :], w_out[:, g, c * P:(c + 1) * P],
                                         zT_all[:, bass.ds(b, 1), g, half * HALF:(half + 1) * HALF].rearrange(
                                             "p b s -> p (b s)"), start=g == 0, stop=g == GROUPS - 1)
                last.then_inc(z1_done, 1)

            def second_projection(group, parity, first):
                pe.wait_ge(z1_taken, group + 1)
                if not first:
                    pe.wait_ge(clamp1_done, group)
                for t in range(GT):
                    for c in range(DC):
                        last = pe.matmul(norm_bank[:, t:t + 1], square[:, parity, c, t * P:(t + 1) * P], ones[:, :],
                                         start=c == 0, stop=c == DC - 1)
                last.then_inc(norm_done, 1)
                if not first:
                    pe.wait_ge(z_ready, group)
                for t in range(GT):
                    for c in range(DC):
                        last = pe.matmul(z2_bank[:, t * D:(t + 1) * D], z1T[:, parity, c, t * P:(t + 1) * P],
                                         w_ff[:, c, :], start=c == 0, stop=c == DC - 1)
                last.then_inc(z2_done, 1)

            first_projection(0, 0, True)
            first_projection(0, 1, True)
            second_projection(0, 0, True)
            with pe.Fori(1, B) as b:
                first_projection(b, 0, False)
                second_projection(2 * b - 1, 1, False)
                first_projection(b, 1, False)
                second_projection(2 * b, 0, False)
            second_projection(2 * B - 1, 1, False)

        @block.scalar
        def _(act):
            def take_first(group, parity):
                act.wait_ge(z1_done, group + 1)
                for c in range(DC):
                    act.copy(z1T[:, parity, c, :], z1_bank[c][:, :])
                    last = act.activation(square[:, parity, c, :], z1_bank[c][:, :], ACT.Square)
                last.then_inc(z1_taken, 1)

            def finish(group):
                act.wait_ge(inv1_ready, group + 1)
                act.wait_ge(z2_done, group + 1)
                for t in range(GT):
                    last = act.activation(z[:, t * D:(t + 1) * D], z2_bank[:, t * D:(t + 1) * D], ACT.Square,
                                          scale=norm_inv[:, 0, t:t + 1], accum_out=square_sum[:, t:t + 1])
                last.then_inc(square_done, 1)
                act.wait_ge(z_ready, group + 1)
                act.activation(z[:, :], z[:, :], ACT.Gelu).then_inc(gelu_done, 1)

            take_first(0, 0)
            take_first(1, 1)
            finish(0)
            with act.Fori(1, B) as b:
                take_first(2 * b, 0)
                finish(2 * b - 1)
                take_first(2 * b + 1, 1)
                finish(2 * b)
            finish(2 * B - 1)

        @block.gpsimd
        def _(pool):
            pool.memset(ones[:, :], 1.0).then_inc(c_set, 1)
            pool.memset(neg_half[:, :], -0.5).then_inc(c_set, 1)
            pool.wait_ge(c_set, 2)
            with pool.Fori(0, 2 * B) as group:
                pool.wait_ge(clamp1_done, group + 1)
                pool.tensor_tensor(norm_inv[:, 0, :], clamped[:, 0, :], neg_half[:, :], ALU.pow
                                   ).then_inc(inv1_ready, 1)
                pool.wait_ge(clamp2_done, group + 1)
                pool.tensor_tensor(norm_inv[:, 1, :], clamped[:, 1, :], neg_half[:, :], ALU.pow
                                   ).then_inc(inv2_ready, 1)
                pool.wait_ge(var_ready, group + 1)
                pool.tensor_tensor(rstd[:, :], var_eps[:, :], neg_half[:, :], ALU.pow).then_inc(rstd_ready, 1)

        @block.vector
        def _(dve):
            def finish(b, parity, first):
                group = 2 * b + parity
                dve.wait_ge(norm_done, group + 1)
                dve.tensor_scalar(clamped[:, 0, :], norm_bank[:, 0:GT], 1e-24, None, ALU.max
                                  ).then_inc(clamp1_done, 1)
                dve.wait_ge(square_done, group + 1)
                dve.tensor_scalar(clamped[:, 1, :], square_sum[:, :], 1e-24, None, ALU.max
                                  ).then_inc(clamp2_done, 1)
                dve.wait_ge(inv2_ready, group + 1)
                dve.tensor_tensor(both_inv[:, :], norm_inv[:, 0, :], norm_inv[:, 1, :], ALU.mult
                                  ).then_inc(both_ready, 1)
                dve.wait_ge(both_ready, group + 1)
                dve.tensor_tensor(z[:, :].rearrange("p (t d) -> p t d", d=D),
                                  z2_bank[:, :].rearrange("p (t d) -> p t d", d=D),
                                  both_inv[:, :].unsqueeze(2).to_broadcast([P, GT, D]), ALU.mult
                                  ).then_inc(z_ready, 1)
                dve.wait_ge(x_landed[parity], b * 16 + 16)
                dve.wait_ge(gelu_done, group + 1)
                dve.tensor_tensor(y[:, :], z[:, :], x_fin[:, parity, :], ALU.add).then_inc(y_ready, 1)
                dve.wait_ge(y_ready, group + 1)
                for t in range(GT):
                    last = dve.bn_stats(stats[:, t, :], y[:, t * D:(t + 1) * D])
                last.then_inc(ln_step, 1)
                dve.wait_ge(ln_step, 2 * group + 1)
                dve.memset(spare[:, :], 0.0)
                for t in range(GT):
                    last = dve.bn_aggr(mean_var[:, t, :], stats[:, t, :])
                last.then_inc(ln_step, 1)
                dve.wait_ge(ln_step, 2 * group + 2)
                dve.tensor_scalar(var_eps[:, :], mean_var[:, :, 1], LN_EPS, None, ALU.add).then_inc(var_ready, 1)
                dve.wait_ge(rstd_ready, group + 1)
                if not first:
                    dve.wait_ge(stored[parity], b * 16)
                for t in range(GT):
                    s = slice(t * D, (t + 1) * D)
                    last = dve.tensor_scalar(o_fin[:, parity, s], y[:, s], mean_var[:, t, 0:1],
                                             rstd[:, t:t + 1], ALU.subtract, ALU.mult)
                last.then_inc(o_ready, 1)

            for parity in range(2):
                finish(0, parity, True)
            with dve.Fori(1, B) as b:
                for parity in range(2):
                    finish(b, parity, False)


def build_layer(nc, x, ctx_768, attn_wq, attn_wk, attn_wv, attn_wo, betas, x_wq, x_wkv, x_wo, x_bias,
                f_wq, f_wk, f_wv, f_wo, f_wff, out):
    B, S, _ = x.shape
    x1 = nc.dram_tensor("after_attention", (B * S, D), F32).ap()
    x2 = nc.dram_tensor("after_cross_attention", (B * S, D), F32).ap()
    parts = nc.dram_tensor("qk_thirds", (B, 2, 3, D, S), BF16).ap()
    with nc.cleanup_on_exit():
        emit_segment_attention(nc, x, attn_wq, attn_wk, attn_wv, attn_wo, betas, x1)
    with nc.cleanup_on_exit():
        emit_cross_attention(nc, x1, ctx_768, x_wq, x_wkv, x_wo, x_bias, x2)
    emit_query_softmax(nc, x2, f_wq, f_wk, f_wv, f_wo, f_wff, parts, out)


_INS = ['x', 'ctx_768', 'L0_attn_Wq', 'L0_attn_Wk', 'L0_attn_Wv', 'L0_attn_Wo', 'L0_attn_betas', 'L0_xattn_w_q',
        'L0_xattn_w_kv', 'L0_xattn_w_out', 'L0_xattn_b_out', 'L0_ffn_Wq', 'L0_ffn_Wk', 'L0_ffn_Wv', 'L0_ffn_Wo',
        'L0_ffn_Wff']


def kernel(**inputs):
    import concourse.bacc as _bacc
    from concourse.bass_utils import run_bass_kernel_spmd as _run

    nc = _bacc.Bacc("TRN2", target_bir_lowering=False, num_devices=1)
    arrays, args = {}, []
    for name in _INS:
        a = np.ascontiguousarray(inputs[name])
        arrays[f"in_{name}_dram"] = a
        args.append(nc.dram_tensor(f"in_{name}_dram", a.shape, mybir.dt.from_np(a.dtype), kind="ExternalInput").ap())
    args.append(nc.dram_tensor("out_0_dram", inputs["x"].shape, F32, kind="ExternalOutput").ap())
    build_layer(nc, *args)
    r = _run(nc, [arrays], core_ids=[0])
    return r.results[0]["out_0_dram"]
```

```python
from contextlib import ExitStack

import numpy as np
import concourse.bass as bass
from concourse import mybir

F32 = mybir.dt.float32
F32R = mybir.dt.float32r
BF16 = mybir.dt.bfloat16
ALU = mybir.AluOpType
ACT = mybir.ActivationFunctionType
AX_X = mybir.AxisListType.X

P = 128
D = 256
DC = D // P
H = 16
DH = 64
INNER = H * DH
PAIRS = H // 2
HALF = 512
TOK = 2 * P
QUADS = 8
LN_EPS = 1e-5


def split_matmuls(pe, out, left, right):
    terms = []
    for (lh, ll), (rh, rl) in zip(left, right):
        terms += [(lh, rh), (lh, rl), (ll, rh)]
    for n, (a, b) in enumerate(terms):
        last = pe.matmul(out, a, b, start=n == 0, stop=n == len(terms) - 1)
    return last


def emit_segment_attention(nc, x, wq, wk, wv, wo, betas, x1):
    B, S, _ = x.shape
    ITER = B * S // TOK
    PER_BATCH = S // TOK
    xf = x.rearrange("b s d -> (b s) d")

    with ExitStack() as ctx:
        def sb(name, shape, dt=F32):
            return ctx.enter_context(nc.sbuf_tensor("a_" + name, shape, dt))

        def sem(name):
            return nc.alloc_semaphore("a_" + name)

        psum = ctx.enter_context(nc.psum_tensor("a_psum", [P, 8, HALF], F32))
        bank = [psum[:, i, :] for i in range(8)]
        S_BANK, PT_BANK, ATT_BANK = bank[0:3], bank[3:5], bank[5:7]
        Y_BANK = (bank[2], bank[7])

        ident = sb("ident", [P, P])
        ident2 = sb("ident2", [P, DH])
        block_ones = sb("block_ones", [P, P])
        fold = sb("fold", [P, P])
        neg_half = sb("neg_half", [P, 1])
        beta_rows = sb("beta_rows", [P, INNER])
        beta_cols = sb("beta_cols", [P, PAIRS])
        gate_cols = sb("gate_cols", [P, PAIRS])
        x_in = sb("x_in", [P, 2, D])
        x_res = sb("x_res", [P, 2, D])
        xT_hi = sb("xT_hi", [P, DC, TOK], F32R)
        xT_lo = sb("xT_lo", [P, DC, TOK], F32R)
        qT = sb("qT", [P, 2 * PAIRS, H, 8])
        phi_qT = sb("phi_qT", [P, 4, HALF])
        phi_tok = sb("phi_tok", [P, 4, HALF])
        phiT = sb("phiT", [P, PAIRS, TOK])
        e_k = sb("e_k", [P, 4, HALF])
        k_pad = sb("k_pad", [P, 2 * PAIRS, 2, H, 8])
        vT = sb("vT", [P, 2 * PAIRS, H, 8])
        v_tok = sb("v_tok", [P, 4, HALF])
        v_gated = sb("v_gated", [P, 4, HALF])
        relu_k = v_gated
        mem = sb("mem", [P, PAIRS, DH])
        mem_w = sb("mem_w", [P, 2, PAIRS, P])
        z_part = sb("z_part", [P, PAIRS, 4 * PAIRS])
        z_fold = sb("z_fold", [P, 4 * PAIRS])
        z_sum = sb("z_sum", [P, 2, PAIRS])
        z_acc = sb("z_acc", [P, 3, PAIRS])
        z_inv = sb("z_inv", [P, 2, PAIRS])
        z_gate = sb("z_gate", [P, 2, PAIRS])
        z_diag = sb("z_diag", [P, 2, PAIRS, DH])
        s_sum = sb("s_sum", [P, 4, 8])
        s_inv = sb("s_inv", [P, 4, 8])
        neg_max = sb("neg_max", [P, QUADS, 4])
        row_sum = sb("row_sum", [P, QUADS, 4])
        row_inv = sb("row_inv", [P, QUADS, 4])
        prob = sb("prob", [P, 3, 4, P])
        probT = sb("probT", [P, 2, 4, P])
        attT_hi = sb("attT_hi", [P, PAIRS, TOK], F32R)
        attT_lo = sb("attT_lo", [P, PAIRS, TOK], F32R)
        y = sb("y", [P, 2, D])
        stats = sb("stats", [P, 2, 6])
        mean_var = sb("mean_var", [P, 2, 2])
        var_eps = sb("var_eps", [P, 2])
        rstd = sb("rstd", [P, 2])
        normed = sb("normed", [P, 2, D])
        spare = sb("spare", [P, 2])
        stage = [qT[:, :, :, :].rearrange("p a b c -> p (a b c)"), v_gated[:, :, :].rearrange("p a b -> p (a b)"),
                 v_tok[:, :, :].rearrange("p a b -> p (a b)"), vT[:, :, :, :].rearrange("p a b c -> p (a b c)")]
        WEIGHT_ORDER = (1, 0, 2, 3)

        def w_in(w):
            return w.rearrange("(c p) n -> p c n", p=P)

        sources = [w_in(w) for w in (wq, wk, wv, wo)]
        landed = [sem(f"w{n}_landed") for n in range(4)]
        high_done, low_done = sem("w_high"), sem("w_low")
        W = []
        for n in range(4):
            W.append((sb(f"w{n}_hi", [P, 2048], F32R), sb(f"w{n}_lo", [P, 2048], F32R)))

        def w_cols(n, c, width, a, b):
            return tuple(w[:, c * width + a:c * width + b] for w in W[n])

        c_zero, c_set, c_ident, c_ones = sem("zero"), sem("set"), sem("ident_done"), sem("ones_done")
        beta_in, beta_exp, gate_ready = sem("beta_in"), sem("beta_exp"), sem("gate_ready")
        gate_step, padding = sem("gate_step"), sem("padding")
        x_landed, xres_landed = sem("x_landed"), sem("xres_landed")
        x_turned, xT_hi_ready, xT_lo_ready = sem("x_turned"), sem("xT_hi_ready"), sem("xT_lo_ready")
        q_done, qT_ready, q_exp, phi_ready = sem("q_done"), sem("qT_ready"), sem("q_exp"), sem("phi_ready")
        phi_tok_done, phi_tok_ready = sem("phi_tok_done"), sem("phi_tok_ready")
        ssum_ready, sinv_ready, phin_ready = sem("ssum_ready"), sem("sinv_ready"), sem("phin_ready")
        k_done, k_exp, k_padded, k_summed = sem("k_done"), sem("k_exp"), sem("k_padded"), sem("k_summed")
        phik_ready, zfold_ready, zfold_done = sem("phik_ready"), sem("zfold_ready"), sem("zfold_done")
        z_read = sem("z_read")
        z_step, zgate_ready, zdiag_ready = sem("z_step"), sem("zgate_ready"), sem("zdiag_ready")
        last_vT_ready = sem("last_vT_ready")
        v_done, vT_ready, v_turned, v_copied, v_gated_ready = (sem("v_done"), sem("vT_ready"), sem("v_turned"),
                                                                sem("v_copied"), sem("v_gated_ready"))
        mem_done, mem_added, gz_done, memw_ready = (sem("mem_done"), sem("mem_added"), sem("gz_done"),
                                                    sem("memw_ready"))
        phi_turned, phiT_ready = sem("phi_turned"), sem("phiT_ready")
        scores_done, max_ready, exp_done = sem("scores_done"), sem("max_ready"), sem("exp_done")
        inv_ready, prob_ready, prob_turned, probT_ready = (sem("inv_ready"), sem("prob_ready"),
                                                           sem("prob_turned"), sem("probT_ready"))
        att_done, att_hi_ready, att_lo_ready = sem("att_done"), sem("att_hi_ready"), sem("att_lo_ready")
        y_done, y_added, ln_step, var_ready, rstd_ready = (sem("y_done"), sem("y_added"), sem("ln_step"),
                                                           sem("var_ready"), sem("rstd_ready"))
        normed_ready, stored = sem("normed_ready"), sem("stored")

        def shift_source(b, r, e):
            return b[r * DH:(r + 1) * DH, :].rearrange("p (j e m i) -> p j e m i", j=2, e=2, i=8)[:, :, e, :, :]

        def shift_target(dst, r, e, f):
            return dst[e * DH:(e + 1) * DH, :, 4 * f + r:4 * f + r + 3:2, :].rearrange("p m j i -> p j m i")

        def att_source(u, e, r):
            return ATT_BANK[u % 2][e * DH:(e + 1) * DH, 0:2 * P].rearrange(
                "p (j q r i) -> p j q r i", j=2, r=2, i=8)[:, :, :, r, :]

        def att_block(dst, e, r, t, f):
            at = t * P + e * DH + 2 * f * 8
            return dst[r * DH:(r + 1) * DH, :, at:at + 16].rearrange("p q (j i) -> p j q i", j=2)

        block = ctx.enter_context(nc.Block())

        @block.sync
        def _(sp):
            def tokens(array, it):
                return array[bass.ds(it * TOK, TOK), :].rearrange("(t p) d -> p t d", p=P)

            sp.dma_start(x_in[:, :, :], tokens(xf, 0)).then_inc(x_landed, 16)
            def load_weight(n):
                sp.dma_start(stage[n].rearrange("p (c n) -> p c n", c=sources[n].shape[1]), sources[n]
                             ).then_inc(landed[n], 16)

            for n in WEIGHT_ORDER[:2]:
                load_weight(n)
            for e in range(2):
                sp.dma_start(beta_rows[:, :].rearrange("p (g e d) -> p g e d", e=2, d=DH)[:, :, e, :],
                             betas[0, e * PAIRS:(e + 1) * PAIRS, 0, :].unsqueeze(0).to_broadcast([P, PAIRS, DH])
                             ).then_inc(beta_in, 16)
            with nc.allow_non_contiguous_dma(reason="1024 elements, once"):
                for e in range(2):
                    sp.dma_start(beta_cols[e * DH:(e + 1) * DH, :],
                                 betas[0, e * PAIRS:(e + 1) * PAIRS, 0, :].rearrange("g d -> d g")
                                 ).then_inc(beta_in, 16)
            for n in WEIGHT_ORDER[2:]:
                load_weight(n)
            sp.dma_start(x_res[:, :, :], tokens(xf, 0)).then_inc(xres_landed, 16)
            with sp.Fori(0, ITER - 1) as it:
                sp.wait_ge(x_turned, it + 1)
                sp.dma_start(x_in[:, :, :], tokens(xf, it + 1)).then_inc(x_landed, 16)
                sp.wait_ge(normed_ready, it * 2 + 2)
                sp.dma_start(tokens(x1, it), normed[:, :, :]).then_inc(stored, 16)
                sp.dma_start(x_res[:, :, :], tokens(xf, it + 1)).then_inc(xres_landed, 16)
            sp.wait_ge(x_turned, ITER)
            sp.dma_start(x_in[:, :, :], tokens(xf, 0)).then_inc(x_landed, 16)
            sp.wait_ge(normed_ready, ITER * 2)
            sp.dma_start(tokens(x1, ITER - 1), normed[:, :, :]).then_inc(stored, 16)
            sp.wait_ge(stored, ITER * 16 + 16)

        @block.tensor
        def _(pe):
            def scores(u, it):
                t, f = u // 4, u % 4
                for j in range(2):
                    p = 2 * f + j
                    last = pe.matmul(S_BANK[u % 3][:, j * 256:(j + 1) * 256],
                                     qT[:, t * PAIRS + p, :, :].rearrange("p c i -> p (c i)"),
                                     k_pad[:, t * PAIRS + p, :, :, :].rearrange("p h c i -> p (h c i)"),
                                     start=True, stop=True)
                last.then_inc(scores_done, 1)

            def turn_probs(u, it):
                pe.wait_ge(prob_ready, it * QUADS + u + 1)
                for j in range(4):
                    last = pe.transpose(PT_BANK[u % 2][:, j * P:(j + 1) * P], prob[:, u % 3, j, :], ident[:, :])
                last.then_inc(prob_turned, 1)

            def attend(u, it):
                t, f = u // 4, u % 4
                pe.wait_ge(probT_ready, it * QUADS + u + 1)
                if u >= 2:
                    pe.wait_ge(att_lo_ready, it * QUADS + u - 1)
                for j in range(2):
                    p = 2 * f + j
                    out = ATT_BANK[u % 2][:, j * P:(j + 1) * P]
                    pe.matmul(out, mem_w[:, t, p, :], phiT[:, p, t * P:(t + 1) * P], start=True, stop=False,
                              skip_group_check=True)
                    for h in range(2):
                        c = (2 * p + h) * DH
                        last = pe.matmul(out[h * DH:(h + 1) * DH, :],
                                         v_gated[:, 2 * t + c // HALF, c % HALF:c % HALF + DH],
                                         probT[:, u % 2, 2 * j + h, :], start=False, stop=True,
                                         skip_group_check=True)
                last.then_inc(att_done, 1)

            def project_out(t, it, pairs=range(PAIRS)):
                pe.wait_ge(att_hi_ready, it * QUADS + 4 * t + 4)
                pe.wait_ge(att_lo_ready, it * QUADS + 4 * t + 4)
                s = slice(t * P, (t + 1) * P)
                for p in pairs:
                    left, right = (attT_hi[:, p, s], attT_lo[:, p, s]), w_cols(3, p, D, 0, D)
                    for n, (i, j) in enumerate(((0, 0), (0, 1), (1, 0))):
                        last = pe.matmul(Y_BANK[t][:, 0:D], left[i], right[j], start=p == 0 and n == 0,
                                         stop=p == PAIRS - 1 and n == 2, skip_group_check=True)
                if PAIRS - 1 in pairs:
                    last.then_inc(y_done, 1)

            pe.wait_ge(c_ident, 3)
            pe.wait_ge(c_ones, 6)

            def turn_x(it):
                pe.wait_ge(x_landed, it * 16 + 16)
                for t in range(2):
                    for c in range(DC):
                        last = pe.transpose(bank[4][:, c * TOK + t * P:c * TOK + (t + 1) * P],
                                            x_in[:, t, c * P:(c + 1) * P], ident[:, :])
                last.then_inc(x_turned, 1)

            turn_x(0)
            with pe.Fori(0, ITER) as it:
                pe.wait_ge(xT_hi_ready, it + 1)
                pe.wait_ge(xT_lo_ready, it + 1)
                xT = [(xT_hi[:, c, :], xT_lo[:, c, :]) for c in range(DC)]
                def project(n, f, done):
                    if f == 0:
                        pe.wait_ge(low_done, WEIGHT_ORDER.index(n) + 1)
                    for j in range(2):
                        p = 2 * f + j
                        last = split_matmuls(pe, bank[f + 4 * (n == 0)][:, j * TOK:(j + 1) * TOK],
                                             [w_cols(n, c, INNER, p * P, (p + 1) * P) for c in range(DC)], xT)
                    last.then_inc(done, 1)

                def turn(source, target, done):
                    for j in range(4):
                        last = pe.transpose(target[:, j * P:(j + 1) * P], source[:, j * P:(j + 1) * P], ident[:, :])
                    last.then_inc(done, 1)

                for f in range(4):
                    if f == 2:
                        pe.wait_ge(y_added, it * 2 + 1)
                    project(1, f, k_done)
                for f in range(4):
                    if f == 3:
                        pe.wait_ge(y_added, it * 2 + 2)
                    project(0, f, q_done)
                for f in range(4):
                    pe.wait_ge(k_exp, it * 4 + f + 1)
                    pe.wait_ge(k_padded, it * 4 + f + 1)
                    project(2, f, v_done)
                for u in range(4):
                    pe.wait_ge(phi_ready, it * 4 + u + 1)
                    turn(phi_qT[:, u, :], bank[4 + u], phi_tok_done)
                pe.wait_ge(vT_ready, it * 3 + 3)
                pe.wait_ge(last_vT_ready, it + 1)
                for u in range(4):
                    turn(vT[:, 4 * u:4 * u + 4, :, :].rearrange("p m c i -> p (m c i)"), bank[u], v_turned)

                def memory(t, banks):
                    pe.wait_ge(v_copied, it * 4 + 2 * t + 2)
                    pe.wait_ge(phi_tok_ready, it * 4 + 2 * t + 2)
                    for p in range(PAIRS):
                        u, c = 2 * t + p // 4, (p % 4) * P
                        last = pe.matmul(banks[p // 4][:, c:c + P], phi_tok[:, u, c:c + P], v_tok[:, u, c:c + P],
                                         start=True, stop=True)
                    last.then_inc(mem_done, 1)

                pe.wait_ge(phi_tok_ready, it * 4 + 1)
                pe.wait_ge(zfold_ready, it + 1)
                pe.matmul(bank[4][:, 0:4 * PAIRS], fold[:, :], z_fold[:, :], start=True, stop=True
                          ).then_inc(zfold_done, 1)
                memory(0, bank[0:2])
                memory(1, bank[2:4])

                def spread_gate(t):
                    pe.wait_ge(zdiag_ready, it * 2 + t + 1)
                    pe.matmul(bank[5 + t][:, :], block_ones[:, :], z_diag[:, t, :, :].rearrange("p a b -> p (a b)"),
                              start=True, stop=True).then_inc(gz_done, 1)

                spread_gate(0)
                pe.wait_ge(mem_added, it * 2 + 1)
                scores(0, it)
                spread_gate(1)
                scores(1, it)
                for u in range(4):
                    if u == 2:
                        pe.wait_ge(mem_added, it * 2 + 2)
                        scores(2, it)
                    pe.wait_ge(phin_ready, it * 4 + u + 1)
                    if u == 0:
                        pe.wait_ge(z_read, it + 1)
                    if u >= 2:
                        pe.wait_ge(memw_ready, it * 2 + u - 1)
                    turn(phi_qT[:, u, :], bank[(4, 7, 5, 6)[u]], phi_turned)
                pe.wait_ge(low_done, 4)
                for u in range(2, QUADS):
                    if u > 2:
                        scores(u, it)
                    if u == 3:
                        pe.wait_ge(phiT_ready, it * 4 + 4)
                    turn_probs(u - 2, it)
                    if u in (3, 7):
                        pe.wait_ge(v_gated_ready, it * 4 + (2 if u == 3 else 4))
                    if u >= 3:
                        attend(u - 3, it)
                turn_probs(6, it)
                attend(5, it)
                project_out(0, it, range(0, 1))
                turn_probs(7, it)
                attend(6, it)
                project_out(0, it, range(1, 3))
                attend(7, it)
                project_out(0, it, range(3, PAIRS))
                turn_x(it + 1)
                project_out(1, it)

        @block.scalar
        def _(act):
            def high_weight(n):
                act.wait_ge(landed[n], 16)
                act.copy(W[n][0][:, :], stage[n]).then_inc(high_done, 1)


            def exp_scores(u, it):
                act.wait_ge(max_ready, it * QUADS + u + 1)
                for j in range(4):
                    last = act.activation(prob[:, u % 3, j, :], S_BANK[u % 3][:, j * P:(j + 1) * P], ACT.Exp,
                                          bias=neg_max[:, u, j:j + 1], accum_out=row_sum[:, u, j:j + 1])
                last.then_inc(exp_done, 1)

            def high_x(it):
                act.wait_ge(x_turned, it + 1)
                for c in range(DC):
                    last = act.copy(xT_hi[:, c, :].rearrange("p (e t n) -> p t e n", e=2, t=2),
                                    bank[4][:, c * TOK:(c + 1) * TOK].rearrange("p (t e n) -> p t e n", e=2, t=2))
                last.then_inc(xT_hi_ready, 1)

            def take_att(u, it):
                t, f = u // 4, u % 4
                act.wait_ge(att_done, it * QUADS + u + 1)
                for e in range(2):
                    for r in range(2):
                        last = act.copy(att_block(attT_hi, e, r, t, f), att_source(u, e, r))
                last.then_inc(att_hi_ready, 1)

            high_x(0)
            for n in WEIGHT_ORDER[:2]:
                high_weight(n)
            act.wait_ge(beta_in, 64)
            act.activation(beta_rows[:, :], beta_rows[:, :], ACT.Exp, scale=-1.0).then_inc(beta_exp, 1)
            act.activation(beta_cols[:, :], beta_cols[:, :], ACT.Exp, scale=-1.0).then_inc(beta_exp, 1)
            for n in WEIGHT_ORDER[2:]:
                high_weight(n)
            with act.Fori(0, ITER) as it:
                for f in range(4):
                    act.wait_ge(k_done, it * 4 + f + 1)
                    act.activation(e_k[:, f, :], bank[f][:, :], ACT.Exp)
                    act.activation(relu_k[:, f, :], bank[f][:, :], ACT.Relu).then_inc(k_exp, 1)
                for f in range(4):
                    act.wait_ge(q_done, it * 4 + f + 1)
                    for r in range(2):
                        for e in range(2):
                            last = act.copy(shift_target(qT, r, e, f), shift_source(bank[4 + f], r, e))
                    last.then_inc(qT_ready, 1)
                act.wait_ge(qT_ready, it * 4 + 4)
                for u in range(4):
                    q_unit = qT[:, 4 * u:4 * u + 4, :, :].rearrange("p m c i -> p (m c i)")
                    act.activation(phi_qT[:, u, :], q_unit, ACT.Exp)
                    act.activation(phi_tok[:, u, :], q_unit, ACT.Relu).then_inc(q_exp, 1)
                act.wait_ge(v_done, it * 4 + 4)
                for r in range(2):
                    for e in range(2):
                        last = act.copy(shift_target(vT, r, e, 3), shift_source(bank[3], r, e))
                last.then_inc(last_vT_ready, 1)
                for u in range(4):
                    act.wait_ge(phi_tok_done, it * 4 + u + 1)
                    act.copy(phi_tok[:, u, :], bank[4 + u][:, :]).then_inc(phi_tok_ready, 1)
                for u in range(4):
                    act.wait_ge(v_turned, it * 4 + u + 1)
                    act.copy(v_tok[:, u, :], bank[u][:, :]).then_inc(v_copied, 1)
                exp_scores(0, it)
                for u in range(4):
                    t, f = u // 2, u % 2
                    if u == 2:
                        exp_scores(1, it)
                    act.wait_ge(phi_turned, it * 4 + u + 1)
                    act.copy(phiT[:, 4 * f:4 * f + 4, t * P:(t + 1) * P],
                             bank[(4, 7, 5, 6)[u]][:, :].rearrange("p (a b) -> p a b", a=4)
                             ).then_inc(phiT_ready, 1)
                for u in range(2, QUADS):
                    exp_scores(u, it)
                    if u >= 3:
                        take_att(u - 3, it)
                take_att(5, it)
                take_att(6, it)
                take_att(7, it)
                high_x(it + 1)

        @block.gpsimd
        def _(pool):
            pool.memset(ident[:, :], 0.0).then_inc(c_zero, 1)
            pool.memset(ident2[:, :], 0.0).then_inc(c_zero, 1)
            pool.memset(block_ones[:, :], 0.0).then_inc(c_zero, 1)
            pool.memset(fold[:, :], 0.0).then_inc(c_zero, 1)
            pool.memset(neg_half[:, :], -0.5).then_inc(c_set, 1)
            pool.wait_ge(c_zero, 4)
            pool.affine_select(out=ident[:, :], in_=ident[:, :], compare_op=ALU.not_equal, fill=1.0, base=0,
                               pattern=[[-1, P]], channel_multiplier=1).then_inc(c_ident, 1)
            for h in range(2):
                rows = ident2[h * DH:(h + 1) * DH, :]
                pool.wait_ge(c_ident, h + 1)
                pool.affine_select(out=rows, in_=rows, compare_op=ALU.not_equal, fill=1.0, base=0,
                                   pattern=[[-1, DH]], channel_multiplier=1).then_inc(c_ident, 1)
                pool.wait_ge(c_ident, h + 2)
                pool.memset(block_ones[h * DH:(h + 1) * DH, h * DH:(h + 1) * DH], 1.0).then_inc(c_ones, 1)
                pool.wait_ge(c_ones, 3 * h + 1)
                for g in range(2):
                    block_of = fold[h * DH:(h + 1) * DH, g * DH:(g + 1) * DH]
                    pool.affine_select(out=block_of, in_=block_of, compare_op=ALU.not_equal, fill=1.0, base=0,
                                       pattern=[[-1, DH]], channel_multiplier=1).then_inc(c_ones, 1)
                    pool.wait_ge(c_ones, 3 * h + g + 2)
            pool.wait_ge(c_ident, 3)
            pool.wait_ge(c_set, 1)
            pool.memset(k_pad[:, :, :, :, :].rearrange("p a b c d -> p (a b c d)"), 0.0).then_inc(padding, 1)
            pool.memset(mem_w[:, :, :, :].rearrange("p a b c -> p (a b c)"), 0.0).then_inc(padding, 1)
            pool.wait_ge(gate_ready, 2)

            def normalise(u, it):
                pool.wait_ge(inv_ready, it * QUADS + u + 1)
                pool.tensor_tensor(prob[:, u % 3, :, :], prob[:, u % 3, :, :],
                                   row_inv[:, u, :].unsqueeze(2).to_broadcast([P, 4, P]), ALU.mult
                                   ).then_inc(prob_ready, 1)

            def root(t, it):
                pool.wait_ge(var_ready, it * 2 + t + 1)
                pool.tensor_tensor(rstd[:, t:t + 1], var_eps[:, t:t + 1], neg_half[:, :], ALU.pow
                                   ).then_inc(rstd_ready, 1)

            with pool.Fori(0, ITER) as it:
                def scale_phi(u):
                    pool.wait_ge(sinv_ready, it * 4 + u + 1)
                    pool.tensor_tensor(phi_qT[:, u, :].rearrange("p (h d) -> p h d", d=DH),
                                       phi_tok[:, u, :].rearrange("p (h d) -> p h d", d=DH),
                                       s_inv[:, u, :].unsqueeze(2).to_broadcast([P, 8, DH]), ALU.mult
                                       ).then_inc(phin_ready, 1)

                def spread_z(t):
                    pool.wait_ge(zgate_ready, it * 2 + t + 1)
                    pool.tensor_tensor(z_diag[:, t, :, :], ident2[:, :].unsqueeze(1).to_broadcast([P, PAIRS, DH]),
                                       z_gate[:, t, :].unsqueeze(2).to_broadcast([P, PAIRS, DH]), ALU.mult
                                       ).then_inc(zdiag_ready, 1)

                def gate_v(u):
                    f = u % 2
                    pool.wait_ge(v_copied, it * 4 + u + 1)
                    pool.wait_ge(k_summed, it * 4 + 4)
                    pool.tensor_tensor(v_gated[:, u, :], v_tok[:, u, :], beta_rows[:, f * HALF:(f + 1) * HALF],
                                       ALU.mult).then_inc(v_gated_ready, 1)

                gate_v(0)
                scale_phi(0)
                scale_phi(1)
                spread_z(0)
                spread_z(1)
                scale_phi(2)
                gate_v(1)
                scale_phi(3)
                normalise(0, it)
                normalise(1, it)
                normalise(2, it)
                gate_v(2)
                normalise(3, it)
                gate_v(3)
                normalise(4, it)
                normalise(5, it)
                normalise(6, it)
                normalise(7, it)
                root(0, it)
                root(1, it)

        @block.vector
        def _(dve):
            dve.memset(stats[:, :, :].rearrange("p a b -> p (a b)"), 0.0).then_inc(stored, 16)
            dve.memset(mean_var[:, :, :].rearrange("p a b -> p (a b)"), 0.0).then_inc(y_added, 2)
            def maxima(u, it):
                dve.wait_ge(scores_done, it * QUADS + u + 1)
                dve.tensor_reduce(neg_max[:, u, :], S_BANK[u % 3][:, :].rearrange("p (a b) -> p a b", a=4),
                                  AX_X, ALU.max, negate=True).then_inc(max_ready, 1)

            def inverse(u, it):
                dve.wait_ge(exp_done, it * QUADS + u + 1)
                dve.reciprocal(row_inv[:, u, :], row_sum[:, u, :]).then_inc(inv_ready, 1)

            def low_att(u, it):
                t, f = u // 4, u % 4
                dve.wait_ge(att_hi_ready, it * QUADS + u + 1)
                for e in range(2):
                    for r in range(2):
                        last = dve.tensor_tensor(att_block(attT_lo, e, r, t, f), att_source(u, e, r),
                                                 att_block(attT_hi, e, r, t, f).bitcast(F32), ALU.subtract)
                last.then_inc(att_lo_ready, 1)

            def residual(t, it):
                if t == 0:
                    dve.wait_ge(xres_landed, it * 16 + 16)
                dve.wait_ge(y_done, it * 2 + t + 1)
                dve.tensor_tensor(y[:, t, :], Y_BANK[t][:, 0:D], x_res[:, t, :], ALU.add).then_inc(y_added, 1)
                dve.wait_ge(y_added, it * 2 + 2 + t + 1)
                dve.bn_stats(stats[:, t, :], y[:, t, :]).then_inc(ln_step, 1)
                dve.wait_ge(ln_step, it * 4 + 2 * t + 1)
                dve.memset(spare[:, t:t + 1], 0.0)
                dve.bn_aggr(mean_var[:, t, :], stats[:, t, :]).then_inc(ln_step, 1)
                dve.wait_ge(ln_step, it * 4 + 2 * t + 2)
                dve.tensor_scalar(var_eps[:, t:t + 1], mean_var[:, t, 1:2], LN_EPS, None, ALU.add
                                  ).then_inc(var_ready, 1)

            def normalise(t, it):
                dve.wait_ge(rstd_ready, it * 2 + t + 1)
                dve.wait_ge(stored, it * 16 + 16)
                dve.tensor_scalar(normed[:, t, :], y[:, t, :], mean_var[:, t, 0:1], rstd[:, t:t + 1],
                                  ALU.subtract, ALU.mult).then_inc(normed_ready, 1)

            def take_probT(u, it):
                dve.wait_ge(prob_turned, it * QUADS + u + 1)
                dve.tensor_copy(probT[:, u % 2, :, :].rearrange("p a b -> p (a b)"), PT_BANK[u % 2][:, :]
                                ).then_inc(probT_ready, 1)

            def low_x(it):
                dve.wait_ge(xT_hi_ready, it + 1)
                for c in range(DC):
                    last = dve.tensor_tensor(
                        xT_lo[:, c, :].rearrange("p (e t n) -> p t e n", e=2, t=2),
                        bank[4][:, c * TOK:(c + 1) * TOK].rearrange("p (t e n) -> p t e n", e=2, t=2),
                        xT_hi[:, c, :].rearrange("p (e t n) -> p t e n", e=2, t=2).bitcast(F32), ALU.subtract)
                last.then_inc(xT_lo_ready, 1)

            low_x(0)
            def low_weight(n):
                dve.wait_ge(high_done, n + 1)
                weight = WEIGHT_ORDER[n]
                dve.tensor_tensor(W[weight][1][:, :], stage[weight], W[weight][0][:, :].bitcast(F32), ALU.subtract
                                  ).then_inc(low_done, 1)

            low_weight(0)
            low_weight(1)
            dve.wait_ge(beta_exp, 2)
            dve.tensor_scalar(beta_rows[:, :], beta_rows[:, :], 1.0, None, ALU.add).then_inc(gate_step, 1)
            dve.tensor_scalar(beta_cols[:, :], beta_cols[:, :], 1.0, None, ALU.add).then_inc(gate_step, 1)
            dve.wait_ge(gate_step, 2)
            dve.reciprocal(beta_rows[:, :], beta_rows[:, :]).then_inc(gate_step, 1)
            dve.reciprocal(gate_cols[:, :], beta_cols[:, :]).then_inc(gate_ready, 1)
            dve.wait_ge(gate_step, 3)
            dve.tensor_scalar(beta_rows[:, :], beta_rows[:, :], -1.0, 1.0, ALU.mult, ALU.add
                              ).then_inc(gate_ready, 1)
            low_weight(2)
            low_weight(3)
            dve.wait_ge(padding, 2)
            with dve.Fori(0, B) as b:
                dve.memset(mem[:, :, :].rearrange("p a b -> p (a b)"), 0.0).then_inc(z_step, 1)
                dve.memset(z_acc[:, 2, :], 0.0).then_inc(z_step, 1)
                with dve.Fori(0, PER_BATCH) as n:
                    it = b * PER_BATCH + n
                    zb = b * (2 + 4 * PER_BATCH) + n * 4 + 2
                    def pad_k(f):
                        dve.wait_ge(k_done, it * 4 + f + 1)
                        dve.wait_ge(k_exp, it * 4 + f + 1)
                        for r in range(2):
                            for e in range(2):
                                last = dve.tensor_scalar(shift_target(k_pad[:, :, e, :, :], r, e, f),
                                                         shift_source(bank[f], r, e), DH ** -0.5, None, ALU.mult)
                        last.then_inc(k_padded, 1)

                    def make_phi_k(f):
                        dve.scalar_tensor_tensor(out=e_k[:, f, :], in0=e_k[:, f, :], scalar=1.0,
                                                 in1=relu_k[:, f, :], op0=ALU.min, op1=ALU.add
                                                 ).then_inc(phik_ready, 1)

                    def sum_phi_k(f):
                        dve.wait_ge(phik_ready, it * 4 + f + 1)
                        dve.tensor_reduce(z_part[:, 2 * f:2 * f + 2, :].rearrange("p j m -> p (j m)"),
                                          e_k[:, f, :].rearrange("p (m i) -> p m i", i=8), AX_X, ALU.add
                                          ).then_inc(k_summed, 1)

                    for f in range(4):
                        pad_k(f)
                    for f in range(4):
                        make_phi_k(f)
                    def shift_v(f):
                        dve.wait_ge(v_done, it * 4 + f + 1)
                        for r in range(2):
                            for e in range(2):
                                last = dve.tensor_copy(shift_target(vT, r, e, f), shift_source(bank[f], r, e))
                        last.then_inc(vT_ready, 1)

                    def make_phi_q(u):
                        dve.wait_ge(q_exp, it * 4 + u + 1)
                        dve.scalar_tensor_tensor(out=phi_qT[:, u, :], in0=phi_qT[:, u, :], scalar=1.0,
                                                 in1=phi_tok[:, u, :], op0=ALU.min, op1=ALU.add
                                                 ).then_inc(phi_ready, 1)

                    shift_v(0)
                    shift_v(1)
                    make_phi_q(0)
                    make_phi_q(1)
                    make_phi_q(2)
                    shift_v(2)
                    make_phi_q(3)
                    def phi_sum(u):
                        dve.wait_ge(phi_tok_ready, it * 4 + u + 1)
                        dve.tensor_reduce(s_sum[:, u, :], phi_tok[:, u, :].rearrange("p (h d) -> p h d", d=DH),
                                          AX_X, ALU.add).then_inc(ssum_ready, 1)
                        dve.wait_ge(ssum_ready, it * 4 + u + 1)
                        dve.reciprocal(s_inv[:, u, :], s_sum[:, u, :]).then_inc(sinv_ready, 1)

                    for f in range(4):
                        sum_phi_k(f)
                    dve.wait_ge(k_summed, it * 4 + 4)
                    dve.tensor_reduce(z_fold[:, :], z_part[:, :, :].rearrange("p a m -> p m a"), AX_X, ALU.add
                                      ).then_inc(zfold_ready, 1)
                    phi_sum(0)
                    phi_sum(1)
                    dve.wait_ge(zfold_done, it + 1)
                    for e in range(2):
                        rows = slice(e * DH, (e + 1) * DH)
                        last = dve.tensor_copy(z_sum[rows, :, :].rearrange("p t g -> p (t g)"),
                                               bank[4][rows, e * 16:(e + 1) * 16])
                    last.then_inc(z_read, 1)
                    dve.wait_ge(z_read, it + 1)
                    dve.wait_ge(z_step, zb)
                    dve.tensor_tensor(z_acc[:, 0, :], z_acc[:, 2, :], z_sum[:, 0, :], ALU.add).then_inc(z_step, 1)
                    dve.wait_ge(z_step, zb + 1)
                    dve.tensor_tensor(z_acc[:, 1, :], z_acc[:, 0, :], z_sum[:, 1, :], ALU.add).then_inc(z_step, 1)
                    dve.wait_ge(z_step, zb + 2)
                    dve.tensor_copy(z_acc[:, 2, :], z_acc[:, 1, :]).then_inc(z_step, 1)
                    dve.reciprocal(z_inv[:, :, :], z_acc[:, 0:2, :]).then_inc(z_step, 1)
                    dve.wait_ge(z_step, zb + 4)
                    for t in range(2):
                        dve.tensor_tensor(z_gate[:, t, :], z_inv[:, t, :], gate_cols[:, :], ALU.mult
                                          ).then_inc(zgate_ready, 1)
                    for t in range(2):
                        if t == 1:
                            dve.wait_ge(memw_ready, it * 2 + 1)
                        dve.wait_ge(mem_done, it * 2 + t + 1)
                        for h in range(2):
                            rows = slice(h * DH, (h + 1) * DH)
                            products = psum[rows, 2 * t:2 * t + 2, :].rearrange("p g (a h d) -> p (g a) h d", a=4, h=2)
                            last = dve.tensor_tensor(mem[rows, :, :], products[:, :, h, :], mem[rows, :, :], ALU.add)
                        last.then_inc(mem_added, 1)
                        if t == 0:
                            phi_sum(2)
                            phi_sum(3)
                        dve.wait_ge(mem_added, it * 2 + t + 1)
                        dve.wait_ge(gz_done, it * 2 + t + 1)
                        for h in range(2):
                            rows = slice(h * DH, (h + 1) * DH)
                            last = dve.tensor_tensor(
                                mem_w[rows, t, :, h * DH:(h + 1) * DH],
                                bank[5 + t][rows, :].rearrange("p (a d) -> p a d", a=PAIRS),
                                mem[rows, :, :], ALU.mult)
                        last.then_inc(memw_ready, 1)
                        maxima(t, it)
                    inverse(0, it)
                    for u in range(2, QUADS):
                        maxima(u, it)
                        inverse(u - 1, it)
                        take_probT(u - 2, it)
                        if u >= 4:
                            low_att(u - 4, it)
                    inverse(7, it)
                    take_probT(6, it)
                    low_att(4, it)
                    take_probT(7, it)
                    low_att(5, it)
                    low_att(6, it)
                    low_att(7, it)
                    low_x(it + 1)
                    residual(0, it)
                    normalise(0, it)
                    residual(1, it)
                    normalise(1, it)


def emit_cross_attention(nc, x1, context, wq, wkv, wo, bias, x2_all):
    B, CTX, CD = context.shape
    CK = CD // 2
    ITER = x1.shape[0] // TOK
    PER_BATCH = ITER // B
    NW = 2 * CTX

    with ExitStack() as ctx:
        def sb(name, shape, dt=F32):
            return ctx.enter_context(nc.sbuf_tensor("x_" + name, shape, dt))

        def sem(name):
            return nc.alloc_semaphore("x_" + name)

        bank = [ctx.enter_context(nc.psum_tensor(f"x_bank{i}", [P, HALF], F32)) for i in range(8)]
        S_BANK, PT_BANK, ATT_BANK, Q_BANK, Y_BANK = bank[0:2], bank[2:4], bank[4:6], bank[6], bank[7]
        START_BANK = bank[2:6]

        ident = sb("ident", [P, P])
        neg_half = sb("neg_half", [P, 1])
        bias_rows = sb("bias_rows", [P, D])
        ctx_in = sb("ctx_in", [CTX, B, CD])
        ctxT = sb("ctxT", [CK, 2, B, CTX])
        w_kv = sb("w_kv", [CK, 2, 2 * INNER])
        k_pad = sb("k_pad", [P, B, PAIRS, 2, CTX])
        v_all = sb("v_all", [P, B, INNER])
        v_now = sb("v_now", [P, INNER])
        x_in = sb("x_in", [P, 2, D])
        x_res = sb("x_res", [P, 2, D])
        x_bias = sb("x_bias", [P, 2, D])
        xT_hi = sb("xT_hi", [P, DC, TOK], F32R)
        xT_lo = sb("xT_lo", [P, DC, TOK], F32R)
        qT = sb("qT", [P, 2, PAIRS, TOK])
        neg_max = sb("neg_max", [P, QUADS, 4])
        row_sum = sb("row_sum", [P, QUADS, 4])
        row_inv = sb("row_inv", [P, QUADS, 4])
        prob = sb("prob", [P, 4, 4, CTX])
        probT = sb("probT", [P, 2, 4, P])
        attT_hi = sb("attT_hi", [P, 4, 2, P], F32R)
        attT_lo = sb("attT_lo", [P, 4, 2, P], F32R)
        y = sb("y", [P, 2, D])
        stats = sb("stats", [P, 2, 6])
        mean_var = sb("mean_var", [P, 2, 2])
        var_eps = sb("var_eps", [P, 2])
        rstd = sb("rstd", [P, 2])
        spare = sb("spare", [P, 2])
        stage = [sb(f"stage{n}", [P, 2048]) for n in range(2)]
        sources = [w.rearrange("(c p) n -> p c n", p=P) for w in (wq, wo)]
        W = [(sb(f"w{n}_hi", [P, 2048], F32R), sb(f"w{n}_lo", [P, 2048], F32R)) for n in range(2)]

        def w_cols(n, c, width, a, b):
            return tuple(w[:, c * width + a:c * width + b] for w in W[n])

        c_zero, c_ident, zeroed = sem("zero"), sem("ident_done"), sem("zeroed")
        landed = [sem("w_landed0"), sem("w_landed1")]
        high_done, low_done, ctx_landed, wkv_landed, bias_landed = (sem("w_high"), sem("w_low"), sem("ctx_landed"),
                                                                    sem("wkv_landed"), sem("bias_landed"))
        ctx_turned, ctxT_ready, ctx_k_done, ctx_k_ready = (sem("ctx_turned"), sem("ctxT_ready"),
                                                           sem("ctx_k_done"), sem("ctx_k_ready"))
        ctx_v_done, ctx_v_ready = sem("ctx_v_done"), sem("ctx_v_ready")
        v_landed = [sem(f"v_landed{f}") for f in range(4)]
        v_zeroed, normed_ready = sem("v_zeroed"), sem("normed_ready")
        x_landed, xres_landed, xbias_ready = sem("x_landed"), sem("xres_landed"), sem("xbias_ready")
        x_turned, xT_hi_ready, xT_lo_ready = sem("x_turned"), sem("xT_hi_ready"), sem("xT_lo_ready")
        q_done, qT_ready = sem("q_done"), sem("qT_ready")
        scores_done, max_ready, exp_done = sem("scores_done"), sem("max_ready"), sem("exp_done")
        inv_ready, prob_ready, prob_turned, probT_ready = (sem("inv_ready"), sem("prob_ready"),
                                                           sem("prob_turned"), sem("probT_ready"))
        att_done, att_hi_ready, att_lo_ready = sem("att_done"), sem("att_hi_ready"), sem("att_lo_ready")
        y_done, y_added, ln_step, var_ready, rstd_ready = (sem("y_done"), sem("y_added"), sem("ln_step"),
                                                           sem("var_ready"), sem("rstd_ready"))

        TURN, ATTEND, PROJECT = 2, 3, 5

        def all_pairs(engine, pair):
            pair(0, 0, True)
            with engine.Fori(1, PER_BATCH // 2) as n:
                pair(0, n, False)
            with engine.Fori(1, B) as b:
                with engine.Fori(0, PER_BATCH // 2) as n:
                    pair(b, b * (PER_BATCH // 2) + n, False)

        block = ctx.enter_context(nc.Block())

        @block.sync
        def _(sp):
            sp.dma_start(ctx_in[:, :, :], context.rearrange("b s d -> s b d")).then_inc(ctx_landed, 16)
            sp.dma_start(w_kv[:, :, :], wkv.rearrange("(c p) n -> p c n", p=CK)).then_inc(wkv_landed, 16)
            for n in range(2):
                sp.dma_start(stage[n][:, :].rearrange("p (c n) -> p c n", c=sources[n].shape[1]), sources[n]
                             ).then_inc(landed[n], 16)
            sp.dma_start(bias_rows[:, :], bias.unsqueeze(0).to_broadcast([P, D])).then_inc(bias_landed, 16)

            def tokens(array, it):
                return array[bass.ds(it * TOK, TOK), :].rearrange("(t p) d -> p t d", p=P)

            sp.dma_start(x_in[:, :, :], tokens(x1, 0)).then_inc(x_landed, 16)
            sp.dma_start(x_res[:, :, :], tokens(x1, 0)).then_inc(xres_landed, 16)
            sp.wait_ge(ctx_v_ready, 2 * B)

            sp.wait_ge(x_turned, 1)
            sp.dma_start(x_in[:, :, :], tokens(x1, 1)).then_inc(x_landed, 16)

            def values(b, first=False):
                for f in range(4):
                    if not first:
                        sp.wait_ge(att_done, b * (PER_BATCH * QUADS) - 3 + f)
                    sp.dma_start(v_now[:, f * 4 * DH:(f + 1) * 4 * DH],
                                 v_all[:, bass.ds(b, 1), f * 4 * DH:(f + 1) * 4 * DH].rearrange("p b n -> p (b n)")
                                 ).then_inc(v_landed[f], 16)

            def ahead(it, distance):
                sp.wait_ge(x_turned, it + 2)
                sp.dma_start(x_in[:, :, :], tokens(x1, it + distance)).then_inc(x_landed, 16)

            def forward(it):
                sp.wait_ge(xbias_ready, it)
                sp.dma_start(x_res[:, :, :], tokens(x1, it)).then_inc(xres_landed, 16)

            values(0, first=True)
            ahead(0, 2)
            with sp.Fori(1, PER_BATCH) as it:
                ahead(it, 2)
                forward(it)
            with sp.Fori(1, B - 1) as b:
                ahead(b * PER_BATCH, 2)
                values(b)
                forward(b * PER_BATCH)
                with sp.Fori(1, PER_BATCH) as n:
                    ahead(b * PER_BATCH + n, 2)
                    forward(b * PER_BATCH + n)
            for it in range(ITER - PER_BATCH, ITER):
                ahead(it, 2 if it + 2 < ITER else 0)
                if it == ITER - PER_BATCH:
                    values(B - 1)
                forward(it)

        @block.tensor
        def _(pe):
            now = 0

            def turn_x(it, first=False):
                pe.wait_ge(x_landed, it * 16 + 16)
                if not first:
                    pe.wait_ge(qT_ready, it * 4)
                for t in range(2):
                    for c in range(DC):
                        last = pe.transpose(Q_BANK[:, c * TOK + t * P:c * TOK + (t + 1) * P],
                                            x_in[:, t, c * P:(c + 1) * P], ident[:, :])
                last.then_inc(x_turned, 1)

            def project_q(p, it, start_bank=None):
                f, j = p // 2, p % 2
                if p == 0:
                    pe.wait_ge(xT_hi_ready, it + 1)
                    pe.wait_ge(xT_lo_ready, it + 1)
                elif j == 0 and start_bank is None:
                    pe.wait_ge(qT_ready, it * 4 + f)
                target = Q_BANK if start_bank is None else start_bank
                last = split_matmuls(pe, target[:, j * TOK:(j + 1) * TOK],
                                     [w_cols(0, c, INNER, p * P, (p + 1) * P) for c in range(DC)],
                                     [(xT_hi[:, c, :], xT_lo[:, c, :]) for c in range(DC)])
                if j == 1:
                    last.then_inc(q_done, 1)

            def scores(u, it, b, first):
                t, f = u // 4, u % 4
                if not first or u >= 2:
                    pe.wait_ge(exp_done, it * QUADS + u - 1)
                for j in range(2):
                    p = 2 * f + j
                    last = pe.matmul(S_BANK[u % 2][:, j * NW:(j + 1) * NW], qT[:, now, p, t * P:(t + 1) * P],
                                     k_pad[:, bass.ds(b, 1), p, :, :].rearrange("p b h n -> p (b h n)"),
                                     start=True, stop=True)
                last.then_inc(scores_done, 1)

            def turn_probs(u, it):
                pe.wait_ge(prob_ready, it * QUADS + u + 1)
                for j in range(4):
                    last = pe.transpose(PT_BANK[u % 2][0:CTX, j * P:(j + 1) * P], prob[:, u % 4, j, :], ident[:, :])
                last.then_inc(prob_turned, 1)

            def attend(u, it, b, first):
                f = u % 4
                if 0 <= u < 4:
                    pe.wait_ge(v_landed[f], b * 16 + 16)
                pe.wait_ge(probT_ready, it * QUADS + u + 1)
                if not first or u >= 2:
                    pe.wait_ge(att_lo_ready, it * QUADS + u - 1)
                for j in range(2):
                    for h in range(2):
                        c = (2 * (2 * f + j) + h) * DH
                        last = pe.matmul(ATT_BANK[u % 2][h * DH:(h + 1) * DH, j * P:(j + 1) * P],
                                         v_now[:, c:c + DH], probT[:, u % 2, 2 * j + h, :], start=True, stop=True)
                last.then_inc(att_done, 1)

            def project_out(u, it, first):
                f = u % 4
                pe.wait_ge(att_hi_ready, it * QUADS + u + 1)
                pe.wait_ge(att_lo_ready, it * QUADS + u + 1)
                if f == 0 and not (first and u == 0):
                    pe.wait_ge(y_added, it * 2 + u // 4)
                n = 0
                for j in range(2):
                    left = [part[:, u % 4, j, :] for part in (attT_hi, attT_lo)]
                    right = w_cols(1, 2 * f + j, D, 0, D)
                    for a, c in ((0, 0), (0, 1), (1, 0)):
                        last = pe.matmul(Y_BANK[:, 0:D], left[a], right[c], start=f == 0 and n == 0,
                                         stop=f == 3 and n == 5, skip_group_check=True)
                        n += 1
                if f == 3:
                    last.then_inc(y_done, 1)

            def step(u, parity, it, b, first, new=True):
                nonlocal now
                now = parity
                if new:
                    scores(u, it, b, first)
                    if u < 7:
                        project_q(u, it + 1)
                    if u == 6:
                        project_q(7, it + 1)
                    if u == 7:
                        turn_x(it + 2)
                if new and u >= TURN or u < TURN and not first:
                    turn_probs(u - TURN, it)
                if new and u >= ATTEND or u < ATTEND and not first:
                    attend(u - ATTEND, it, b, first)
                if new and u >= PROJECT or u < PROJECT and not first:
                    project_out(u - PROJECT, it, first)
            pe.wait_ge(c_ident, 1)
            pe.wait_ge(ctx_landed, 16)
            for c in range(2):
                for b in range(B):
                    last = pe.transpose(bank[c][0:CK, b * CTX:(b + 1) * CTX], ctx_in[:, b, c * CK:(c + 1) * CK],
                                        ident[0:CTX, 0:CTX])
            last.then_inc(ctx_turned, 1)
            pe.wait_ge(ctxT_ready, 1)
            pe.wait_ge(wkv_landed, 16)
            for p in range(PAIRS):
                if p >= 6:
                    pe.wait_ge(ctx_k_ready, p - 5)
                for c in range(2):
                    last = pe.matmul(bank[2 + p % 6][:, 0:B * CTX], w_kv[:, c, p * P:(p + 1) * P],
                                     ctxT[:, c, :, :].rearrange("p b n -> p (b n)"), start=c == 0, stop=c == 1)
                last.then_inc(ctx_k_done, 1)
            pe.wait_ge(ctx_k_ready, 5)
            turn_x(0, first=True)
            for n in range(2 * B):
                b, f = n // 2, n % 2
                if n >= 2:
                    pe.wait_ge(ctx_v_ready, n - 1)
                for c in range(2):
                    last = pe.matmul(bank[n % 2][0:CTX, :], ctxT[:, c, b, :],
                                     w_kv[:, c, INNER + f * HALF:INNER + (f + 1) * HALF], start=c == 0, stop=c == 1)
                last.then_inc(ctx_v_done, 1)
            pe.wait_ge(ctx_k_ready, PAIRS)
            pe.wait_ge(ctx_v_ready, 2 * B)
            pe.wait_ge(low_done, 2)
            for p in range(PAIRS):
                project_q(p, 0, START_BANK[p // 2])
            turn_x(1, first=True)
            pe.wait_ge(qT_ready, 4)

            def pair(b, n, start):
                for parity in range(2):
                    for u in range(QUADS):
                        step(u, parity, 2 * n + parity, b, start and parity == 0)

            all_pairs(pe, pair)
            for u in range(PROJECT):
                step(u, 0, ITER, B, False, new=False)

        @block.scalar
        def _(act):
            for n in range(2):
                act.wait_ge(landed[n], 16)
                act.copy(W[n][0][:, :], stage[n][:, :]).then_inc(high_done, 1)
            def high_x(it):
                act.wait_ge(x_turned, it + 1)
                act.copy(xT_hi[:, :, :].rearrange("p a b -> p (a b)"), Q_BANK[:, :]).then_inc(xT_hi_ready, 1)

            high_x(0)
            act.wait_ge(v_zeroed, 1)
            for n in range(2 * B):
                b, f = n // 2, n % 2
                act.wait_ge(ctx_v_done, n + 1)
                act.copy(v_all[0:CTX, b, f * HALF:(f + 1) * HALF], bank[n % 2][0:CTX, :]).then_inc(ctx_v_ready, 1)

            def exp_scores(u, it):
                act.wait_ge(max_ready, it * QUADS + u + 1)
                for j in range(4):
                    last = act.activation(prob[:, u % 4, j, :], S_BANK[u % 2][:, j * CTX:(j + 1) * CTX], ACT.Exp,
                                          bias=neg_max[:, u, j:j + 1], accum_out=row_sum[:, u, j:j + 1])
                last.then_inc(exp_done, 1)

            def take_att(u, it):
                act.wait_ge(att_done, it * QUADS + u + 1)
                act.copy(attT_hi[:, u % 4, :, :], ATT_BANK[u % 2][:, 0:2 * P].rearrange("p (a b) -> p a b", a=2)
                         ).then_inc(att_hi_ready, 1)

            high_x(1)

            def pair(b, n, start):
                for parity in range(2):
                    it = 2 * n + parity
                    for u in range(QUADS):
                        if u == 7:
                            high_x(it + 2)
                        exp_scores(u, it)
                        if u >= ATTEND or not (start and parity == 0):
                            take_att(u - ATTEND, it)

            all_pairs(act, pair)
            for u in range(ATTEND):
                take_att(u - ATTEND, ITER)

        @block.gpsimd
        def _(pool):
            pool.memset(ident[:, :], 0.0).then_inc(c_zero, 1)
            pool.memset(neg_half[:, :], -0.5).then_inc(c_zero, 1)
            pool.wait_ge(c_zero, 2)
            pool.affine_select(out=ident[:, :], in_=ident[:, :], compare_op=ALU.not_equal, fill=1.0, base=0,
                               pattern=[[-1, P]], channel_multiplier=1).then_inc(c_ident, 1)
            pool.memset(v_all[:, :, :].rearrange("p a b -> p (a b)"), 0.0).then_inc(v_zeroed, 1)
            pool.wait_ge(bias_landed, 16)

            def normalise(u, it):
                pool.wait_ge(inv_ready, it * QUADS + u + 1)
                pool.tensor_tensor(prob[:, u % 4, :, :], prob[:, u % 4, :, :],
                                   row_inv[:, u, :].unsqueeze(2).to_broadcast([P, 4, CTX]), ALU.mult
                                   ).then_inc(prob_ready, 1)

            def add_bias(it, first=False):
                pool.wait_ge(xres_landed, it * 16 + 16)
                if not first:
                    pool.wait_ge(y_added, it * 2)
                pool.tensor_tensor(x_bias[:, :, :], x_res[:, :, :],
                                   bias_rows[:, :].unsqueeze(1).to_broadcast([P, 2, D]), ALU.add
                                   ).then_inc(xbias_ready, 1)

            def root(t, it):
                pool.wait_ge(var_ready, it * 2 + t + 1)
                pool.tensor_tensor(rstd[:, t:t + 1], var_eps[:, t:t + 1], neg_half[:, :], ALU.pow
                                   ).then_inc(rstd_ready, 1)

            def pair(b, n, start):
                for parity in range(2):
                    it = 2 * n + parity
                    first = start and parity == 0
                    for u in range(QUADS):
                        normalise(u, it)
                        if u == 1 and not first:
                            root(0, it - 1)
                        if u == 5 and not first:
                            root(1, it - 1)
                    add_bias(it, first)

            all_pairs(pool, pair)
            root(0, ITER - 1)
            root(1, ITER - 1)

        @block.vector
        def _(dve):
            dve.memset(k_pad[:, :, :, :, :].rearrange("p a b c d -> p (a b c d)"), 0.0).then_inc(zeroed, 1)
            dve.wait_ge(ctx_turned, 1)
            for c in range(2):
                last = dve.tensor_copy(ctxT[:, c, :, :].rearrange("p b n -> p (b n)"), bank[c][0:CK, 0:B * CTX])
            last.then_inc(ctxT_ready, 1)
            dve.memset(probT[:, :, :, :].rearrange("p a b c -> p (a b c)"), 0.0).then_inc(zeroed, 1)
            dve.wait_ge(zeroed, 2)
            for p in range(PAIRS):
                dve.wait_ge(ctx_k_done, p + 1)
                for h in range(2):
                    rows = slice(h * DH, (h + 1) * DH)
                    last = dve.tensor_copy(k_pad[rows, :, p, h, :],
                                           bank[2 + p % 6][rows, 0:B * CTX].rearrange("p (b n) -> p b n", b=B))
                last.then_inc(ctx_k_ready, 1)
            def low_x(it):
                dve.wait_ge(xT_hi_ready, it + 1)
                dve.tensor_tensor(xT_lo[:, :, :].rearrange("p a b -> p (a b)"), Q_BANK[:, :],
                                  xT_hi[:, :, :].rearrange("p a b -> p (a b)").bitcast(F32), ALU.subtract
                                  ).then_inc(xT_lo_ready, 1)

            low_x(0)
            for n in range(2):
                dve.wait_ge(high_done, n + 1)
                dve.tensor_tensor(W[n][1][:, :], stage[n][:, :], W[n][0][:, :].bitcast(F32), ALU.subtract
                                  ).then_inc(low_done, 1)

            def maxima(u, it):
                dve.wait_ge(scores_done, it * QUADS + u + 1)
                dve.tensor_reduce(neg_max[:, u, :], S_BANK[u % 2][:, 0:4 * CTX].rearrange("p (a b) -> p a b", a=4),
                                  AX_X, ALU.max, negate=True).then_inc(max_ready, 1)

            def inverse(u, it):
                dve.wait_ge(exp_done, it * QUADS + u + 1)
                dve.reciprocal(row_inv[:, u, :], row_sum[:, u, :]).then_inc(inv_ready, 1)

            def low_att(u, it):
                dve.wait_ge(att_hi_ready, it * QUADS + u + 1)
                dve.tensor_tensor(attT_lo[:, u % 4, :, :],
                                  ATT_BANK[u % 2][:, 0:2 * P].rearrange("p (a b) -> p a b", a=2),
                                  attT_hi[:, u % 4, :, :].bitcast(F32), ALU.subtract
                                  ).then_inc(att_lo_ready, 1)

            def residual(t, it):
                if t == 0:
                    dve.wait_ge(xbias_ready, it + 1)
                dve.wait_ge(y_done, it * 2 + t + 1)
                dve.tensor_tensor(y[:, t, :], Y_BANK[:, 0:D], x_bias[:, t, :], ALU.add).then_inc(y_added, 1)

            def statistics(t, it):
                dve.wait_ge(y_added, it * 2 + t + 1)
                dve.bn_stats(stats[:, t, :], y[:, t, :]).then_inc(ln_step, 1)
                dve.wait_ge(ln_step, it * 4 + 2 * t + 1)
                dve.memset(spare[:, t:t + 1], 0.0)
                dve.bn_aggr(mean_var[:, t, :], stats[:, t, :]).then_inc(ln_step, 1)
                dve.wait_ge(ln_step, it * 4 + 2 * t + 2)
                dve.tensor_scalar(var_eps[:, t:t + 1], mean_var[:, t, 1:2], LN_EPS, None, ALU.add
                                  ).then_inc(var_ready, 1)

            def normalise(t, it):
                dve.wait_ge(rstd_ready, it * 2 + t + 1)
                dve.tensor_scalar(x2_all[:, bass.ds(it * 2 + t, 1), :].rearrange("p a d -> p (a d)"), y[:, t, :],
                                  mean_var[:, t, 0:1], rstd[:, t:t + 1], ALU.subtract, ALU.mult
                                  ).then_inc(normed_ready, 1)

            def take_q(f, it, parity, source=Q_BANK):
                dve.wait_ge(q_done, it * 4 + f + 1)
                dve.tensor_scalar(qT[:, parity, 2 * f:2 * f + 2, :].rearrange("p a b -> p (a b)"), source[:, :],
                                  DH ** -0.5, None, ALU.mult).then_inc(qT_ready, 1)

            def take_probT(u, it):
                dve.wait_ge(prob_turned, it * QUADS + u + 1)
                dve.tensor_copy(probT[0:CTX, u % 2, :, :].rearrange("p a b -> p (a b)"), PT_BANK[u % 2][0:CTX, :]
                                ).then_inc(probT_ready, 1)

            for f in range(4):
                take_q(f, 0, 0, START_BANK[f])
            low_x(1)

            def step(u, parity, it, first, new=True):
                if new:
                    maxima(u, it)
                if u in (1, 5) and not first:
                    residual(u // 4, it - 1)
                if new and u in (1, 3, 5, 6):
                    take_q((1, 3, 5, 6).index(u), it + 1, 1 - parity)
                if u in (1, 5) and not first:
                    statistics(u // 4, it - 1)
                if new and u >= TURN or u < TURN and not first:
                    take_probT(u - TURN, it)
                if new and u == 7:
                    low_x(it + 2)
                if new:
                    inverse(u, it)
                if u in (2, 6) and not first:
                    normalise(u // 4, it - 1)
                if new and u >= ATTEND or u < ATTEND and not first:
                    low_att(u - ATTEND, it)

            def pair(b, n, start):
                for parity in range(2):
                    for u in range(QUADS):
                        step(u, parity, 2 * n + parity, start and parity == 0)

            all_pairs(dve, pair)
            for u in range(PROJECT + 2):
                step(u, 0, ITER, False, new=False)


HD = D // H
GROUPS = H // 4
ZC = GROUPS // 2
Q_PART = (0, 1, 0, 1, 2, 0, 2, 1)
K_PART = (0, 0, 1, 1, 0, 2, 1, 2)
NSTACK = 16 * 16


def load_stacks(sp, parts, b, group, slot, stacks, landed):
    for n, (stack, order) in enumerate(zip(stacks, (Q_PART, K_PART))):
        for blk, part in enumerate(order):
            src = parts[bass.ds(b, 1), n, part, group * 4 * HD:(group + 1) * 4 * HD, :].rearrange(
                "b (h i) s -> i (b h) s", i=HD)
            sp.dma_start(stack[blk * HD:(blk + 1) * HD, slot, :, :], src).then_inc(landed[slot], 16)


def emit_query_softmax(nc, x2_all, wq, wk, wv, wo, wff, parts, out):
    B, S = out.shape[0], out.shape[1]
    with ExitStack() as ctx:
        def sb(name, shape, dt=F32):
            return ctx.enter_context(nc.sbuf_tensor("f_" + name, shape, dt))

        v_all = sb("v_all", [P, B, S // P, D])
        stacks = [sb(f"stack{n}", [P, 2, 4, S], BF16) for n in range(2)]
        stack_landed = [ctx.enter_context(nc.semaphore(f"f_stack{n}_landed")) for n in range(2)]
        emit_thirds(nc, x2_all, wq, wk, wv, parts, v_all, stacks, stack_landed, B, S)
        zT_all = sb("zT_all", [P, B, ZC, S])
        w_out = sb("w_out", [P, ZC, D])
        w_ff = sb("w_ff", [P, DC, D])
        emit_key_softmax(nc, parts, v_all, stacks, stack_landed, zT_all, wo, wff, w_out, w_ff, B, S)
        emit_gelu_output(nc, x2_all, zT_all, w_out, w_ff, out, B, S)


def emit_thirds(nc, x2_all, wq, wk, wv, parts, v_all, stacks, stack_landed, B, S):
    KT = S // P
    with ExitStack() as ctx:
        def sb(name, shape, dt=F32):
            return ctx.enter_context(nc.sbuf_tensor("p_" + name, shape, dt))

        def sem(name):
            return ctx.enter_context(nc.semaphore("p_" + name))

        wide = [ctx.enter_context(nc.psum_tensor(f"p_wide{i}", [P, S], F32)) for i in range(4)]
        X_WIDE, QK_WIDE, V_WIDE = wide[0:2], (wide[2], wide[3], wide[0], wide[1]), wide[2:4]
        ident = sb("ident", [P, P])
        W = [sb(f"w{n}_in", [P, DC, D]) for n in range(3)]
        W_hi = [sb(f"w{n}_hi", [P, DC, D], F32R) for n in range(3)]
        W_lo = [sb(f"w{n}_lo", [P, DC, D], F32R) for n in range(3)]
        xT_hi = sb("xT_hi", [P, 2, DC, S], F32R)
        xT_lo = sb("xT_lo", [P, 2, DC, S], F32R)
        third = sb("third", [P, 4, 3, S], BF16)
        rest = sb("rest", [P, 2, S])

        c_zero, c_ident = sem("zero"), sem("ident_done")
        w_landed = [sem(f"w{n}_landed") for n in range(3)]
        high_done, low_done = sem("w_high"), sem("w_low")
        x_turned, xT_hi_ready, xT_lo_ready = sem("x_turned"), sem("xT_hi_ready"), sem("xT_lo_ready")
        qk_done, first_ready, rest_ready, second_ready, third_ready = (
            sem("qk_done"), sem("first_ready"), sem("rest_ready"), sem("second_ready"), sem("third_ready"))
        v_done, v_ready = sem("v_done"), sem("v_ready")
        parts_stored = [sem(f"parts{m}_stored") for m in range(4)]

        block = ctx.enter_context(nc.Block())

        @block.sync
        def _(sp):
            def batch(b):
                for m in range(4):
                    sp.wait_ge(third_ready, b * 4 + m + 1)
                    sp.dma_start(parts[bass.ds(b, 1), m // 2, :, (m % 2) * P:(m % 2 + 1) * P, :].rearrange(
                        "b a p s -> p (b a) s"), third[:, m, :, :]).then_inc(parts_stored[m], 16)

            for n, w in enumerate((wq, wk, wv)):
                sp.dma_start(W[n][:, :, :], w.rearrange("(c p) n -> p c n", p=P)).then_inc(w_landed[n], 16)
            for b in range(B):
                batch(b)
                if b == 0:
                    for m in range(4):
                        sp.wait_ge(parts_stored[m], 16)
                if b < 2:
                    load_stacks(sp, parts, 0, b, b, stacks, stack_landed)
            for m in range(4):
                sp.wait_ge(parts_stored[m], 16 * B)

        @block.tensor
        def _(pe):
            pe.wait_ge(c_ident, 1)

            def turn_x(b, first=False):
                if not first:
                    pe.wait_ge(rest_ready, b * 4)
                for c in range(DC):
                    for t in range(KT):
                        last = pe.transpose(X_WIDE[c][:, t * P:(t + 1) * P], x2_all[:, b * KT + t, c * P:(c + 1) * P],
                                            ident[:, :])
                last.then_inc(x_turned, 1)

            def project(m, b, parity, first):
                n, s = m // 2, slice((m % 2) * P, (m % 2 + 1) * P)
                if m < 2 and not first:
                    pe.wait_ge(v_ready, b * 2 - 1 + m)
                pe.wait_ge(low_done, n + 1)
                for f in range(2):
                    last = split_matmuls(pe, QK_WIDE[m][:, f * HALF:(f + 1) * HALF],
                                         [(W_hi[n][:, c, s], W_lo[n][:, c, s]) for c in range(DC)],
                                         [tuple(a[:, parity, c, f * HALF:(f + 1) * HALF] for a in (xT_hi, xT_lo))
                                          for c in range(DC)])
                last.then_inc(qk_done, 1)

            def project_v(f, b, parity):
                pe.wait_ge(low_done, 3)
                pe.wait_ge(rest_ready, b * 4 + f + 1)
                for t in range(4 * f, 4 * f + 4):
                    s = slice(t * P, (t + 1) * P)
                    last = split_matmuls(pe, V_WIDE[f][:, (t % 4) * D:(t % 4 + 1) * D],
                                         [tuple(a[:, parity, c, s] for a in (xT_hi, xT_lo)) for c in range(DC)],
                                         [(W_hi[2][:, c, :], W_lo[2][:, c, :]) for c in range(DC)])
                last.then_inc(v_done, 1)

            def batch(b, parity, first=False, last=False):
                pe.wait_ge(xT_hi_ready, b * 2 + 2)
                pe.wait_ge(xT_lo_ready, b * 2 + 2)
                for m in range(4):
                    project(m, b, parity, first)
                project_v(0, b, parity)
                if not last:
                    turn_x(b + 1)
                project_v(1, b, parity)

            turn_x(0, first=True)
            for b in range(B):
                batch(b, b % 2, b == 0, b == B - 1)

        @block.scalar
        def _(act):
            def high_x(b, parity):
                act.wait_ge(x_turned, b + 1)
                for c in range(DC):
                    act.copy(xT_hi[:, parity, c, :], X_WIDE[c][:, :]).then_inc(xT_hi_ready, 1)

            def batch(b, parity, first=False, last=False):
                def first_third(m):
                    act.wait_ge(qk_done, b * 4 + m + 1)
                    if not first:
                        act.wait_ge(parts_stored[m], b * 16)
                    act.mul(third[:, m, 0, :], QK_WIDE[m][:, :], D ** -0.5 if m < 2 else 1.0
                            ).then_inc(first_ready, 1)

                first_third(0)
                for m in range(4):
                    if m < 3:
                        first_third(m + 1)
                    act.wait_ge(rest_ready, b * 4 + m + 1)
                    act.copy(third[:, m, 1, :], rest[:, m % 2, :]).then_inc(second_ready, 1)
                for f in range(2):
                    act.wait_ge(v_done, b * 2 + f + 1)
                    act.copy(v_all[:, bass.ds(b, 1), 4 * f:4 * f + 4, :].rearrange("p b t d -> p (b t d)"),
                             V_WIDE[f][:, :]).then_inc(v_ready, 1)
                    if f == 0 and not last:
                        high_x(b + 1, 1 - parity)

            high_x(0, 0)
            for n in range(3):
                act.wait_ge(w_landed[n], 16)
                act.copy(W_hi[n][:, :, :].rearrange("p a b -> p (a b)"), W[n][:, :, :].rearrange("p a b -> p (a b)")
                         ).then_inc(high_done, 1)
            for b in range(B):
                batch(b, b % 2, b == 0, b == B - 1)

        @block.gpsimd
        def _(pool):
            pool.memset(ident[:, :], 0.0).then_inc(c_zero, 1)
            pool.wait_ge(c_zero, 1)
            pool.affine_select(out=ident[:, :], in_=ident[:, :], compare_op=ALU.not_equal, fill=1.0, base=0,
                               pattern=[[-1, P]], channel_multiplier=1).then_inc(c_ident, 1)

        @block.vector
        def _(dve):
            def low_x(b, parity):
                for c in range(DC):
                    dve.wait_ge(xT_hi_ready, b * 2 + c + 1)
                    dve.tensor_tensor(xT_lo[:, parity, c, :], X_WIDE[c][:, :],
                                      xT_hi[:, parity, c, :].bitcast(F32), ALU.subtract).then_inc(xT_lo_ready, 1)

            def batch(b, parity, last=False):
                def leave_rest(m):
                    if m >= 2:
                        dve.wait_ge(third_ready, b * 4 + m - 1)
                    dve.wait_ge(first_ready, b * 4 + m + 1)
                    dve.scalar_tensor_tensor(out=rest[:, m % 2, :], in0=QK_WIDE[m][:, :],
                                             scalar=D ** -0.5 if m < 2 else 1.0,
                                             in1=third[:, m, 0, :], op0=ALU.mult, op1=ALU.subtract
                                             ).then_inc(rest_ready, 1)

                leave_rest(0)
                for m in range(4):
                    if m < 3:
                        leave_rest(m + 1)
                    dve.wait_ge(second_ready, b * 4 + m + 1)
                    dve.tensor_tensor(third[:, m, 2, :], rest[:, m % 2, :], third[:, m, 1, :], ALU.subtract
                                      ).then_inc(third_ready, 1)
                if not last:
                    low_x(b + 1, 1 - parity)

            low_x(0, 0)
            for n in range(3):
                dve.wait_ge(high_done, n + 1)
                dve.tensor_tensor(W_lo[n][:, :, :].rearrange("p a b -> p (a b)"),
                                  W[n][:, :, :].rearrange("p a b -> p (a b)"),
                                  W_hi[n][:, :, :].rearrange("p a b -> p (a b)").bitcast(F32), ALU.subtract
                                  ).then_inc(low_done, 1)
            for b in range(B):
                batch(b, b % 2, b == B - 1)


def emit_key_softmax(nc, parts, v_all, stacks, stack_landed, zT_all, wo, wff, w_out, w_ff, B, S):
    KT = S // P
    STEPS = GROUPS * KT
    TURNS = 4 * STEPS
    PIECE = S // 4
    q_stack, k_stack = stacks
    with ExitStack() as ctx:
        def sb(name, shape, dt=F32):
            return ctx.enter_context(nc.sbuf_tensor("s_" + name, shape, dt))

        def sem(name):
            return ctx.enter_context(nc.semaphore("s_" + name))

        ring = [ctx.enter_context(nc.psum_tensor(f"s_ring{i}", [P, S], F32)) for i in range(3)]
        acc = ctx.enter_context(nc.psum_tensor("s_acc", [P, S], F32))
        neg_max = sb("neg_max", [P, 2, 4])
        row_sum = sb("row_sum", [P, 2, 4])
        row_inv = sb("row_inv", [P, 2, 4])
        prob = sb("prob", [P, 4, 4, S])
        v_norm = sb("v_norm", [P, 2, 4, 4, 32])

        v_zeroed, w_landed = sem("v_zeroed"), sem("w_landed")
        scores_done, max_ready, exp_done, inv_ready, vnorm_ready, pv_done, zT_ready = (
            sem("scores_done"), sem("max_ready"), sem("exp_done"), sem("inv_ready"), sem("vnorm_ready"),
            sem("pv_done"), sem("zT_ready"))

        block = ctx.enter_context(nc.Block())

        @block.sync
        def _(sp):
            sp.dma_start(w_ff[:, :, :], wff.rearrange("(c p) n -> p c n", p=P)).then_inc(w_landed, 16)
            for j in range(4):
                for half in range(2):
                    at = 32 * j + half * HD
                    sp.dma_start(w_out[at:at + HD, :, :],
                                 wo.rearrange("(c r h i) n -> r h i c n", c=ZC, r=2, h=4)[half, j]
                                 ).then_inc(w_landed, 16)

            def batch(b, first=0):
                for group in range(first, GROUPS):
                    sp.wait_ge(scores_done, b * TURNS + (group - 1) * (TURNS // GROUPS))
                    load_stacks(sp, parts, b, group, group % 2, stacks, stack_landed)

            batch(0, first=2)
            with sp.Fori(1, B) as b:
                batch(b)
            sp.wait_ge(w_landed, 16 * 9)

        @block.tensor
        def _(pe):
            def scores(b, step, j, first):
                n = step * 4 + j
                slot, kt = (step // KT) % 2, step % KT
                if n >= 3:
                    pe.wait_ge(exp_done, b * TURNS + n - 2)
                elif not first:
                    pe.wait_ge(exp_done, b * TURNS + (TURNS - 1 - (TURNS - 1 - n) % 3) - TURNS + 1)
                for f in range(2):
                    last = pe.matmul(ring[n % 3][:, f * HALF:(f + 1) * HALF],
                                     k_stack[:, slot, j, kt * P:(kt + 1) * P],
                                     q_stack[:, slot, j, f * HALF:(f + 1) * HALF], start=True, stop=True)
                last.then_inc(scores_done, 1)

            def values(b, step, piece, first):
                s = slice(piece * PIECE, (piece + 1) * PIECE)
                if piece == 0:
                    pe.wait_ge(vnorm_ready, b * STEPS + step + 1)
                    if step % (2 * KT) == 0 and not (first and step == 0):
                        pe.wait_ge(zT_ready, b * ZC + step // (2 * KT))
                for j in range(4):
                    last = pe.matmul(acc[32 * j:32 * j + 32, s], v_norm[:, step // KT % 2, step % 4, j, :],
                                     prob[:, step % 4, j, s], start=step % (2 * KT) == 0 and piece % 2 == 0,
                                     stop=step % (2 * KT) == 2 * KT - 1, skip_group_check=True)
                if piece == 3:
                    last.then_inc(pv_done, 1)

            def batch(b, first=False):
                for step in range(STEPS):
                    if step % KT == 0:
                        pe.wait_ge(stack_landed[(step // KT) % 2], b * (2 * NSTACK) + (step // KT // 2 + 1) * NSTACK)
                    for j in range(4):
                        scores(b, step, j, first)
                        if step >= 2 or not first:
                            values(b, step - 2, j, first)

            batch(0, first=True)
            with pe.Fori(1, B) as b:
                batch(b)
            for step in range(2):
                for j in range(4):
                    values(B, step - 2, j, False)

        @block.scalar
        def _(act):
            def take_outputs(b, chunk):
                act.wait_ge(pv_done, b * STEPS + (chunk + 1) * 2 * KT)
                batch_at, chunk = (b, chunk) if chunk >= 0 else (b - 1, chunk + ZC)
                act.copy(zT_all[:, bass.ds(batch_at, 1), chunk, :].rearrange("p b s -> p (b s)"), acc[:, :]
                         ).then_inc(zT_ready, 1)

            def batch(b, first=False):
                for step in range(STEPS):
                    for j in range(4):
                        n = step * 4 + j
                        act.wait_ge(max_ready, b * TURNS + n + 1)
                        act.activation(prob[:, step % 4, j, :], ring[n % 3][:, :], ACT.Exp,
                                       bias=neg_max[:, step % 2, j:j + 1],
                                       accum_out=row_sum[:, step % 2, j:j + 1]).then_inc(exp_done, 1)
                        if step % (2 * KT) == 1 and j == 2 and not (first and step == 1):
                            take_outputs(b, step // (2 * KT) - 1)

            batch(0, first=True)
            with act.Fori(1, B) as b:
                batch(b)
            take_outputs(B, -1)

        @block.gpsimd
        def _(pool):
            pool.memset(v_norm[:, :, :, :, :].rearrange("p a b c d -> p (a b c d)"), 0.0).then_inc(v_zeroed, 1)
            pool.wait_ge(v_zeroed, 1)
            with pool.Fori(0, B) as b:
                for step in range(STEPS):
                    group, kt = step // KT, step % KT
                    pool.wait_ge(inv_ready, b * STEPS + step + 1)
                    at = group % 2 * HD
                    pool.tensor_tensor(v_norm[:, group % 2, step % 4, :, at:at + HD],
                                       v_all[:, bass.ds(b, 1), kt, group * 4 * HD:(group + 1) * 4 * HD].rearrange(
                                           "p b (h d) -> p (b h) d", d=HD),
                                       row_inv[:, step % 2, :].unsqueeze(2).to_broadcast([P, 4, HD]), ALU.mult
                                       ).then_inc(vnorm_ready, 1)

        @block.vector
        def _(dve):
            def inverse(b, step):
                dve.wait_ge(exp_done, b * TURNS + step * 4 + 4)
                dve.reciprocal(row_inv[:, step % 2, :], row_sum[:, step % 2, :]).then_inc(inv_ready, 1)

            def batch(b, first=False):
                for step in range(STEPS):
                    for j in range(4):
                        n = step * 4 + j
                        dve.wait_ge(scores_done, b * TURNS + n + 1)
                        dve.tensor_reduce(neg_max[:, step % 2, j:j + 1], ring[n % 3][:, :], AX_X, ALU.max,
                                          negate=True).then_inc(max_ready, 1)
                        if j == 1 and not (first and step == 0):
                            inverse(b, step - 1)

            batch(0, first=True)
            with dve.Fori(1, B) as b:
                batch(b)
            inverse(B, -1)


def emit_gelu_output(nc, x2_all, zT_all, w_out, w_ff, out, B, S):
    GT = HALF // P
    outf = out.rearrange("b s d -> (b s) d")
    with ExitStack() as ctx:
        def sb(name, shape, dt=F32):
            return ctx.enter_context(nc.sbuf_tensor("g_" + name, shape, dt))

        def sem(name):
            return ctx.enter_context(nc.semaphore("g_" + name))

        z1_bank = [ctx.enter_context(nc.psum_tensor(f"g_z1_{c}", [P, HALF], F32)) for c in range(DC)]
        z2_bank = ctx.enter_context(nc.psum_tensor("g_z2", [P, GT * D], F32))
        norm_bank = ctx.enter_context(nc.psum_tensor("g_norm", [P, HALF], F32))
        ones = sb("ones", [P, 1])
        neg_half = sb("neg_half", [P, GT])
        z1T = sb("z1T", [P, 2, DC, HALF])
        square = sb("square", [P, 2, DC, HALF])
        clamped = sb("clamped", [P, 2, GT])
        norm_inv = sb("norm_inv", [P, 2, GT])
        both_inv = sb("both_inv", [P, GT])
        square_sum = sb("square_sum", [P, GT])
        z = sb("z", [P, 2, GT * D])
        y = sb("y", [P, 2, GT * D])
        o_fin = sb("o_fin", [P, 2, GT * D])
        stats = sb("stats", [P, GT, 6])
        mean_var = sb("mean_var", [P, GT, 2])
        var_eps = sb("var_eps", [P, GT])
        rstd = sb("rstd", [P, GT])
        spare = sb("spare", [P, 1])

        c_set = sem("set")
        z1_done, z1_taken, norm_done, clamp1_done, inv1_ready = (
            sem("z1_done"), sem("z1_taken"), sem("norm_done"), sem("clamp1_done"), sem("inv1_ready"))
        z2_done, square_done, clamp2_done, inv2_ready, both_ready, z_ready = (
            sem("z2_done"), sem("square_done"), sem("clamp2_done"), sem("inv2_ready"), sem("both_ready"),
            sem("z_ready"))
        gelu_done, y_ready, ln_step, var_ready, rstd_ready, o_ready = (
            sem("gelu_done"), sem("y_ready"), sem("ln_step"), sem("var_ready"), sem("rstd_ready"), sem("o_ready"))
        stored = [sem("stored0"), sem("stored1")]

        block = ctx.enter_context(nc.Block())


        @block.sync
        def _(sp):
            def tokens(array, group):
                return array[bass.ds(group * HALF, HALF), :].rearrange("(t p) d -> p t d", p=P)

            with sp.Fori(0, B - 1) as b:
                for parity in range(2):
                    sp.wait_ge(o_ready, 2 * b + parity + 1)
                    sp.dma_start(tokens(outf, 2 * b + parity),
                                 o_fin[:, parity, :].rearrange("p (t d) -> p t d", d=D)).then_inc(stored[parity], 16)
            for parity in range(2):
                sp.wait_ge(o_ready, 2 * B - 1 + parity)
                sp.dma_start(tokens(outf, 2 * B - 2 + parity),
                             o_fin[:, parity, :].rearrange("p (t d) -> p t d", d=D)).then_inc(stored[parity], 16)
            for parity in range(2):
                sp.wait_ge(stored[parity], 16 * B + 16)

        @block.tensor
        def _(pe):
            pe.wait_ge(c_set, 1)

            def first_projection(b, half, first):
                if not (first and half == 0):
                    pe.wait_ge(z1_taken, 2 * b + half)
                for c in range(DC):
                    for g in range(ZC):
                        last = pe.matmul(z1_bank[c][:, :], w_out[:, g, c * P:(c + 1) * P],
                                         zT_all[:, bass.ds(b, 1), g, half * HALF:(half + 1) * HALF].rearrange(
                                             "p b s -> p (b s)"), start=g == 0, stop=g == ZC - 1)
                last.then_inc(z1_done, 1)

            def second_projection(group, parity, first):
                pe.wait_ge(z1_taken, group + 1)
                if not first:
                    pe.wait_ge(clamp1_done, group)
                for t in range(GT):
                    for c in range(DC):
                        last = pe.matmul(norm_bank[:, t:t + 1], square[:, parity, c, t * P:(t + 1) * P], ones[:, :],
                                         start=c == 0, stop=c == DC - 1)
                last.then_inc(norm_done, 1)
                if not first:
                    pe.wait_ge(z_ready, group)
                for t in range(GT):
                    for c in range(DC):
                        last = pe.matmul(z2_bank[:, t * D:(t + 1) * D], z1T[:, parity, c, t * P:(t + 1) * P],
                                         w_ff[:, c, :], start=c == 0, stop=c == DC - 1)
                last.then_inc(z2_done, 1)

            first_projection(0, 0, True)
            first_projection(0, 1, True)
            second_projection(0, 0, True)
            with pe.Fori(1, B) as b:
                first_projection(b, 0, False)
                second_projection(2 * b - 1, 1, False)
                first_projection(b, 1, False)
                second_projection(2 * b, 0, False)
            second_projection(2 * B - 1, 1, False)

        @block.scalar
        def _(act):
            def take_first(group, parity):
                act.wait_ge(z1_done, group + 1)
                for c in range(DC):
                    act.copy(z1T[:, parity, c, :], z1_bank[c][:, :])
                    last = act.activation(square[:, parity, c, :], z1_bank[c][:, :], ACT.Square)
                last.then_inc(z1_taken, 1)

            def square_second(group, parity):
                act.wait_ge(inv1_ready, group + 1)
                act.wait_ge(z2_done, group + 1)
                for t in range(GT):
                    last = act.activation(z[:, parity, t * D:(t + 1) * D], z2_bank[:, t * D:(t + 1) * D], ACT.Square,
                                          scale=norm_inv[:, 0, t:t + 1], accum_out=square_sum[:, t:t + 1])
                last.then_inc(square_done, 1)

            def gelu(group, parity):
                act.wait_ge(z_ready, group + 1)
                act.activation(z[:, parity, :], z[:, parity, :], ACT.Gelu).then_inc(gelu_done, 1)

            take_first(0, 0)
            take_first(1, 1)
            square_second(0, 0)
            with act.Fori(1, B) as b:
                take_first(2 * b, 0)
                gelu(2 * b - 2, 0)
                square_second(2 * b - 1, 1)
                take_first(2 * b + 1, 1)
                gelu(2 * b - 1, 1)
                square_second(2 * b, 0)
            gelu(2 * B - 2, 0)
            square_second(2 * B - 1, 1)
            gelu(2 * B - 1, 1)

        @block.gpsimd
        def _(pool):
            pool.memset(ones[:, :], 1.0).then_inc(c_set, 1)
            pool.memset(neg_half[:, :], -0.5).then_inc(c_set, 1)
            pool.wait_ge(c_set, 2)

            def root(out_of, of, ready, done, group):
                pool.wait_ge(ready, group + 1)
                pool.tensor_tensor(out_of, of, neg_half[:, :], ALU.pow).then_inc(done, 1)

            def norms_of_first(group):
                root(norm_inv[:, 0, :], clamped[:, 0, :], clamp1_done, inv1_ready, group)

            def norms_of_second(group):
                root(norm_inv[:, 1, :], clamped[:, 1, :], clamp2_done, inv2_ready, group)

            def deviations(group):
                root(rstd[:, :], var_eps[:, :], var_ready, rstd_ready, group)

            norms_of_first(0)
            norms_of_second(0)
            with pool.Fori(1, 2 * B) as group:
                norms_of_first(group)
                deviations(group - 1)
                norms_of_second(group)
            deviations(2 * B - 1)

        @block.vector
        def _(dve):
            dve.memset(stats[:, 0, :], 0.0).then_inc(stored[0], 16)
            dve.memset(stats[:, 1, :], 0.0).then_inc(stored[1], 16)

            def clamp_first(group):
                dve.wait_ge(norm_done, group + 1)
                dve.tensor_scalar(clamped[:, 0, :], norm_bank[:, 0:GT], 1e-24, None, ALU.max
                                  ).then_inc(clamp1_done, 1)

            def scale_second(group, parity):
                dve.wait_ge(square_done, group + 1)
                dve.tensor_scalar(clamped[:, 1, :], square_sum[:, :], 1e-24, None, ALU.max
                                  ).then_inc(clamp2_done, 1)
                dve.wait_ge(inv2_ready, group + 1)
                dve.tensor_tensor(both_inv[:, :], norm_inv[:, 0, :], norm_inv[:, 1, :], ALU.mult
                                  ).then_inc(both_ready, 1)
                dve.wait_ge(both_ready, group + 1)
                dve.tensor_tensor(z[:, parity, :].rearrange("p (t d) -> p t d", d=D),
                                  z2_bank[:, :].rearrange("p (t d) -> p t d", d=D),
                                  both_inv[:, :].unsqueeze(2).to_broadcast([P, GT, D]), ALU.mult
                                  ).then_inc(z_ready, 1)

            def residual(b, parity):
                group = 2 * b + parity
                dve.wait_ge(gelu_done, group + 1)
                dve.tensor_tensor(y[:, parity, :], z[:, parity, :],
                                  x2_all[:, bass.ds(group * GT, GT), :].rearrange("p t d -> p (t d)"), ALU.add
                                  ).then_inc(y_ready, 1)
                dve.wait_ge(y_ready, group + 1)
                for t in range(GT):
                    last = dve.bn_stats(stats[:, t, :], y[:, parity, t * D:(t + 1) * D])
                last.then_inc(ln_step, 1)
                dve.wait_ge(ln_step, 2 * group + 1)
                dve.memset(spare[:, :], 0.0)
                for t in range(GT):
                    last = dve.bn_aggr(mean_var[:, t, :], stats[:, t, :])
                last.then_inc(ln_step, 1)
                dve.wait_ge(ln_step, 2 * group + 2)
                dve.tensor_scalar(var_eps[:, :], mean_var[:, :, 1], LN_EPS, None, ALU.add).then_inc(var_ready, 1)

            def normalise(b, parity):
                dve.wait_ge(rstd_ready, 2 * b + parity + 1)
                dve.wait_ge(stored[parity], b * 16 + 16)
                for t in range(GT):
                    s = slice(t * D, (t + 1) * D)
                    last = dve.tensor_scalar(o_fin[:, parity, s], y[:, parity, s], mean_var[:, t, 0:1],
                                             rstd[:, t:t + 1], ALU.subtract, ALU.mult)
                last.then_inc(o_ready, 1)

            clamp_first(0)
            scale_second(0, 0)
            clamp_first(1)
            residual(0, 0)
            scale_second(1, 1)
            normalise(0, 0)
            with dve.Fori(1, B) as b:
                clamp_first(2 * b)
                residual(b - 1, 1)
                scale_second(2 * b, 0)
                normalise(b - 1, 1)
                clamp_first(2 * b + 1)
                residual(b, 0)
                scale_second(2 * b + 1, 1)
                normalise(b, 0)
            residual(B - 1, 1)
            normalise(B - 1, 1)


def build_layer(nc, x, ctx_768, attn_wq, attn_wk, attn_wv, attn_wo, betas, x_wq, x_wkv, x_wo, x_bias,
                f_wq, f_wk, f_wv, f_wo, f_wff, out):
    B, S, _ = x.shape
    x1 = nc.dram_tensor("after_attention", (B * S, D), F32).ap()
    parts = nc.dram_tensor("qk_thirds", (B, 2, 3, D, S), BF16).ap()
    with nc.cleanup_on_exit():
        emit_segment_attention(nc, x, attn_wq, attn_wk, attn_wv, attn_wo, betas, x1)
    with nc.sbuf_tensor("after_cross_attention", [P, B * S // P, D], F32) as x2_all:
        with nc.cleanup_on_exit():
            emit_cross_attention(nc, x1, ctx_768, x_wq, x_wkv, x_wo, x_bias, x2_all)
        emit_query_softmax(nc, x2_all, f_wq, f_wk, f_wv, f_wo, f_wff, parts, out)


_INS = ['x', 'ctx_768', 'L0_attn_Wq', 'L0_attn_Wk', 'L0_attn_Wv', 'L0_attn_Wo', 'L0_attn_betas', 'L0_xattn_w_q',
        'L0_xattn_w_kv', 'L0_xattn_w_out', 'L0_xattn_b_out', 'L0_ffn_Wq', 'L0_ffn_Wk', 'L0_ffn_Wv', 'L0_ffn_Wo',
        'L0_ffn_Wff']


def kernel(**inputs):
    import concourse.bacc as _bacc
    from concourse.bass_utils import run_bass_kernel_spmd as _run

    nc = _bacc.Bacc("TRN2", target_bir_lowering=False, num_devices=1)
    arrays, args = {}, []
    for name in _INS:
        a = np.ascontiguousarray(inputs[name])
        arrays[f"in_{name}_dram"] = a
        args.append(nc.dram_tensor(f"in_{name}_dram", a.shape, mybir.dt.from_np(a.dtype), kind="ExternalInput").ap())
    args.append(nc.dram_tensor("out_0_dram", inputs["x"].shape, F32, kind="ExternalOutput").ap())
    build_layer(nc, *args)
    r = _run(nc, [arrays], core_ids=[0])
    return r.results[0]["out_0_dram"]
```
